# Optimizing a Trainium2 kernel written in Bass

```python
import numpy as np
import jax
import jax.numpy as jnp

def _softmax(x, axis=-1):
    return jax.nn.softmax(x, axis=axis)

def _gelu(x):
    return jax.nn.gelu(x, approximate=True)

def _silu(x):
    return jax.nn.silu(x)

def _sigmoid(x):
    return jax.nn.sigmoid(x)

def _layernorm(x, axis=-1, eps=1e-05):
    m = jnp.mean(x, axis=axis, keepdims=True)
    v = jnp.var(x, axis=axis, keepdims=True)
    return (x - m) / jnp.sqrt(v + eps)

def _scatter_add(tgt, idx, src, axis=0):
    return tgt.at[idx].add(src)

def _segment_sum(src, seg, n):
    return jax.ops.segment_sum(src, seg, n)
kernel_name = 'mk_seq_preln_d4_jaxref_r8_98fa4c'

def setup_inputs(seed: int=0):
    np.random.seed(seed)
    _w = jnp.asarray

    def _L0_attn_setup():
        import jax, jax.numpy as jnp
        import numpy as np
        HEADS = 16
        EMBED_SIZE = 128
        HEAD_OUT = EMBED_SIZE // HEADS
        B, T = (4, 256)
        key = jax.random.key(seed)
        ks = jax.random.split(key, 7)
        std = 0.02
        return {'embeddings': jax.random.normal(ks[0], (B, T, EMBED_SIZE), dtype=jnp.float32), 'Wq': jax.random.normal(ks[1], (HEAD_OUT, EMBED_SIZE), dtype=jnp.float32) * std, 'bq': jax.random.normal(ks[2], (HEAD_OUT,), dtype=jnp.float32) * std, 'Wk': jax.random.normal(ks[3], (HEAD_OUT, EMBED_SIZE), dtype=jnp.float32) * std, 'bk': jax.random.normal(ks[4], (HEAD_OUT,), dtype=jnp.float32) * std, 'Wv': jax.random.normal(ks[5], (HEAD_OUT, EMBED_SIZE), dtype=jnp.float32) * std, 'bv': jax.random.normal(ks[6], (HEAD_OUT,), dtype=jnp.float32) * std}
    _L0_attn_in = _L0_attn_setup()

    def _L0_ffn_setup():
        import jax, jax.numpy as jnp
        import numpy as np

        def _bitlinear(x, w_latent):
            scale = jax.lax.stop_gradient(jnp.clip(jnp.mean(jnp.abs(w_latent), axis=1, keepdims=True), 1e-05, None))
            tern = jnp.clip(jnp.round(w_latent / scale), -1.0, 1.0)
            w = w_latent + jax.lax.stop_gradient(tern - w_latent)
            return x @ (w * scale).T
        key = jax.random.key(seed)
        ks = jax.random.split(key, 6)
        dim, hidden, rank = (128, 512, 16)
        B, S = (4, 512)
        x = jax.random.normal(ks[0], (B, S, dim), dtype=jnp.float32)
        w_fc = 0.02 * jax.random.normal(ks[1], (hidden, dim), dtype=jnp.float32)
        w_proj = 0.02 * jax.random.normal(ks[2], (dim, hidden), dtype=jnp.float32)
        u = 0.02 * jax.random.normal(ks[3], (hidden, rank), dtype=jnp.float32)
        v = 0.02 * jax.random.normal(ks[4], (rank, dim), dtype=jnp.float32)
        fast_b = jax.random.normal(ks[5], (rank, rank), dtype=jnp.float32)
        gate = jnp.float32(0.05)
        return {'x': x, 'fast_b': fast_b, 'w_fc': w_fc, 'w_proj': w_proj, 'u': u, 'v': v, 'gate': gate}
    _L0_ffn_in = _L0_ffn_setup()

    def _L1_attn_setup():
        import jax, jax.numpy as jnp
        import numpy as np
        B, S, D, H = (2, 256, 128, 16)
        DEPTH = D // H
        EPS = 1e-06

        def _split_heads(t):
            b, s, _ = t.shape
            return t.reshape(b, s, H, DEPTH).transpose(0, 2, 1, 3)
        key = jax.random.key(seed)
        ks = jax.random.split(key, 6)
        glorot = lambda k: jax.random.uniform(k, (D, D), jnp.float32, -1.0, 1.0) * np.sqrt(6.0 / (D + D))
        return {'x': jax.random.normal(ks[0], (B, S, D), jnp.float32), 'Wq': glorot(ks[1]), 'bq': jnp.zeros((D,), jnp.float32), 'Wk': glorot(ks[2]), 'bk': jnp.zeros((D,), jnp.float32), 'Wv': glorot(ks[3]), 'bv': jnp.zeros((D,), jnp.float32), 'Wo': glorot(ks[4]), 'bo': jnp.zeros((D,), jnp.float32), 'gamma': jnp.ones((D,), jnp.float32), 'beta': jnp.zeros((D,), jnp.float32)}
    _L1_attn_in = _L1_attn_setup()

    def _L1_ffn_setup():
        import jax, jax.numpy as jnp
        import numpy as np
        EPS = 1e-06
        LN_EPS = 1e-05

        def _absmean_core(W):
            gamma = jnp.mean(jnp.abs(W)) + EPS
            Ws = W / gamma
            Wq = jnp.sign(Ws) * jnp.minimum(jnp.round(jnp.abs(Ws)), 1.0)
            return (Wq, gamma)

        @jax.custom_vjp
        def absmean(W):
            return _absmean_core(W)[0]

        def _absmean_fwd(W):
            Wq, gamma = _absmean_core(W)
            return (Wq, gamma)

        def _absmean_bwd(gamma, g):
            return (g / gamma,)
        absmean.defvjp(_absmean_fwd, _absmean_bwd)

        def layernorm(x, w, b, eps=LN_EPS):
            mu = jnp.mean(x, axis=-1, keepdims=True)
            var = jnp.mean((x - mu) ** 2, axis=-1, keepdims=True)
            return (x - mu) * jax.lax.rsqrt(var + eps) * w + b
        key = jax.random.key(seed)
        k1, k2, k3 = jax.random.split(key, 3)
        d, h = (128, 512)
        B, T = (8, 256)
        return {'x': jax.random.normal(k1, (B, T, d), jnp.float32), 'W_fc': jax.random.normal(k2, (h, d), jnp.float32), 'ln_w': jnp.ones((h,), jnp.float32), 'ln_b': jnp.zeros((h,), jnp.float32), 'W_proj': jax.random.normal(k3, (d, h), jnp.float32)}
    _L1_ffn_in = _L1_ffn_setup()

    def _L2_attn_setup():
        import jax, jax.numpy as jnp
        import numpy as np
        import math

        def _alibi_slopes(n_heads):

            def pow2(n):
                start = 2 ** (-2 ** (-(math.log2(n) - 3)))
                return [start ** i for i in range(n)]
            if math.log2(n_heads).is_integer():
                slopes = pow2(n_heads)
            else:
                closest = 2 ** math.floor(math.log2(n_heads))
                slopes = pow2(closest) + _alibi_slopes(2 * closest).tolist()[0::2][:n_heads - closest]
            return np.asarray(slopes, dtype=np.float32)
        key = jax.random.key(seed)
        ks = jax.random.split(key, 4)
        B, L, D = (2, 256, 128)
        s = 1.0 / math.sqrt(D)
        return {'x': jax.random.normal(ks[0], (B, L, D), jnp.float32), 'Wqkv': jax.random.normal(ks[1], (D, 3 * D), jnp.float32) * s, 'bqkv': jnp.zeros((3 * D,), jnp.float32), 'Wout': jax.random.normal(ks[2], (D, D), jnp.float32) * s, 'bout': jnp.zeros((D,), jnp.float32)}
    _L2_attn_in = _L2_attn_setup()

    def _L2_ffn_setup():
        import jax, jax.numpy as jnp
        import numpy as np
        DIM = 128
        DEPTH = 6
        HEADS = 16
        DIM_HEAD = 64
        WINDOW = 32
        INNER = HEADS * DIM_HEAD
        DIM_INNER = int(DIM * 4 * 2 / 3)
        QK_SCALE = 8.0

        def shift_tokens(t):
            a, s = jnp.split(t, 2, -1)
            s = jnp.pad(s, ((0, 0), (1, 0), (0, 0)))[:, :-1]
            return jnp.concatenate([a, s], -1)

        def l2norm(t):
            return t / jnp.maximum(jnp.linalg.norm(t, axis=-1, keepdims=True), 1e-12)

        def rotate_half(x):
            x1, x2 = jnp.split(x, 2, -1)
            return jnp.concatenate([-x2, x1], -1)

        def rotary_tables(n):
            half = jnp.arange(0, DIM_HEAD, 2, dtype=jnp.float32)
            inv_freq = 1.0 / 10000.0 ** (half / DIM_HEAD)
            t = jnp.arange(n, dtype=jnp.float32)
            freqs = t[:, None] * inv_freq[None, :]
            freqs = jnp.concatenate([freqs, freqs], -1)
            base_scale = (half + 0.4 * DIM_HEAD) / (1.4 * DIM_HEAD)
            power = (t - n // 2) / (WINDOW // 2)
            scale = base_scale[None, :] ** power[:, None]
            scale = jnp.concatenate([scale, scale], -1)
            return (freqs, scale)

        def local_attention(q, k, v):
            b, h, n, d = q.shape
            w = WINDOW
            nw = n // w
            bq = q.reshape(b, h, nw, w, d)
            bk = k.reshape(b, h, nw, w, d)
            bv = v.reshape(b, h, nw, w, d)

            def look(t):
                p = jnp.pad(t, ((0, 0), (0, 0), (1, 0), (0, 0), (0, 0)))
                return jnp.concatenate([p[:, :, :nw], p[:, :, 1:]], axis=3)
            bk2, bv2 = (look(bk), look(bv))
            seq = jnp.arange(n).reshape(nw, w)
            seq_p = jnp.pad(seq, ((1, 0), (0, 0)), constant_values=-1)
            jt = jnp.concatenate([seq_p[:nw], seq_p[1:]], axis=1)
            it = seq[:, :, None]
            jb = jt[:, None, :]
            mask = (it < jb) | (it > jb + w) | (jb == -1)
            sim = jnp.einsum('bhwie,bhwje->bhwij', bq, bk2) * QK_SCALE
            sim = jnp.where(mask, -jnp.finfo(sim.dtype).max, sim)
            attn = jax.nn.softmax(sim, -1)
            out = jnp.einsum('bhwij,bhwje->bhwie', attn, bv2)
            return out.reshape(b, h, n, d)

        def attn_layer(x, Wqkv, qs, ksc, Wo):
            b, n, _ = x.shape
            qkv = x @ Wqkv
            q, k, v = jnp.split(qkv, 3, -1)
            sh = lambda t: t.reshape(b, n, HEADS, DIM_HEAD).transpose(0, 2, 1, 3)
            q, k, v = (sh(q), sh(k), sh(v))
            q = l2norm(q) * qs
            k = l2norm(k) * ksc
            freqs, scale = rotary_tables(n)
            cos, sin = (jnp.cos(freqs), jnp.sin(freqs))
            q = q * cos * scale + rotate_half(q) * sin * scale
            inv = 1.0 / scale
            k = k * cos * inv + rotate_half(k) * sin * inv
            out = local_attention(q, k, v)
            out = out.transpose(0, 2, 1, 3).reshape(b, n, INNER)
            return out @ Wo

        def ffn_layer(x, g, bln, W1, b1, W2, b2):
            mu = x.mean(-1, keepdims=True)
            var = ((x - mu) ** 2).mean(-1, keepdims=True)
            xn = (x - mu) / jnp.sqrt(var + 1e-05) * g + bln
            hg = xn @ W1 + b1
            a, gate = jnp.split(hg, 2, -1)
            return a * jax.nn.gelu(gate, approximate=False) @ W2 + b2
        key = jax.random.key(seed)
        ks = jax.random.split(key, 8)
        B, N = (2, 256)
        init = lambda k, shape: jax.random.normal(k, shape, jnp.float32) * 0.02
        return {'x': jax.random.normal(ks[0], (B, N, DIM), jnp.float32), 'Wqkv': init(ks[1], (DEPTH, DIM, 3 * INNER)), 'q_scale': jnp.ones((DEPTH, DIM_HEAD), jnp.float32), 'k_scale': jnp.ones((DEPTH, DIM_HEAD), jnp.float32), 'Wo': init(ks[2], (DEPTH, INNER, DIM)), 'ln_g': jnp.ones((DEPTH, DIM), jnp.float32), 'ln_b': jnp.zeros((DEPTH, DIM), jnp.float32), 'W1': init(ks[3], (DEPTH, DIM, 2 * DIM_INNER)), 'b1': jnp.zeros((DEPTH, 2 * DIM_INNER), jnp.float32), 'W2': init(ks[4], (DEPTH, DIM_INNER, DIM)), 'b2': jnp.zeros((DEPTH, DIM), jnp.float32)}
    _L2_ffn_in = _L2_ffn_setup()

    def _L3_attn_setup():
        import jax, jax.numpy as jnp
        import numpy as np
        ALPHA = 0.99
        EMBED_DIM = 128
        SEQ_LEN = 256
        BATCH = 4
        key = jax.random.key(seed)
        k1, k2, k3 = jax.random.split(key, 3)
        x = jax.random.normal(k1, (BATCH, SEQ_LEN, EMBED_DIM), dtype=jnp.float32)
        scale = 1.0 / np.sqrt(EMBED_DIM)
        W_qkv = jax.random.uniform(k2, (3 * EMBED_DIM, EMBED_DIM), dtype=jnp.float32, minval=-scale, maxval=scale)
        b_qkv = jax.random.uniform(k3, (3 * EMBED_DIM,), dtype=jnp.float32, minval=-scale, maxval=scale)
        return {'x': x, 'W_qkv': W_qkv, 'b_qkv': b_qkv}
    _L3_attn_in = _L3_attn_setup()

    def _L3_ffn_setup():
        import jax, jax.numpy as jnp
        import numpy as np
        L, E, H, F, K = (4, 4, 128, 512, 2)
        B, S = (4, 256)
        EPS = 1e-05

        def _moe_layer(x, rw, rb, g, b, w1, b1, w2, b2):
            logits = jnp.einsum('bsh,he->bse', x, rw) + rb
            probs = jax.nn.softmax(logits, axis=-1)
            vals, idx = jax.lax.top_k(probs, K)
            vals = vals / vals.sum(axis=-1, keepdims=True)
            mu = x.mean(axis=-1, keepdims=True)
            xc = x - mu
            xhat = xc * jax.lax.rsqrt((xc * xc).mean(axis=-1, keepdims=True) + EPS)
            xe = xhat[None] * g[:, None, None, :] + b[:, None, None, :]
            h = jax.nn.gelu(jnp.einsum('ebsh,ehf->ebsf', xe, w1) + b1[:, None, None, :], approximate=False)
            y = jnp.einsum('ebsf,efh->ebsh', h, w2) + b2[:, None, None, :]
            expert_out = x[None] + y
            comb = jnp.einsum('bsk,bske->bse', vals, jax.nn.one_hot(idx, E, dtype=x.dtype))
            return jnp.einsum('bse,ebsh->bsh', comb, expert_out)
        key = jax.random.key(seed)
        ks = jax.random.split(key, 4)
        return {'hidden_states': jax.random.normal(ks[0], (B, S, H), jnp.float32), 'router_w': 0.02 * jax.random.normal(ks[1], (L, H, E), jnp.float32), 'router_b': jnp.zeros((L, E), jnp.float32), 'ln_g': jnp.ones((L, E, H), jnp.float32), 'ln_b': jnp.zeros((L, E, H), jnp.float32), 'w1': 0.02 * jax.random.normal(ks[2], (L, E, H, F), jnp.float32), 'b1': jnp.zeros((L, E, F), jnp.float32), 'w2': 0.02 * jax.random.normal(ks[3], (L, E, F, H), jnp.float32), 'b2': jnp.zeros((L, E, H), jnp.float32)}
    _L3_ffn_in = _L3_ffn_setup()
    _d = {'L0_attn_embeddings': _L0_attn_in['embeddings'], 'L0_attn_Wq': _L0_attn_in['Wq'], 'L0_attn_bq': _L0_attn_in['bq'], 'L0_attn_Wk': _L0_attn_in['Wk'], 'L0_attn_bk': _L0_attn_in['bk'], 'L0_attn_Wv': _L0_attn_in['Wv'], 'L0_attn_bv': _L0_attn_in['bv'], 'L0_ffn_fast_b': _L0_ffn_in['fast_b'], 'L0_ffn_w_fc': _L0_ffn_in['w_fc'], 'L0_ffn_w_proj': _L0_ffn_in['w_proj'], 'L0_ffn_u': _L0_ffn_in['u'], 'L0_ffn_v': _L0_ffn_in['v'], 'L0_ffn_gate': _L0_ffn_in['gate'], 'L1_attn_Wq': _L1_attn_in['Wq'], 'L1_attn_bq': _L1_attn_in['bq'], 'L1_attn_Wk': _L1_attn_in['Wk'], 'L1_attn_bk': _L1_attn_in['bk'], 'L1_attn_Wv': _L1_attn_in['Wv'], 'L1_attn_bv': _L1_attn_in['bv'], 'L1_attn_Wo': _L1_attn_in['Wo'], 'L1_attn_bo': _L1_attn_in['bo'], 'L1_attn_gamma': _L1_attn_in['gamma'], 'L1_attn_beta': _L1_attn_in['beta'], 'L1_ffn_W_fc': _L1_ffn_in['W_fc'], 'L1_ffn_ln_w': _L1_ffn_in['ln_w'], 'L1_ffn_ln_b': _L1_ffn_in['ln_b'], 'L1_ffn_W_proj': _L1_ffn_in['W_proj'], 'L2_attn_Wqkv': _L2_attn_in['Wqkv'], 'L2_attn_bqkv': _L2_attn_in['bqkv'], 'L2_attn_Wout': _L2_attn_in['Wout'], 'L2_attn_bout': _L2_attn_in['bout'], 'L2_ffn_Wqkv': _L2_ffn_in['Wqkv'], 'L2_ffn_q_scale': _L2_ffn_in['q_scale'], 'L2_ffn_k_scale': _L2_ffn_in['k_scale'], 'L2_ffn_Wo': _L2_ffn_in['Wo'], 'L2_ffn_ln_g': _L2_ffn_in['ln_g'], 'L2_ffn_ln_b': _L2_ffn_in['ln_b'], 'L2_ffn_W1': _L2_ffn_in['W1'], 'L2_ffn_b1': _L2_ffn_in['b1'], 'L2_ffn_W2': _L2_ffn_in['W2'], 'L2_ffn_b2': _L2_ffn_in['b2'], 'L3_attn_W_qkv': _L3_attn_in['W_qkv'], 'L3_attn_b_qkv': _L3_attn_in['b_qkv'], 'L3_ffn_router_w': _L3_ffn_in['router_w'], 'L3_ffn_router_b': _L3_ffn_in['router_b'], 'L3_ffn_ln_g': _L3_ffn_in['ln_g'], 'L3_ffn_ln_b': _L3_ffn_in['ln_b'], 'L3_ffn_w1': _L3_ffn_in['w1'], 'L3_ffn_b1': _L3_ffn_in['b1'], 'L3_ffn_w2': _L3_ffn_in['w2'], 'L3_ffn_b2': _L3_ffn_in['b2']}
    _x0 = _d['L0_attn_embeddings']
    _d['L0_attn_embeddings'] = jax.random.normal(jax.random.fold_in(jax.random.key(seed), 1), (16, 256, 128), dtype=_x0.dtype)
    del _x0
    return _d

def reference(L0_attn_embeddings, L0_attn_Wq, L0_attn_bq, L0_attn_Wk, L0_attn_bk, L0_attn_Wv, L0_attn_bv, L0_ffn_fast_b, L0_ffn_w_fc, L0_ffn_w_proj, L0_ffn_u, L0_ffn_v, L0_ffn_gate, L1_attn_Wq, L1_attn_bq, L1_attn_Wk, L1_attn_bk, L1_attn_Wv, L1_attn_bv, L1_attn_Wo, L1_attn_bo, L1_attn_gamma, L1_attn_beta, L1_ffn_W_fc, L1_ffn_ln_w, L1_ffn_ln_b, L1_ffn_W_proj, L2_attn_Wqkv, L2_attn_bqkv, L2_attn_Wout, L2_attn_bout, L2_ffn_Wqkv, L2_ffn_q_scale, L2_ffn_k_scale, L2_ffn_Wo, L2_ffn_ln_g, L2_ffn_ln_b, L2_ffn_W1, L2_ffn_b1, L2_ffn_W2, L2_ffn_b2, L3_attn_W_qkv, L3_attn_b_qkv, L3_ffn_router_w, L3_ffn_router_b, L3_ffn_ln_g, L3_ffn_ln_b, L3_ffn_w1, L3_ffn_b1, L3_ffn_w2, L3_ffn_b2):

    def _L0_attn_ref(embeddings, Wq, bq, Wk, bk, Wv, bv):
        import jax, jax.numpy as jnp
        import numpy as np
        HEADS = 16
        EMBED_SIZE = 128
        HEAD_OUT = EMBED_SIZE // HEADS
        B, T = (4, 256)
        b, t, c = embeddings.shape
        x = embeddings.reshape(b * t, c)
        q = x @ Wq.T + bq
        k = x @ Wk.T + bk
        v = x @ Wv.T + bv
        scale = jnp.asarray(c, dtype=x.dtype) ** 0.5
        att = jax.nn.softmax(q @ k.T / scale, axis=-1)
        y = (att @ v).reshape(b, t, -1)
        return jnp.tile(y, (1, 1, HEADS))

    def _L0_ffn_ref(x, fast_b, w_fc, w_proj, u, v, gate):
        import jax, jax.numpy as jnp
        import numpy as np

        def _bitlinear(x, w_latent):
            scale = jax.lax.stop_gradient(jnp.clip(jnp.mean(jnp.abs(w_latent), axis=1, keepdims=True), 1e-05, None))
            tern = jnp.clip(jnp.round(w_latent / scale), -1.0, 1.0)
            w = w_latent + jax.lax.stop_gradient(tern - w_latent)
            return x @ (w * scale).T
        h = _bitlinear(x, w_fc) + gate * (x @ v.T @ fast_b.T @ u.T)
        r = jnp.maximum(h, 0.0)
        return _bitlinear(r * r, w_proj)

    def _L1_attn_ref(x, Wq, bq, Wk, bk, Wv, bv, Wo, bo, gamma, beta):
        import jax, jax.numpy as jnp
        import numpy as np
        B, S, D, H = (2, 256, 128, 16)
        DEPTH = D // H
        EPS = 1e-06

        def _split_heads(t):
            b, s, _ = t.shape
            return t.reshape(b, s, H, DEPTH).transpose(0, 2, 1, 3)
        b, s, d = x.shape
        q = _split_heads(x @ Wq + bq)
        k = _split_heads(x @ Wk + bk)
        v = _split_heads(x @ Wv + bv)
        q = jax.nn.elu(q) + 1.0
        k = jax.nn.elu(k) + 1.0
        k = k / jnp.sqrt(jnp.sum(k * k, axis=-1, keepdims=True) + EPS)
        scores = jnp.einsum('bhqd,bhkd->bhqk', q, k)
        attn = jnp.einsum('bhqk,bhkd->bhqd', scores, v)
        attn = attn.transpose(0, 2, 1, 3).reshape(b, s, d)
        out = attn @ Wo + bo
        y = x + out
        mu = jnp.mean(y, axis=-1, keepdims=True)
        var = jnp.mean(jnp.square(y - mu), axis=-1, keepdims=True)
        return (y - mu) / jnp.sqrt(var + EPS) * gamma + beta

    def _L1_ffn_ref(x, W_fc, ln_w, ln_b, W_proj):
        import jax, jax.numpy as jnp
        import numpy as np
        EPS = 1e-06
        LN_EPS = 1e-05

        def _absmean_core(W):
            gamma = jnp.mean(jnp.abs(W)) + EPS
            Ws = W / gamma
            Wq = jnp.sign(Ws) * jnp.minimum(jnp.round(jnp.abs(Ws)), 1.0)
            return (Wq, gamma)

        @jax.custom_vjp
        def absmean(W):
            return _absmean_core(W)[0]

        def _absmean_fwd(W):
            Wq, gamma = _absmean_core(W)
            return (Wq, gamma)

        def _absmean_bwd(gamma, g):
            return (g / gamma,)
        absmean.defvjp(_absmean_fwd, _absmean_bwd)

        def layernorm(x, w, b, eps=LN_EPS):
            mu = jnp.mean(x, axis=-1, keepdims=True)
            var = jnp.mean((x - mu) ** 2, axis=-1, keepdims=True)
            return (x - mu) * jax.lax.rsqrt(var + eps) * w + b
        h = jnp.einsum('btd,hd->bth', x, absmean(W_fc))
        h = jax.nn.gelu(h, approximate=False)
        h = layernorm(h, ln_w, ln_b)
        return jnp.einsum('bth,dh->btd', h, absmean(W_proj))

    def _L2_attn_ref(x, Wqkv, bqkv, Wout, bout):
        import jax, jax.numpy as jnp
        import numpy as np
        import math

        def _alibi_slopes(n_heads):

            def pow2(n):
                start = 2 ** (-2 ** (-(math.log2(n) - 3)))
                return [start ** i for i in range(n)]
            if math.log2(n_heads).is_integer():
                slopes = pow2(n_heads)
            else:
                closest = 2 ** math.floor(math.log2(n_heads))
                slopes = pow2(closest) + _alibi_slopes(2 * closest).tolist()[0::2][:n_heads - closest]
            return np.asarray(slopes, dtype=np.float32)
        n_heads = 16
        B, L, D = x.shape
        head_dim = D // n_heads
        qkv = (x @ Wqkv + bqkv).reshape(B, L, 3, n_heads, head_dim)
        q, k, v = (qkv[:, :, 0], qkv[:, :, 1], qkv[:, :, 2])
        scores = jnp.einsum('bqhd,bkhd->bhqk', q, k) / math.sqrt(head_dim)
        pos = jnp.arange(L)
        bias = -jnp.abs(pos[None, :] - pos[:, None]).astype(jnp.float32)
        slopes = jnp.asarray(_alibi_slopes(n_heads))
        scores = scores + slopes[None, :, None, None] * bias[None, None]
        probs = jax.nn.softmax(scores, axis=-1)
        out = jnp.einsum('bhqk,bkhd->bqhd', probs, v).reshape(B, L, D)
        return out @ Wout + bout

    def _L2_ffn_ref(x, Wqkv, q_scale, k_scale, Wo, ln_g, ln_b, W1, b1, W2, b2):
        import jax, jax.numpy as jnp
        import numpy as np
        DIM = 128
        DEPTH = 6
        HEADS = 16
        DIM_HEAD = 64
        WINDOW = 32
        INNER = HEADS * DIM_HEAD
        DIM_INNER = int(DIM * 4 * 2 / 3)
        QK_SCALE = 8.0

        def shift_tokens(t):
            a, s = jnp.split(t, 2, -1)
            s = jnp.pad(s, ((0, 0), (1, 0), (0, 0)))[:, :-1]
            return jnp.concatenate([a, s], -1)

        def l2norm(t):
            return t / jnp.maximum(jnp.linalg.norm(t, axis=-1, keepdims=True), 1e-12)

        def rotate_half(x):
            x1, x2 = jnp.split(x, 2, -1)
            return jnp.concatenate([-x2, x1], -1)

        def rotary_tables(n):
            half = jnp.arange(0, DIM_HEAD, 2, dtype=jnp.float32)
            inv_freq = 1.0 / 10000.0 ** (half / DIM_HEAD)
            t = jnp.arange(n, dtype=jnp.float32)
            freqs = t[:, None] * inv_freq[None, :]
            freqs = jnp.concatenate([freqs, freqs], -1)
            base_scale = (half + 0.4 * DIM_HEAD) / (1.4 * DIM_HEAD)
            power = (t - n // 2) / (WINDOW // 2)
            scale = base_scale[None, :] ** power[:, None]
            scale = jnp.concatenate([scale, scale], -1)
            return (freqs, scale)

        def local_attention(q, k, v):
            b, h, n, d = q.shape
            w = WINDOW
            nw = n // w
            bq = q.reshape(b, h, nw, w, d)
            bk = k.reshape(b, h, nw, w, d)
            bv = v.reshape(b, h, nw, w, d)

            def look(t):
                p = jnp.pad(t, ((0, 0), (0, 0), (1, 0), (0, 0), (0, 0)))
                return jnp.concatenate([p[:, :, :nw], p[:, :, 1:]], axis=3)
            bk2, bv2 = (look(bk), look(bv))
            seq = jnp.arange(n).reshape(nw, w)
            seq_p = jnp.pad(seq, ((1, 0), (0, 0)), constant_values=-1)
            jt = jnp.concatenate([seq_p[:nw], seq_p[1:]], axis=1)
            it = seq[:, :, None]
            jb = jt[:, None, :]
            mask = (it < jb) | (it > jb + w) | (jb == -1)
            sim = jnp.einsum('bhwie,bhwje->bhwij', bq, bk2) * QK_SCALE
            sim = jnp.where(mask, -jnp.finfo(sim.dtype).max, sim)
            attn = jax.nn.softmax(sim, -1)
            out = jnp.einsum('bhwij,bhwje->bhwie', attn, bv2)
            return out.reshape(b, h, n, d)

        def attn_layer(x, Wqkv, qs, ksc, Wo):
            b, n, _ = x.shape
            qkv = x @ Wqkv
            q, k, v = jnp.split(qkv, 3, -1)
            sh = lambda t: t.reshape(b, n, HEADS, DIM_HEAD).transpose(0, 2, 1, 3)
            q, k, v = (sh(q), sh(k), sh(v))
            q = l2norm(q) * qs
            k = l2norm(k) * ksc
            freqs, scale = rotary_tables(n)
            cos, sin = (jnp.cos(freqs), jnp.sin(freqs))
            q = q * cos * scale + rotate_half(q) * sin * scale
            inv = 1.0 / scale
            k = k * cos * inv + rotate_half(k) * sin * inv
            out = local_attention(q, k, v)
            out = out.transpose(0, 2, 1, 3).reshape(b, n, INNER)
            return out @ Wo

        def ffn_layer(x, g, bln, W1, b1, W2, b2):
            mu = x.mean(-1, keepdims=True)
            var = ((x - mu) ** 2).mean(-1, keepdims=True)
            xn = (x - mu) / jnp.sqrt(var + 1e-05) * g + bln
            hg = xn @ W1 + b1
            a, gate = jnp.split(hg, 2, -1)
            return a * jax.nn.gelu(gate, approximate=False) @ W2 + b2
        for i in range(DEPTH):
            x = attn_layer(shift_tokens(x), Wqkv[i], q_scale[i], k_scale[i], Wo[i]) + x
            x = ffn_layer(shift_tokens(x), ln_g[i], ln_b[i], W1[i], b1[i], W2[i], b2[i]) + x
        return x

    def _L3_attn_ref(x, W_qkv, b_qkv):
        import jax, jax.numpy as jnp
        import numpy as np
        ALPHA = 0.99
        EMBED_DIM = 128
        SEQ_LEN = 256
        BATCH = 4
        bs, sl, d = x.shape
        qkv = x @ W_qkv.T + b_qkv
        q, k, v = jnp.split(qkv, 3, axis=-1)
        idx = jnp.arange(sl)
        diff = (idx[:, None] - idx[None, :]).astype(jnp.float32)
        M = jnp.where(idx[:, None] >= idx[None, :], ALPHA ** diff, 0.0)
        dim_sqrt = jnp.float32(np.sqrt(d))
        scores = jnp.einsum('bqd,bkd->bqk', q, k) / dim_sqrt * M
        out = scores @ v
        return out

    def _L3_ffn_ref(hidden_states, router_w, router_b, ln_g, ln_b, w1, b1, w2, b2):
        import jax, jax.numpy as jnp
        import numpy as np
        L, E, H, F, K = (4, 4, 128, 512, 2)
        B, S = (4, 256)
        EPS = 1e-05

        def _moe_layer(x, rw, rb, g, b, w1, b1, w2, b2):
            logits = jnp.einsum('bsh,he->bse', x, rw) + rb
            probs = jax.nn.softmax(logits, axis=-1)
            vals, idx = jax.lax.top_k(probs, K)
            vals = vals / vals.sum(axis=-1, keepdims=True)
            mu = x.mean(axis=-1, keepdims=True)
            xc = x - mu
            xhat = xc * jax.lax.rsqrt((xc * xc).mean(axis=-1, keepdims=True) + EPS)
            xe = xhat[None] * g[:, None, None, :] + b[:, None, None, :]
            h = jax.nn.gelu(jnp.einsum('ebsh,ehf->ebsf', xe, w1) + b1[:, None, None, :], approximate=False)
            y = jnp.einsum('ebsf,efh->ebsh', h, w2) + b2[:, None, None, :]
            expert_out = x[None] + y
            comb = jnp.einsum('bsk,bske->bse', vals, jax.nn.one_hot(idx, E, dtype=x.dtype))
            return jnp.einsum('bse,ebsh->bsh', comb, expert_out)
        x = hidden_states
        for l in range(L):
            x = _moe_layer(x, router_w[l], router_b[l], ln_g[l], ln_b[l], w1[l], b1[l], w2[l], b2[l])
        return x
    x = L0_attn_embeddings
    x = x + _L0_attn_ref(_layernorm(x, axis=-1), L0_attn_Wq, L0_attn_bq, L0_attn_Wk, L0_attn_bk, L0_attn_Wv, L0_attn_bv)
    x = x + _L0_ffn_ref(_layernorm(x, axis=-1), L0_ffn_fast_b, L0_ffn_w_fc, L0_ffn_w_proj, L0_ffn_u, L0_ffn_v, L0_ffn_gate)
    x = x + _L1_attn_ref(_layernorm(x, axis=-1), L1_attn_Wq, L1_attn_bq, L1_attn_Wk, L1_attn_bk, L1_attn_Wv, L1_attn_bv, L1_attn_Wo, L1_attn_bo, L1_attn_gamma, L1_attn_beta)
    x = x + _L1_ffn_ref(_layernorm(x, axis=-1), L1_ffn_W_fc, L1_ffn_ln_w, L1_ffn_ln_b, L1_ffn_W_proj)
    x = x + _L2_attn_ref(_layernorm(x, axis=-1), L2_attn_Wqkv, L2_attn_bqkv, L2_attn_Wout, L2_attn_bout)
    x = x + _L2_ffn_ref(_layernorm(x, axis=-1), L2_ffn_Wqkv, L2_ffn_q_scale, L2_ffn_k_scale, L2_ffn_Wo, L2_ffn_ln_g, L2_ffn_ln_b, L2_ffn_W1, L2_ffn_b1, L2_ffn_W2, L2_ffn_b2)
    x = x + _L3_attn_ref(_layernorm(x, axis=-1), L3_attn_W_qkv, L3_attn_b_qkv)
    x = x + _L3_ffn_ref(_layernorm(x, axis=-1), L3_ffn_router_w, L3_ffn_router_b, L3_ffn_ln_g, L3_ffn_ln_b, L3_ffn_w1, L3_ffn_b1, L3_ffn_w2, L3_ffn_b2)
    return x

_drawn_inputs = setup_inputs


def setup_inputs(seed=0):
    import zlib

    import numpy as np

    out = dict(_drawn_inputs(seed))
    spreads = {'L1_attn_bq': (0.0, 0.363),
     'L1_attn_bk': (0.0, 0.644),
     'L1_attn_bv': (0.0, 0.1),
     'L1_attn_bo': (0.0, 2.0),
     'L1_attn_gamma': (1.0, 0.2),
     'L1_attn_beta': (0.0, 0.1),
     'L1_ffn_ln_w': (1.0, 0.2),
     'L1_ffn_ln_b': (0.0, 0.1),
     'L2_attn_bqkv': (0.0, 0.8),
     'L2_attn_bout': (0.0, 0.8),
     'L2_ffn_q_scale': (1.0, 0.6),
     'L2_ffn_k_scale': (1.0, 0.6),
     'L2_ffn_ln_g': (1.0, 0.6),
     'L2_ffn_ln_b': (0.0, 0.8),
     'L2_ffn_b1': (0.0, 0.8),
     'L2_ffn_b2': (0.0, 0.558),
     'L3_ffn_router_b': (0.0, 2.0),
     'L3_ffn_ln_g': (1.0, 0.6),
     'L3_ffn_ln_b': (0.0, 2.0),
     'L3_ffn_b1': (0.0, 2.0),
     'L3_ffn_b2': (0.0, 2.0)}
    factors = {'L0_attn_Wq': 8.0,
     'L0_attn_bq': 64.0,
     'L0_attn_Wk': 8.0,
     'L0_attn_bk': 64.0,
     'L0_attn_Wv': 3.652,
     'L0_ffn_fast_b': 8.0,
     'L0_ffn_w_fc': 5.515,
     'L0_ffn_u': 8.0,
     'L0_ffn_v': 8.0,
     'L2_ffn_Wqkv': 4.232,
     'L2_ffn_Wo': 4.02,
     'L2_ffn_W1': 8.0,
     'L2_ffn_W2': 8.0,
     'L3_ffn_router_w': 64.0,
     'L3_ffn_w1': 64.0,
     'L3_ffn_w2': 59.761,
     'L3_attn_W_qkv': 8.0,
     'L3_attn_b_qkv': 8.0}
    for name, (base, spread) in spreads.items():
        noise = np.random.default_rng([zlib.crc32(name.encode()), seed]).standard_normal(out[name].shape)
        drawn = base * np.exp(spread * noise) if base else spread * noise
        out[name] = jnp.asarray(drawn.astype(out[name].dtype))
    for name, factor in factors.items():
        out[name] = (out[name] * factor).astype(out[name].dtype)
    return out
```

```python
import math
from contextlib import ExitStack

import concourse.bass as bass
from concourse import mybir

F32 = mybir.dt.float32
BF16 = mybir.dt.bfloat16
ALU = mybir.AluOpType
ACT = mybir.ActivationFunctionType
AX = mybir.AxisListType

P = 128
D = 128
SEQS = 16
LEN = 256
TPS = LEN // P
TILES = SEQS * TPS
LN_EPS = 1e-5


def slope_parts(heads=16):
    import numpy as np
    out = []
    for h in range(heads):
        rest = np.float32((2.0 ** (-2.0 ** (-(math.log2(heads) - 3)))) ** h)
        while rest:
            bits = np.array([rest], np.float32).view(np.uint32)
            bits = (bits + np.uint32(0x7FFF) + ((bits >> np.uint32(16)) & np.uint32(1))) & np.uint32(0xFFFF0000)
            part = bits.view(np.float32)[0]
            out.append((h, -float(part)))
            rest = np.float32(rest - part)
    return out


SLOPE_PARTS = slope_parts()


class Core:

    def __init__(self, nc, dram, ctx):
        self.nc = nc
        self.dram = dram
        self.ctx = ctx
        self.x = self.sb("x", [P, TILES, D])
        self.ident = self.sb("ident", [P, P])
        self.ident_bf = self.sb("ident_bf", [P, P], BF16)
        self.mean = self.sb("mean", [P, TILES])
        self.rstd = self.sb("rstd", [P, TILES])
        self.banks = ctx.enter_context(nc.psum_tensor("banks", [P, 8, 512], F32))
        self.passed = ctx.enter_context(nc.semaphore("passed"))
        self.bank = [self.banks[:, i, :] for i in range(8)]

    def sb(self, name, shape, dt=F32):
        return self.ctx.enter_context(self.nc.sbuf_tensor(name, shape, dt))

    def sem(self, name):
        handle = self.sublayer.enter_context(self.nc.semaphore(name))
        self.sems.append(handle)
        return handle

    def run(self, sublayer):
        nc = self.nc
        with ExitStack() as self.sublayer:
            self.sems = []
            sublayer(self)
            with nc.Block() as block:
                @block.gpsimd
                def _(pool):
                    for handle in self.sems:
                        nc.gpsimd.sem_clear(handle)


class Chain:

    def __init__(self, eng, sem, base=0):
        self.eng, self.sem, self.base, self.n = eng, sem, base, 0

    def __call__(self, instruction):
        self.n += 1
        instruction.then_inc(self.sem, 1)
        self.eng.wait_ge(self.sem, self.base + self.n)


def scratch(core, stack):
    def sb(name, shape, dt=F32):
        return stack.enter_context(core.nc.sbuf_tensor(name, shape, dt))
    return sb, core.sem


def load_block(core, name, loads):
    nc = core.nc
    landed = core.sem(f"{name}_landed")
    with nc.Block() as block:
        @block.sync
        def _(sp):
            for dst, src in loads:
                sp.dma_start(dst, src).then_inc(landed, 16)
            sp.wait_ge(landed, 16 * len(loads))


def load_layer(core, name, loads, layer):
    nc = core.nc
    landed = core.sem(f"{name}_landed")
    with nc.Block() as block:
        @block.sync
        def _(sp):
            for dst, src in loads:
                sp.dma_start(dst, src).then_inc(landed, 16)
            sp.wait_ge(landed, layer * (16 * len(loads)) + 16 * len(loads))
            sp.sem_inc(core.passed, 1)


def stats_block(core, name, src, eps, layer=None, width=D):
    nc = core.nc
    U = 4
    with ExitStack() as stack:
        sb, sem = scratch(core, stack)
        raw = sb(f"{name}_raw", [P, TILES, 6])
        eps_col = sb(f"{name}_eps", [P, 1])
        gap = sb(f"{name}_gap", [P, TILES])
        var = sb(f"{name}_var", [P, TILES])
        std = sb(f"{name}_std", [P, TILES])
        gathered, merged, eps_set, rooted = (sem(f"{name}_{n}") for n in ("gathered", "merged", "eps_set", "rooted"))
        n = 0 if layer is None else layer
        MERGES = 5
        with nc.Block() as block:
            @block.vector
            def _(dve):
                nc.vector.memset(eps_col[:], eps).then_inc(eps_set, 1)
                with dve.Fori(0, TILES // U) as i:
                    for k in range(U):
                        nc.vector.bn_stats(flat(raw[:, tile(U * i + k), :]), flat(src[:, tile(U * i + k), :])).then_inc(gathered, 1)
                dve.wait_ge(gathered, n * TILES + TILES)
                then = Chain(dve, merged, n * MERGES)
                nc.vector.tensor_tensor(core.mean[:], raw[:, :, 1], raw[:, :, 4], ALU.add)
                nc.vector.tensor_tensor(var[:], raw[:, :, 2], raw[:, :, 5], ALU.add)
                then(nc.vector.tensor_tensor(gap[:], raw[:, :, 1], raw[:, :, 4], ALU.subtract))
                then(nc.vector.tensor_tensor(gap[:], gap[:], gap[:], ALU.mult))
                then(nc.vector.tensor_scalar(gap[:], gap[:], 0.25, None, ALU.mult))
                then(nc.vector.scalar_tensor_tensor(var[:], var[:], 1.0 / width, gap[:], ALU.mult, ALU.add))
                then(nc.vector.tensor_scalar(core.mean[:], core.mean[:], 0.5, None, ALU.mult))
                dve.wait_ge(rooted, n + 1)
                nc.vector.reciprocal(core.rstd[:], std[:])

            @block.scalar
            def _(act):
                act.wait_ge(eps_set, n + 1)
                act.wait_ge(merged, n * MERGES + MERGES)
                nc.scalar.activation(std[:], var[:], ACT.Sqrt, bias=eps_col[:]).then_inc(rooted, 1)


def tile(t, k=1):
    return bass.ds(t, k)


def flat(ap):
    return ap.rearrange("p a d -> p (a d)")


def l0_attention(core):
    nc, x, bank, dram = core.nc, core.x, core.bank, core.dram
    HD = 8
    SCALE = float(D) ** -0.5
    PAIRS = [(0, 0), (0, 1), (1, 0), (1, 1), (0, 2), (2, 0), (1, 2), (2, 1)]
    KQ = HD * len(PAIRS)
    with ExitStack() as stack:
        sb, sem = scratch(core, stack)
        w = sb("a0_w", [D, 3 * HD])
        bias = sb("a0_bias", [P, 3 * HD])
        load_block(core, "a0", [(w[:], dram["L0_wqkv"]), (bias[:], dram["L0_bqkv"])])
        stats_block(core, "a0s", x, LN_EPS)

        stage = sb("a0_stage", [P, TPS, D])
        xT = sb("a0_xT", [D, LEN])
        qkv = sb("a0_qkv", [P, TILES, 3 * HD])
        v1 = sb("a0_v1", [P, TILES, HD + 1])
        staged, turned, xT_ready, projected, biased = (sem("a0_" + n) for n in
                                                       ("staged", "turned", "xT_ready", "projected", "biased"))
        with nc.Block() as block:
            @block.vector
            def _(dve):
                with dve.Fori(0, SEQS) as b:
                    for t in range(TPS):
                        i = 2 * b + t
                        nc.vector.tensor_scalar(stage[:, t, :], flat(x[:, tile(i), :]), core.mean[:, tile(i)],
                                                core.rstd[:, tile(i)], ALU.subtract, ALU.mult).then_inc(staged, 1)
                    dve.wait_ge(projected, b + 1)
                    nc.vector.tensor_tensor(qkv[:, tile(2 * b, 2), :],
                                            bank[1][:, 0:2 * 3 * HD].rearrange("p (t c) -> p t c", t=TPS),
                                            bias[:, None, :].to_broadcast([P, TPS, 3 * HD]), ALU.add).then_inc(biased, 1)

            @block.tensor
            def _(pe):
                with pe.Fori(0, SEQS) as b:
                    pe.wait_ge(staged, 2 * b + 2)
                    for t in range(TPS):
                        mm = pe.transpose(bank[0][:, t * P:(t + 1) * P], stage[:, t, :], core.ident[:])
                    mm.then_inc(turned, 1)
                    pe.wait_ge(xT_ready, b + 1)
                    for t in range(TPS):
                        mm = pe.matmul(bank[1][:, t * 3 * HD:(t + 1) * 3 * HD], xT[:, t * P:(t + 1) * P], w[:],
                                       start=True, stop=True)
                    mm.then_inc(projected, 1)

            @block.scalar
            def _(act):
                with act.Fori(0, SEQS) as b:
                    act.wait_ge(turned, b + 1)
                    nc.scalar.copy(xT[:], bank[0][:, 0:LEN]).then_inc(xT_ready, 1)

        parts = sb("a0_parts", [P, 3, TILES, 2 * HD], BF16)
        rest = sb("a0_rest", [P, 2, TILES, 2 * HD])
        q_rows = sb("a0_q_rows", [P, TILES, P], BF16)
        k_rows = sb("a0_k_rows", [P, TILES, P], BF16)
        split, laid = sem("a0_split"), sem("a0_laid")
        with nc.Block() as block:
            @block.vector
            def _(dve):
                then = Chain(dve, split)
                qk = qkv[:, :, 0:2 * HD]
                then(nc.vector.tensor_copy(parts[:, 0], qk))
                then(nc.vector.tensor_tensor(rest[:, 0], qk, parts[:, 0], ALU.subtract))
                then(nc.vector.tensor_copy(parts[:, 1], rest[:, 0]))
                then(nc.vector.tensor_tensor(rest[:, 1], rest[:, 0], parts[:, 1], ALU.subtract))
                then(nc.vector.tensor_copy(parts[:, 2], rest[:, 1]))
                nc.vector.memset(v1[:, :, HD:HD + 1], 1.0)
                nc.vector.tensor_copy(v1[:, :, 0:HD], qkv[:, :, 2 * HD:3 * HD])
                nc.vector.memset(q_rows[:, :, KQ:P], 0.0)
                nc.vector.memset(k_rows[:, :, KQ:P], 1.0)
                for n, (a, b) in enumerate(PAIRS):
                    nc.vector.tensor_copy(q_rows[:, :, n * HD:(n + 1) * HD], parts[:, a, :, 0:HD])
                    nc.vector.tensor_copy(k_rows[:, :, n * HD:(n + 1) * HD], parts[:, b, :, HD:2 * HD])

        qT = sb("a0_qT", [P, TILES, P], BF16)
        kT = sb("a0_kT", [P, TILES, P], BF16)

        def turn_rows(name, jobs):
            G = 8
            turned_g, copied = sem(f"a0_turned_{name}"), sem(f"a0_copied_{name}")
            steps = [(dst, src, g) for dst, src in jobs for g in range(TILES // G)]
            with nc.Block() as block:
                @block.tensor
                def _(pe):
                    for n, (dst, src, g) in enumerate(steps):
                        if n >= 2:
                            pe.wait_ge(copied, n - 1)
                        out = bank[n % 2].bitcast(BF16)
                        for k in range(G):
                            mm = pe.transpose(out[:, k * P:(k + 1) * P], src[:, g * G + k, :], core.ident_bf[:])
                        mm.then_inc(turned_g, 1)

                @block.vector
                def _(dve):
                    for n, (dst, src, g) in enumerate(steps):
                        dve.wait_ge(turned_g, n + 1)
                        nc.vector.tensor_copy(flat(dst[:, g * G:(g + 1) * G, :]), bank[n % 2].bitcast(BF16)).then_inc(copied, 1)

        turn_rows("qk", [(qT, q_rows), (kT, k_rows)])

        top = sb("a0_top", [P, TILES, 2])
        scored, halved = sem("a0_scored"), sem("a0_halved")
        HALF = TILES * P // 2
        with nc.Block() as block:
            @block.tensor
            def _(pe):
                with pe.Fori(0, TILES) as t:
                    for h in range(2):
                        pe.wait_ge(halved, 2 * t + h + 1)
                        for c in range(4):
                            mm = pe.matmul(bank[4 * h + c], flat(qT[:, tile(t), :]),
                                           kT[:, 16 * h + 4 * c:16 * h + 4 * c + 4, :].rearrange("p a d -> p (a d)"),
                                           start=True, stop=True)
                        mm.then_inc(scored, 1)

            @block.vector
            def _(dve):
                dve.sem_inc(halved, 2)
                with dve.Fori(0, TILES) as t:
                    for h in range(2):
                        dve.wait_ge(scored, 2 * t + h + 1)
                        nc.vector.tensor_reduce(top[:, tile(t), h:h + 1].rearrange("p a c -> p (a c)"),
                                                core.banks[:, 4 * h:4 * h + 4, :], AX.XY, ALU.max).then_inc(halved, 1)

        low = sb("a0_low", [P, 3, TILES])
        cut = sem("a0_cut")
        with nc.Block() as block:
            @block.vector
            def _(dve):
                then = Chain(dve, cut)
                m = [q_rows[:, :, KQ + c:KQ + c + 1].rearrange("p t a -> p (t a)") for c in range(3)]
                then(nc.vector.tensor_tensor(low[:, 0], top[:, :, 0], top[:, :, 1], ALU.max))
                then(nc.vector.tensor_scalar(low[:, 0], low[:, 0], -1.0, None, ALU.mult))
                then(nc.vector.tensor_copy(m[0], low[:, 0]))
                then(nc.vector.tensor_tensor(low[:, 1], low[:, 0], m[0], ALU.subtract))
                then(nc.vector.tensor_copy(m[1], low[:, 1]))
                then(nc.vector.tensor_tensor(low[:, 2], low[:, 1], m[1], ALU.subtract))
                nc.vector.tensor_copy(m[2], low[:, 2])

        turn_rows("m", [(qT, q_rows)])

        QC = 4
        CHUNKS = TILES // QC
        expd = sb("a0_expd", [P, 2, 2, QC * P])
        inv = sb("a0_inv", [P, QC])
        y = sb("a0_y", [P, QC, HD])
        paired, expd_ready, expd_used, sums_read, inverted = (
            sem("a0_" + n) for n in ("paired", "expd_ready", "expd_used", "sums_read", "inverted"))
        KPAIRS = TILES // 2
        acc = bank[4][:, 0:QC * (HD + 1)].rearrange("p (s c) -> p s c", s=QC)
        with nc.Block() as block:
            @block.tensor
            def _(pe):
                def scores(c, kt, n, par):
                    pe.wait_ge(expd_ready, n + 1)
                    for h in range(2):
                        mm = pe.matmul(bank[2 * par + h], flat(kT[:, tile(kt + h), :]),
                                       qT[:, tile(c * QC, QC), :].rearrange("p a d -> p (a d)"), start=True, stop=True)
                    mm.then_inc(paired, 1)

                def sums(kt, n, par, first, last):
                    pe.wait_ge(expd_ready, n + 3)
                    for h in range(2):
                        for s in range(QC):
                            mm = pe.matmul(acc[:, s, :], expd[:, par, h, s * P:(s + 1) * P], flat(v1[:, tile(kt + h), :]),
                                           start=first and h == 0 and s == 0, stop=last and h == 1, skip_group_check=True)
                    mm.then_inc(expd_used, 1)

                with pe.Fori(0, CHUNKS) as c:
                    scores(c, 0, c * KPAIRS, 0)
                    scores(c, 2, c * KPAIRS + 1, 1)
                    pe.wait_ge(sums_read, c + 1)
                    sums(0, c * KPAIRS, 0, True, False)
                    scores(c, 4, c * KPAIRS + 2, 0)
                    sums(2, c * KPAIRS + 1, 1, False, False)
                    scores(c, 6, c * KPAIRS + 3, 1)
                    with pe.Fori(1, KPAIRS // 2 - 1) as k:
                        for par in range(2):
                            sums(4 * k + 2 * par, c * KPAIRS + 2 * k + par, par, False, False)
                            scores(c, 4 * k + 2 * par + 4, c * KPAIRS + 2 * k + par + 2, par)
                    for par in range(2):
                        sums(TILES - 4 + 2 * par, c * KPAIRS + KPAIRS - 2 + par, par, False, par == 1)

            @block.scalar
            def _(act):
                act.sem_inc(expd_ready, 2)
                with act.Fori(0, CHUNKS * KPAIRS // 2) as k:
                    for par in range(2):
                        act.wait_ge(paired, 2 * k + par + 1)
                        act.wait_ge(expd_used, 2 * k + par + 1)
                        nc.scalar.activation(expd[:, par], core.banks[:, 2 * par:2 * par + 2, :], ACT.Exp, scale=SCALE)\
                            .then_inc(expd_ready, 1)

            @block.vector
            def _(dve):
                dve.sem_inc(sums_read, 1)
                dve.sem_inc(expd_used, 2)
                with dve.Fori(0, CHUNKS) as c:
                    dve.wait_ge(expd_used, c * KPAIRS + KPAIRS + 2)
                    nc.vector.reciprocal(inv[:], acc[:, :, HD]).then_inc(inverted, 1)
                    dve.wait_ge(inverted, c + 1)
                    nc.vector.tensor_tensor(y[:], acc[:, :, 0:HD], inv[:, :, None].to_broadcast([P, QC, HD]), ALU.mult)\
                        .then_inc(sums_read, 1)
                    dve.wait_ge(sums_read, c + 2)
                    for s in range(QC):
                        xs = flat(x[:, tile(c * QC + s), :]).rearrange("p (r f) -> p r f", f=HD)
                        nc.vector.tensor_tensor(xs, xs, y[:, s, None, :].to_broadcast([P, D // HD, HD]), ALU.add)


def l0_feedforward(core):
    nc, x, bank, dram = core.nc, core.x, core.bank, core.dram
    H = 512
    C = H // P
    R = 16
    with ExitStack() as stack:
        sb, sem = scratch(core, stack)
        fc = sb("f0_fc", [P, C, D])
        proj = sb("f0_proj", [P, H])
        uT = sb("f0_uT", [R, H])
        v = sb("f0_v", [R, D])
        fbT = sb("f0_fbT", [R, R])
        gate = sb("f0_gate", [P, 1])
        load_block(core, "f0", [(fc[:], dram["L0_fc"].rearrange("(c p) d -> p c d", p=P)), (proj[:], dram["L0_proj"]),
                                (uT[:], dram["L0_uT"]), (v[:], dram["L0_v"]), (fbT[:], dram["L0_fbT"]), (gate[:], dram["L0_gate"])])
        stats_block(core, "f0s", x, LN_EPS)

        w1 = sb("f0_w1", [D, H])
        w2 = sb("f0_w2", [P, C, D])
        fbv = sb("f0_fbv", [R, D])
        scale = sb("f0_scale", [P, C + 1])
        edge = sb("f0_edge", [P, 2, C + 1])
        tern = sb("f0_tern", [P, 2, C, D])
        below = sb("f0_below", [P, 2, C, D])
        made, small, turned = sem("f0_made"), sem("f0_small"), sem("f0_turned")
        with nc.Block() as block:
            @block.vector
            def _(dve):
                then = Chain(dve, made)
                then(nc.vector.tensor_reduce(scale[:, 0:C], fc[:], AX.X, ALU.add, apply_absolute_value=True))
                then(nc.vector.tensor_reduce(scale[:, C:C + 1], proj[:], AX.X, ALU.add, apply_absolute_value=True))
                then(nc.vector.tensor_scalar(scale[:, 0:C], scale[:, 0:C], 1.0 / D, 1e-5, ALU.mult, ALU.max))
                then(nc.vector.tensor_scalar(scale[:, C:C + 1], scale[:, C:C + 1], 1.0 / H, 1e-5, ALU.mult, ALU.max))
                then(nc.vector.tensor_scalar(edge[:, 0], scale[:], 0.5, None, ALU.mult))
                then(nc.vector.tensor_scalar(edge[:, 1], scale[:], -0.5, None, ALU.mult))
                for c in range(C):
                    for m, src, e in ((0, fc[:, c, :], c), (1, proj[:, c * P:(c + 1) * P], C)):
                        then(nc.vector.tensor_scalar(below[:, m, c], src, edge[:, 1, e:e + 1], None, ALU.is_lt))
                        then(nc.vector.scalar_tensor_tensor(tern[:, m, c], src, edge[:, 0, e:e + 1], below[:, m, c],
                                                            ALU.is_gt, ALU.subtract))
                        then(nc.vector.tensor_scalar(tern[:, m, c], tern[:, m, c], scale[:, e:e + 1], None, ALU.mult))
                dve.wait_ge(small, 1)
                then(nc.vector.tensor_copy(fbv[:], bank[0][0:R, 0:D]))
                dve.wait_ge(small, 2)
                then(nc.vector.scalar_tensor_tensor(tern[:, 0], bank[1].rearrange("p (c d) -> p c d", c=C), gate[:, 0:1],
                                                    tern[:, 0], ALU.mult, ALU.add))
                dve.wait_ge(turned, 1)
                then(nc.vector.tensor_copy(w1[:], bank[2]))
                then(nc.vector.tensor_copy(w2[:].rearrange("p c d -> p (c d)"), bank[3]))

            @block.tensor
            def _(pe):
                pe.matmul(bank[0][0:R, 0:D], fbT[:], v[:], start=True, stop=True).then_inc(small, 1)
                FBV = 6 + 3 * 2 * C + 1
                pe.wait_ge(made, FBV)
                for c in range(C):
                    mm = pe.matmul(bank[1][:, c * D:(c + 1) * D], uT[:, c * P:(c + 1) * P], fbv[:], start=True, stop=True)
                mm.then_inc(small, 1)
                pe.wait_ge(made, FBV + 1)
                for c in range(C):
                    pe.transpose(bank[2][:, c * P:(c + 1) * P], tern[:, 0, c, :], core.ident[:])
                    mm = pe.transpose(bank[3][:, c * P:(c + 1) * P], tern[:, 1, c, :], core.ident[:])
                mm.then_inc(turned, 1)

        stage = sb("f0_stage", [P, TPS, D])
        xT = sb("f0_xT", [D, LEN])
        relu = sb("f0_relu", [P, C * LEN])
        hid = sb("f0_hid", [P, C, LEN])
        staged, turned_x, xT_ready, hidden, clipped, squared, projected, added = (
            sem("f0_" + n) for n in ("staged", "turned_x", "xT_ready", "hidden", "clipped", "squared", "projected", "added"))
        with nc.Block() as block:
            @block.vector
            def _(dve):
                def put(b):
                    for t in range(TPS):
                        i = 2 * b + t
                        nc.vector.tensor_scalar(stage[:, t, :], flat(x[:, tile(i), :]), core.mean[:, tile(i)],
                                                core.rstd[:, tile(i)], ALU.subtract, ALU.mult).then_inc(staged, 1)
                with dve.Fori(0, SEQS) as b:
                    put(b)
                    dve.wait_ge(clipped, b + 1)
                    nc.vector.tensor_tensor(hid[:].rearrange("p c t -> p (c t)"), relu[:], relu[:], ALU.mult).then_inc(squared, 1)
                    dve.wait_ge(projected, b + 1)
                    nc.vector.tensor_tensor(x[:, tile(2 * b, 2), :], x[:, tile(2 * b, 2), :],
                                            bank[4][:, 0:LEN].rearrange("p (t d) -> p t d", t=TPS), ALU.add)

            @block.tensor
            def _(pe):
                with pe.Fori(0, SEQS) as b:
                    pe.wait_ge(staged, 2 * b + 2)
                    for t in range(TPS):
                        mm = pe.transpose(bank[0][:, t * P:(t + 1) * P], stage[:, t, :], core.ident[:])
                    mm.then_inc(turned_x, 1)
                    pe.wait_ge(xT_ready, b + 1)
                    for c in range(C):
                        mm = pe.matmul(bank[2 + c // 2][:, (c % 2) * LEN:(c % 2 + 1) * LEN], w1[:, c * P:(c + 1) * P], xT[:],
                                       start=True, stop=True)
                    mm.then_inc(hidden, 1)
                    pe.wait_ge(squared, b + 1)
                    for t in range(TPS):
                        for c in range(C):
                            mm = pe.matmul(bank[4][:, t * D:(t + 1) * D], hid[:, c, t * P:(t + 1) * P], w2[:, c, :],
                                           start=c == 0, stop=c == C - 1)
                    mm.then_inc(projected, 1)

            @block.scalar
            def _(act):
                with act.Fori(0, SEQS) as b:
                    act.wait_ge(turned_x, b + 1)
                    nc.scalar.copy(xT[:], bank[0][:, 0:LEN]).then_inc(xT_ready, 1)
                    act.wait_ge(hidden, b + 1)
                    nc.scalar.activation(relu[:].rearrange("p (a f) -> p a f", a=2), core.banks[:, 2:4, :], ACT.Relu).then_inc(clipped, 1)


def put_normalized(core, dve, b, stage, staged):
    nc = core.nc
    for t in range(TPS):
        i = TPS * b + t
        nc.vector.tensor_scalar(stage[:, t, :], flat(core.x[:, tile(i), :]), core.mean[:, tile(i)], core.rstd[:, tile(i)],
                                ALU.subtract, ALU.mult).then_inc(staged, 1)


def enter_stream(core, name, saved):
    nc = core.nc
    stats_block(core, name, core.x, LN_EPS)
    kept = core.sem(f"{name}_kept")
    with nc.Block() as block:
        @block.vector
        def _(dve):
            nc.vector.tensor_copy(saved[:], core.x[:]).then_inc(kept, 1)
            dve.wait_ge(kept, 1)
            for t in range(TILES):
                nc.vector.tensor_scalar(core.x[:, t, :], saved[:, t, :], core.mean[:, t:t + 1], core.rstd[:, t:t + 1],
                                        ALU.subtract, ALU.mult)


def leave_stream(core, saved):
    nc = core.nc
    with nc.Block() as block:
        @block.vector
        def _(dve):
            nc.vector.tensor_tensor(core.x[:], core.x[:], saved[:], ALU.add)


def l1_attention(core):
    nc, x, bank, dram = core.nc, core.x, core.bank, core.dram
    HEADS, HD = 16, 8
    EPS = 1e-6
    with ExitStack() as stack:
        sb, sem = scratch(core, stack)
        wq, wkv, wo, blocks = sb("a1_wq", [D, D]), sb("a1_wkv", [D, 2 * D]), sb("a1_wo", [D, D]), sb("a1_blocks", [D, D])
        bq, bkv, bo = sb("a1_bq", [D, 1]), sb("a1_bkv", [P, 2 * D]), sb("a1_bo", [P, D])
        gamma, beta = sb("a1_gamma", [P, D]), sb("a1_beta", [P, D])
        load_block(core, "a1", [(wq[:], dram["L1_wq"]), (wkv[:], dram["L1_wkv"]), (wo[:], dram["L1_wo"]),
                                (blocks[:], dram["L1_blocks"]), (bq[:], dram["L1_bq"]), (bkv[:], dram["L1_bkv"]),
                                (bo[:], dram["L1_bo"]), (gamma[:], dram["L1_gamma"]), (beta[:], dram["L1_beta"])])
        stats_block(core, "a1s", x, LN_EPS)
        stage = sb("a1_stage", [P, TPS, D])
        xT = sb("a1_xT", [D, LEN])
        q_raw, q_exp, q_lin, q = (sb("a1_" + n, [D, LEN]) for n in ("q_raw", "q_exp", "q_lin", "q"))
        kv = sb("a1_kv", [P, TPS, 2 * D])
        k_exp, k_lin, k_sq = (sb("a1_" + n, [P, TPS, D]) for n in ("k_exp", "k_lin", "k_sq"))
        k_sum, k_norm, k_inv = (sb("a1_" + n, [P, TPS * HEADS]) for n in ("k_sum", "k_norm", "k_inv"))
        vk, m = sb("a1_vk", [D, D]), sb("a1_m", [D, D])
        y = sb("a1_y", [P, TPS, D])
        raw, mv, std, inv = sb("a1_raw", [P, TPS, 6]), sb("a1_mv", [P, TPS, 2]), sb("a1_std", [P, TPS]), sb("a1_inv", [P, TPS])
        eps_col = sb("a1_eps_col", [P, 1])
        (eps_set, staged, turned, xT_ready, q_made, q_biased, kv_made, q_exp_ready, kv_ready, k_exp_ready, k_summed, k_rooted,
         q_ready, k_ready, vk_made, vk_ready, m_made, m_ready, y_made, y_varied, y_rooted, chain) = (
            sem("a1_" + n) for n in (
                "eps_set", "staged", "turned", "xT_ready", "q_made", "q_biased", "kv_made", "q_exp_ready", "kv_ready", "k_exp_ready",
                "k_summed", "k_rooted", "q_ready", "k_ready", "vk_made", "vk_ready", "m_made", "m_ready", "y_made",
                "y_varied", "y_rooted", "chain"))
        CHAIN = 12
        with nc.Block() as block:
            @block.vector
            def _(dve):
                nc.vector.memset(eps_col[:], EPS).then_inc(eps_set, 1)
                with dve.Fori(0, SEQS) as b:
                    then = Chain(dve, chain, b * CHAIN)
                    put_normalized(core, dve, b, stage, staged)
                    dve.wait_ge(q_made, b + 1)
                    nc.vector.tensor_scalar(q_raw[:], bank[1][:, 0:LEN], bq[:, 0:1], None, ALU.add).then_inc(q_biased, 1)
                    dve.wait_ge(q_biased, b + 1)
                    then(nc.vector.tensor_scalar(q_lin[:], q_raw[:], 0.0, None, ALU.max))
                    dve.wait_ge(q_exp_ready, b + 1)
                    nc.vector.scalar_tensor_tensor(q[:], q_exp[:], 1.0, q_lin[:], ALU.min, ALU.add).then_inc(q_ready, 1)
                    dve.wait_ge(kv_made, b + 1)
                    nc.vector.tensor_tensor(kv[:], bank[2].rearrange("p (t c) -> p t c", t=TPS),
                                            bkv[:, None, :].to_broadcast([P, TPS, 2 * D]), ALU.add).then_inc(kv_ready, 1)
                    dve.wait_ge(kv_ready, b + 1)
                    then(nc.vector.tensor_scalar(k_lin[:], kv[:, :, 0:D], 0.0, None, ALU.max))
                    dve.wait_ge(k_exp_ready, b + 1)
                    then(nc.vector.scalar_tensor_tensor(k_lin[:], k_exp[:], 1.0, k_lin[:], ALU.min, ALU.add))
                    then(nc.vector.tensor_tensor(k_sq[:], k_lin[:], k_lin[:], ALU.mult))
                    nc.vector.tensor_reduce(k_sum[:], k_sq[:].rearrange("p t (h f) -> p (t h) f", f=HD), AX.X, ALU.add)\
                        .then_inc(k_summed, 1)
                    dve.wait_ge(k_rooted, b + 1)
                    then(nc.vector.reciprocal(k_inv[:], k_norm[:]))
                    nc.vector.tensor_tensor(k_sq[:].rearrange("p t (h f) -> p (t h) f", f=HD),
                                            k_lin[:].rearrange("p t (h f) -> p (t h) f", f=HD),
                                            k_inv[:, :, None].to_broadcast([P, TPS * HEADS, HD]), ALU.mult).then_inc(k_ready, 1)
                    dve.wait_ge(vk_made, b + 1)
                    nc.vector.tensor_tensor(vk[:], bank[3][:, 0:D], blocks[:], ALU.mult).then_inc(vk_ready, 1)
                    dve.wait_ge(y_made, b + 1)
                    then(nc.vector.tensor_tensor(y[:], bank[5][:, 0:LEN].rearrange("p (t d) -> p t d", t=TPS),
                                                 bo[:, None, :].to_broadcast([P, TPS, D]), ALU.add))
                    then(nc.vector.tensor_tensor(y[:], y[:], stage[:], ALU.add))
                    nc.vector.bn_stats(raw[:, 0, :], y[:, 0, :])
                    then(nc.vector.bn_stats(raw[:, 1, :], y[:, 1, :]))
                    xs = x[:, tile(TPS * b, TPS), :]
                    nc.vector.tensor_tensor(xs, xs, beta[:, None, :].to_broadcast([P, TPS, D]), ALU.add)
                    nc.vector.bn_aggr(mv[:, 0, :], raw[:, 0, :])
                    nc.vector.bn_aggr(mv[:, 1, :], raw[:, 1, :]).then_inc(y_varied, 1)
                    dve.wait_ge(y_rooted, b + 1)
                    then(nc.vector.reciprocal(inv[:], std[:]))
                    for t in range(TPS):
                        ins = nc.vector.tensor_scalar(y[:, t, :], y[:, t, :], mv[:, t, 0:1], inv[:, t:t + 1],
                                                      ALU.subtract, ALU.mult)
                    then(ins)
                    then(nc.vector.tensor_tensor(y[:], y[:], gamma[:, None, :].to_broadcast([P, TPS, D]), ALU.mult))
                    then(nc.vector.tensor_tensor(xs, xs, y[:], ALU.add))
                    assert then.n == CHAIN, then.n

            @block.tensor
            def _(pe):
                with pe.Fori(0, SEQS) as b:
                    pe.wait_ge(staged, TPS * b + TPS)
                    for t in range(TPS):
                        mm = pe.transpose(bank[0][:, t * P:(t + 1) * P], stage[:, t, :], core.ident[:])
                    mm.then_inc(turned, 1)
                    pe.wait_ge(xT_ready, b + 1)
                    pe.matmul(bank[1][:, 0:LEN], wq[:], xT[:], start=True, stop=True).then_inc(q_made, 1)
                    for t in range(TPS):
                        mm = pe.matmul(bank[2][:, t * 2 * D:(t + 1) * 2 * D], xT[:, t * P:(t + 1) * P], wkv[:],
                                       start=True, stop=True)
                    mm.then_inc(kv_made, 1)
                    pe.wait_ge(k_ready, b + 1)
                    for t in range(TPS):
                        mm = pe.matmul(bank[3][:, 0:D], kv[:, t, D:2 * D], k_sq[:, t, :], start=t == 0, stop=t == TPS - 1)
                    mm.then_inc(vk_made, 1)
                    pe.wait_ge(vk_ready, b + 1)
                    pe.matmul(bank[4][:, 0:D], vk[:], wo[:], start=True, stop=True).then_inc(m_made, 1)
                    pe.wait_ge(m_ready, b + 1)
                    pe.wait_ge(q_ready, b + 1)
                    for t in range(TPS):
                        mm = pe.matmul(bank[5][:, t * D:(t + 1) * D], q[:, t * P:(t + 1) * P], m[:], start=True, stop=True)
                    mm.then_inc(y_made, 1)

            @block.scalar
            def _(act):
                act.wait_ge(eps_set, 1)
                with act.Fori(0, SEQS) as b:
                    act.wait_ge(turned, b + 1)
                    nc.scalar.copy(xT[:], bank[0][:, 0:LEN]).then_inc(xT_ready, 1)
                    act.wait_ge(q_biased, b + 1)
                    nc.scalar.activation(q_exp[:], q_raw[:], ACT.Exp).then_inc(q_exp_ready, 1)
                    act.wait_ge(kv_ready, b + 1)
                    nc.scalar.activation(k_exp[:], kv[:, :, 0:D], ACT.Exp).then_inc(k_exp_ready, 1)
                    act.wait_ge(k_summed, b + 1)
                    nc.scalar.activation(k_norm[:], k_sum[:], ACT.Sqrt, bias=eps_col[:]).then_inc(k_rooted, 1)
                    act.wait_ge(m_made, b + 1)
                    nc.scalar.copy(m[:], bank[4][:, 0:D]).then_inc(m_ready, 1)
                    act.wait_ge(y_varied, b + 1)
                    nc.scalar.activation(std[:], mv[:, :, 1], ACT.Sqrt, bias=eps_col[:]).then_inc(y_rooted, 1)


def l1_feedforward(core):
    nc, x, bank, dram = core.nc, core.x, core.bank, core.dram
    H = 512
    C = H // P
    with ExitStack() as stack:
        sb, sem = scratch(core, stack)
        fc, proj = sb("f1_fc", [P, C, D]), sb("f1_proj", [P, H])
        ln_w, ln_b = sb("f1_ln_w", [P, C]), sb("f1_ln_b", [P, C])
        load_block(core, "f1", [(fc[:], dram["L1_fc"].rearrange("(c p) d -> p c d", p=P)), (proj[:], dram["L1_proj"]),
                                (ln_w[:], dram["L1_ln_w"]), (ln_b[:], dram["L1_ln_b"])])
        stats_block(core, "f1s", x, LN_EPS)

        ones = sb("f1_ones", [P, P])
        total, edge = sb("f1_total", [P, 2]), sb("f1_edge", [P, 2, 2])
        tern, below = sb("f1_tern", [P, 2, H]), sb("f1_below", [P, 2, H])
        w1, w2, w2_plain = sb("f1_w1", [D, H]), sb("f1_w2", [P, C, D]), sb("f1_w2_plain", [P, C, D])
        b_rows, shift = sb("f1_b_rows", [P, C, P]), sb("f1_shift", [P, D])
        made, product = sem("f1_made"), sem("f1_product")
        with nc.Block() as block:
            @block.vector
            def _(dve):
                then = Chain(dve, made)
                nc.vector.memset(ones[:], 1.0)
                nc.vector.tensor_reduce(total[:, 0:1], fc[:].rearrange("p c d -> p (c d)"), AX.X, ALU.add, apply_absolute_value=True)
                then(nc.vector.tensor_reduce(total[:, 1:2], proj[:], AX.X, ALU.add, apply_absolute_value=True))
                dve.wait_ge(product, 1)
                then(nc.vector.tensor_scalar(edge[:, 0], bank[0][:, 0:2], 1.0 / (H * D), 1e-6, ALU.mult, ALU.add))
                then(nc.vector.tensor_scalar(edge[:, 1], edge[:, 0], -0.5, None, ALU.mult))
                then(nc.vector.tensor_scalar(edge[:, 0], edge[:, 0], 0.5, None, ALU.mult))
                for n, src in ((0, fc[:].rearrange("p c d -> p (c d)")), (1, proj[:])):
                    then(nc.vector.tensor_scalar(below[:, n], src, edge[:, 1, n:n + 1], None, ALU.is_lt))
                    then(nc.vector.scalar_tensor_tensor(tern[:, n], src, edge[:, 0, n:n + 1], below[:, n],
                                                        ALU.is_gt, ALU.subtract))
                for c in range(C):
                    nc.vector.tensor_copy(b_rows[:, c, :], ln_b[:, c:c + 1].to_broadcast([P, P]))
                dve.wait_ge(product, 2)
                nc.vector.tensor_copy(w1[:], bank[1])
                for c in range(C):
                    nc.vector.tensor_scalar(w2[:, c, :], bank[2][:, c * D:(c + 1) * D], ln_w[:, c:c + 1], None, ALU.mult)
                then(nc.vector.tensor_copy(w2_plain[:].rearrange("p c d -> p (c d)"), bank[2]))
                dve.wait_ge(product, 3)
                nc.vector.tensor_copy(shift[:], bank[3][:, 0:D])

            @block.tensor
            def _(pe):
                pe.wait_ge(made, 1)
                pe.matmul(bank[0][:, 0:2], ones[:], total[:], start=True, stop=True).then_inc(product, 1)
                pe.wait_ge(made, 8)
                for c in range(C):
                    pe.transpose(bank[1][:, c * P:(c + 1) * P], tern[:, 0, c * P:(c + 1) * P], core.ident[:])
                    mm = pe.transpose(bank[2][:, c * P:(c + 1) * P], tern[:, 1, c * P:(c + 1) * P], core.ident[:])
                mm.then_inc(product, 1)
                pe.wait_ge(made, 9)
                for c in range(C):
                    mm = pe.matmul(bank[3][:, 0:D], b_rows[:, c, :], w2_plain[:, c, :], start=c == 0, stop=c == C - 1)
                mm.then_inc(product, 1)

        hid = sb("f1_hid", [P, TILES, H])
        stage, xT = sb("f1_stage", [P, TPS, D]), sb("f1_xT", [D, LEN])
        staged, turned, xT_ready, hidden, bent = (sem("f1_" + n) for n in ("staged", "turned", "xT_ready", "hidden", "bent"))
        with nc.Block() as block:
            @block.vector
            def _(dve):
                dve.sem_inc(turned, 1)
                with dve.Fori(0, SEQS) as b:
                    dve.wait_ge(turned, b + 1)
                    put_normalized(core, dve, b, stage, staged)

            @block.tensor
            def _(pe):
                with pe.Fori(0, SEQS) as b:
                    pe.wait_ge(staged, TPS * b + TPS)
                    for t in range(TPS):
                        mm = pe.transpose(bank[0][:, t * P:(t + 1) * P], stage[:, t, :], core.ident[:])
                    mm.then_inc(turned, 1)
                    pe.wait_ge(xT_ready, b + 1)
                    for t in range(TPS):
                        mm = pe.matmul(bank[1 + t], xT[:, t * P:(t + 1) * P], w1[:], start=True, stop=True)
                    mm.then_inc(hidden, 1)

            @block.scalar
            def _(act):
                with act.Fori(0, SEQS) as b:
                    act.wait_ge(turned, b + 2)
                    nc.scalar.copy(xT[:], bank[0][:, 0:LEN]).then_inc(xT_ready, 1)
                    act.wait_ge(hidden, b + 1)
                    nc.scalar.activation(hid[:, tile(TPS * b, TPS), :], core.banks[:, 1:3, :], ACT.Gelu).then_inc(bent, 1)

        stats_block(core, "f1h", hid, LN_EPS, width=H)

        norm, normT = sb("f1_norm", [P, TPS, H]), sb("f1_normT", [P, TPS, H])
        normed, flipped, normT_ready, projected, added = (sem("f1_" + n) for n in
                                                          ("normed", "flipped", "normT_ready", "projected", "added"))
        with nc.Block() as block:
            @block.vector
            def _(dve):
                with dve.Fori(0, SEQS) as b:
                    for t in range(TPS):
                        i = TPS * b + t
                        nc.vector.tensor_scalar(norm[:, t, :], flat(hid[:, tile(i), :]), core.mean[:, tile(i)],
                                                core.rstd[:, tile(i)], ALU.subtract, ALU.mult).then_inc(normed, 1)
                    dve.wait_ge(projected, b + 1)
                    xs = x[:, tile(TPS * b, TPS), :]
                    nc.vector.tensor_tensor(xs, xs, bank[3][:, 0:LEN].rearrange("p (t d) -> p t d", t=TPS), ALU.add)\
                        .then_inc(added, 1)
                    dve.wait_ge(added, 2 * b + 1)
                    nc.vector.tensor_tensor(xs, xs, shift[:, None, :].to_broadcast([P, TPS, D]), ALU.add).then_inc(added, 1)

            @block.tensor
            def _(pe):
                with pe.Fori(0, SEQS) as b:
                    for t in range(TPS):
                        pe.wait_ge(normed, TPS * b + t + 1)
                        for c in range(C):
                            mm = pe.transpose(bank[1 + t][:, c * P:(c + 1) * P], norm[:, t, c * P:(c + 1) * P], core.ident[:])
                        mm.then_inc(flipped, 1)
                    for t in range(TPS):
                        pe.wait_ge(normT_ready, TPS * b + t + 1)
                        for c in range(C):
                            mm = pe.matmul(bank[3][:, t * D:(t + 1) * D], normT[:, t, c * P:(c + 1) * P], w2[:, c, :],
                                           start=c == 0, stop=c == C - 1)
                    mm.then_inc(projected, 1)

            @block.scalar
            def _(act):
                with act.Fori(0, SEQS) as b:
                    for t in range(TPS):
                        act.wait_ge(flipped, TPS * b + t + 1)
                        nc.scalar.copy(normT[:, t, :], bank[1 + t]).then_inc(normT_ready, 1)


def l2_attention(core):
    nc, x, bank, dram = core.nc, core.x, core.bank, core.dram
    HEADS, HD, G = 16, 8, 4
    R = P // G
    with ExitStack() as stack:
        sb, sem = scratch(core, stack)
        wq, wk, wv = sb("a2_wq", [D, G, P]), sb("a2_wk", [D, G, P]), sb("a2_wv", [D, D])
        wo, bo, bv = sb("a2_wo", [D, D]), sb("a2_bo", [P, D]), sb("a2_bv", [P, D])
        bq, bk = sb("a2_bq", [P, G]), sb("a2_bk", [P, G])
        apart_f = sb("a2_apart_f", [P, TPS, LEN])
        slopes = sb("a2_slopes", [P, len(SLOPE_PARTS)])
        load_block(core, "a2", [(wq[:], dram["L2_wq"]), (wk[:], dram["L2_wk"]), (wv[:], dram["L2_wv"]), (wo[:], dram["L2_wo"]),
                                (bo[:], dram["L2_bo"]), (bv[:], dram["L2_bv"]), (bq[:], dram["L2_bq"]), (bk[:], dram["L2_bk"]),
                                (apart_f[:], dram["L2_apart"]), (slopes[:], dram["L2_slopes"])])
        stats_block(core, "a2s", x, LN_EPS)
        apart = sb("a2_apart", [P, TPS, LEN], BF16)
        diag = sb("a2_diag", [P, len(SLOPE_PARTS), P], BF16)
        first_part = [sum(1 for h, _ in SLOPE_PARTS if h < n) for n in range(HEADS + 1)]
        with nc.Block() as block:
            @block.vector
            def _(dve):
                nc.vector.tensor_copy(apart[:], apart_f[:])
                for n in range(len(SLOPE_PARTS)):
                    nc.vector.tensor_scalar(diag[:, n, :], core.ident[:], slopes[:, n:n + 1], None, ALU.mult)

        stage, xT = sb("a2_stage", [P, TPS, D]), sb("a2_xT", [D, LEN])
        q, k, v = sb("a2_q", [P, G, LEN]), sb("a2_k", [P, G, LEN]), sb("a2_v", [P, TPS, D])
        neg_top, total, inv = sb("a2_neg_top", [P, 2, TPS]), sb("a2_total", [P, TPS, HEADS]), sb("a2_inv", [P, TPS, HEADS])
        prob, probT = sb("a2_prob", [P, 2, TPS, LEN]), sb("a2_probT", [P, 2, 2 * LEN])
        att, attT = sb("a2_att", [P, TPS, D]), sb("a2_attT", [D, LEN])
        (staged, turned, xT_ready, projected, q_ready, k_ready, v_ready, scored, topped, expd, flipped, probT_ready, summed,
         inverted, att_ready, att_turned, attT_ready, out_made, added) = (
            sem("a2_" + n) for n in (
                "staged", "turned", "xT_ready", "projected", "q_ready", "k_ready", "v_ready", "scored", "topped", "expd",
                "flipped", "probT_ready", "summed", "inverted", "att_ready", "att_turned", "attT_ready", "out_made", "added"))
        with nc.Block() as block:
            @block.vector
            def _(dve):
                with dve.Fori(0, SEQS) as b:
                    put_normalized(core, dve, b, stage, staged)
                    dve.wait_ge(projected, b + 1)
                    for g in range(G):
                        nc.vector.tensor_scalar(q[:, g, :], bank[g // 2][:, g % 2 * LEN:(g % 2 + 1) * LEN], bq[:, g:g + 1],
                                                float(HD) ** -0.5, ALU.add, ALU.mult).then_inc(q_ready, 1)
                    nc.vector.tensor_tensor(v[:], bank[4][:, 0:LEN].rearrange("p (t d) -> p t d", t=TPS),
                                            bv[:, None, :].to_broadcast([P, TPS, D]), ALU.add).then_inc(v_ready, 1)
                    for h in range(HEADS + 1):
                        if h < HEADS:
                            dve.wait_ge(scored, b * HEADS + h + 1)
                            nc.vector.tensor_reduce(neg_top[:, h % 2, :], bank[h % 2].rearrange("p (t k) -> p t k", t=TPS),
                                                    AX.X, ALU.max, negate=True).then_inc(topped, 1)
                        if h >= 1:
                            u = h - 1
                            dve.wait_ge(flipped, b * HEADS + u + 1)
                            if u >= 2:
                                dve.wait_ge(summed, b * HEADS + u - 1)
                            nc.vector.tensor_copy(probT[:, u % 2, :], bank[2 + u % 2]).then_inc(probT_ready, 1)
                    nc.vector.reciprocal(inv[:], total[:]).then_inc(inverted, 1)
                    dve.wait_ge(inverted, b + 1)
                    dve.wait_ge(summed, b * HEADS + HEADS)
                    nc.vector.tensor_tensor(att[:].rearrange("p t (h f) -> p (t h) f", f=HD),
                                            bank[5][:, 0:LEN].rearrange("p (a f) -> p a f", f=HD),
                                            inv[:].rearrange("p t h -> p (t h)")[:, :, None].to_broadcast([P, TPS * HEADS, HD]),
                                            ALU.mult).then_inc(att_ready, 1)
                    dve.wait_ge(out_made, b + 1)
                    xs = x[:, tile(TPS * b, TPS), :]
                    nc.vector.tensor_tensor(xs, xs, bank[7][:, 0:LEN].rearrange("p (t d) -> p t d", t=TPS), ALU.add)\
                        .then_inc(added, 1)
                    dve.wait_ge(added, 2 * b + 1)
                    nc.vector.tensor_tensor(xs, xs, bo[:, None, :].to_broadcast([P, TPS, D]), ALU.add).then_inc(added, 1)

            @block.tensor
            def _(pe):
                def scores(b, h):
                    g, r = h // G, h % G * R
                    if h >= 2:
                        pe.wait_ge(expd, b * HEADS + h - 1)
                    for t in range(TPS):
                        out = bank[h % 2][:, t * LEN:(t + 1) * LEN]
                        for n in range(first_part[h], first_part[h + 1]):
                            pe.matmul(out, diag[:, n, :], apart[:, t, :], start=n == first_part[h], stop=False)
                        mm = pe.matmul(out, q[r:r + R, g, t * P:(t + 1) * P], k[r:r + R, g, :], start=False, stop=True)
                    mm.then_inc(scored, 1)

                def attend(b, h):
                    pe.wait_ge(expd, b * HEADS + h + 1)
                    for t in range(TPS):
                        for c in range(TPS):
                            mm = pe.transpose(bank[2 + h % 2][:, (t * TPS + c) * P:(t * TPS + c + 1) * P],
                                              prob[:, h % 2, t, c * P:(c + 1) * P], core.ident[:])
                    mm.then_inc(flipped, 1)

                def values(b, h):
                    pe.wait_ge(probT_ready, b * HEADS + h + 1)
                    for t in range(TPS):
                        for c in range(TPS):
                            o = t * D + h * HD
                            mm = pe.matmul(bank[5][:, o:o + HD], probT[:, h % 2, (t * TPS + c) * P:(t * TPS + c + 1) * P],
                                           v[:, c, h * HD:(h + 1) * HD], start=c == 0, stop=c == TPS - 1)
                    mm.then_inc(summed, 1)

                with pe.Fori(0, SEQS) as b:
                    pe.wait_ge(staged, TPS * b + TPS)
                    for t in range(TPS):
                        mm = pe.transpose(bank[6][:, t * P:(t + 1) * P], stage[:, t, :], core.ident[:])
                    mm.then_inc(turned, 1)
                    pe.wait_ge(xT_ready, b + 1)
                    for g in range(G):
                        pe.matmul(bank[g // 2][:, g % 2 * LEN:(g % 2 + 1) * LEN], wq[:, g, :], xT[:], start=True, stop=True)
                        pe.matmul(bank[2 + g // 2][:, g % 2 * LEN:(g % 2 + 1) * LEN], wk[:, g, :], xT[:], start=True, stop=True)
                    for t in range(TPS):
                        mm = pe.matmul(bank[4][:, t * D:(t + 1) * D], xT[:, t * P:(t + 1) * P], wv[:], start=True, stop=True)
                    mm.then_inc(projected, 1)
                    pe.wait_ge(q_ready, b * G + G)
                    pe.wait_ge(k_ready, b * G + G)
                    pe.wait_ge(v_ready, b + 1)
                    for h in range(HEADS + 2):
                        if h < HEADS:
                            scores(b, h)
                        if h >= 2:
                            values(b, h - 2)
                        if 1 <= h <= HEADS:
                            attend(b, h - 1)
                    pe.wait_ge(att_ready, b + 1)
                    for t in range(TPS):
                        mm = pe.transpose(bank[6][:, t * P:(t + 1) * P], att[:, t, :], core.ident[:])
                    mm.then_inc(att_turned, 1)
                    pe.wait_ge(attT_ready, b + 1)
                    for t in range(TPS):
                        mm = pe.matmul(bank[7][:, t * D:(t + 1) * D], attT[:, t * P:(t + 1) * P], wo[:], start=True, stop=True)
                    mm.then_inc(out_made, 1)

            @block.scalar
            def _(act):
                with act.Fori(0, SEQS) as b:
                    act.wait_ge(turned, b + 1)
                    nc.scalar.copy(xT[:], bank[6][:, 0:LEN]).then_inc(xT_ready, 1)
                    act.wait_ge(projected, b + 1)
                    for g in range(G):
                        nc.scalar.activation(k[:, g, :], bank[2 + g // 2][:, g % 2 * LEN:(g % 2 + 1) * LEN], ACT.Identity,
                                             bias=bk[:, g:g + 1]).then_inc(k_ready, 1)
                    for h in range(HEADS):
                        act.wait_ge(topped, b * HEADS + h + 1)
                        if h >= 2:
                            act.wait_ge(flipped, b * HEADS + h - 1)
                        for t in range(TPS):
                            e = nc.scalar.activation(prob[:, h % 2, t, :], bank[h % 2][:, t * LEN:(t + 1) * LEN], ACT.Exp,
                                                     bias=neg_top[:, h % 2, t:t + 1], accum_out=total[:, t, h:h + 1])
                        e.then_inc(expd, 1)
                    act.wait_ge(att_turned, b + 1)
                    nc.scalar.copy(attT[:], bank[6][:, 0:LEN]).then_inc(attT_ready, 1)


def l2_feedforward(core):
    nc, dram = core.nc, core.dram
    DEPTH = 6
    with ExitStack() as stack:
        sb, sem = scratch(core, stack)
        tables = sb("r_tables", [P, 2, 2, LEN])
        masks_f = sb("r_masks_f", [P, TPS, WINDOW_KEYS])
        masks = sb("r_masks", [P, TPS, WINDOW_KEYS], BF16)
        head_ones = sb("r_head_ones", [P, 2])
        load_block(core, "r", [(tables[:], dram["r_tables"]), (masks_f[:], dram["r_masks"]), (head_ones[:], dram["r_head_ones"])])
        with nc.Block() as block:
            @block.vector
            def _(dve):
                nc.vector.tensor_copy(masks[:], masks_f[:])

        saved = sb("r_saved", [P, TILES, D])
        enter_stream(core, "rs", saved)
        with nc.Fori(0, DEPTH) as layer:
            windowed_attention(core, layer, tables, masks, head_ones)
            gated_feedforward(core, layer)
        leave_stream(core, saved)


HEADS2, HD2 = 16, 64
WINDOW = 32
PAIRS2 = HEADS2 // 2
WINDOW_KEYS = WINDOW + P


def windowed_attention(core, layer, tables, masks, head_ones):
    nc, x, bank, dram = core.nc, core.x, core.bank, core.dram
    INNER = HEADS2 * HD2
    H2 = INNER // 2
    with ExitStack() as stack:
        sb, sem = scratch(core, stack)
        w = sb("w_w", [D, 5, INNER])
        wo = sb("w_wo", [P, PAIRS2, D])
        qk_scale = sb("w_qk_scale", [P, 4])
        load_layer(core, "w", [(w[:].rearrange("p a n -> p (a n)"), flat2(dram["r_w"][tile(layer)])),
                               (wo[:].rearrange("p a n -> p (a n)"), flat2(dram["r_wo"][tile(layer)])),
                               (qk_scale[:], flat2(dram["r_qk_scale"][tile(layer)]))], layer)
        cos_t, sin_t = sb("w_cos", [P, 2 * LEN]), sb("w_sin", [P, 2 * LEN])
        stage, xT = sb("w_stage", [P, LEN]), sb("w_xT", [D, LEN + 1])
        v = sb("w_v", [P, TPS, INNER])
        by_cos, by_sin, square = (sb("w_" + n, [P, 2, 2 * LEN]) for n in ("by_cos", "by_sin", "square"))
        rope = sb("w_rope", [P, PAIRS2, 2 * LEN])
        NORMS = 2 * TPS * HEADS2
        norm, inv_norm = sb("w_norm", [P, NORMS]), sb("w_inv_norm", [P, NORMS])
        k_inv = sb("w_k_inv", [P, TPS, HEADS2, HD2])
        k = sb("w_k", [P, 2, WINDOW + LEN])
        top, neg_top = (sb("w_" + n, [P, 2, 4]) for n in ("top", "neg_top"))
        total, inv = sb("w_total", [P, 4, 4]), sb("w_inv", [P, 4, 4])
        prob = sb("w_prob", [P, 2, 4, 2 * P])
        probT = sb("w_probT", [P, 2, 4 * P])
        prevT = sb("w_prevT", [P, 2, 2, P])
        att, attT = sb("w_att", [P, 2, TPS * P]), sb("w_attT", [P, 2, LEN])
        names = ("tabled", "staged", "turned", "xT_ready", "v_made", "v_low", "v_high", "qk_made", "cos_done", "sin_done",
                 "squared", "roped", "sums_made", "rooted", "norms_ready", "k_spread", "k_turned", "k_ready", "scored",
                 "topped", "expd", "flipped", "probT_ready", "prevT_ready", "attended", "att_ready", "att_turned",
                 "attT_ready", "out_made", "added", "inverted")
        (tabled, staged, turned, xT_ready, v_made, v_low, v_high, qk_made, cos_done, sin_done, squared, roped, sums_made,
         rooted, norms_ready, k_spread, k_turned, k_ready, scored, topped, expd, flipped, probT_ready, prevT_ready, attended,
         att_ready, att_turned, attT_ready, out_made, added, inverted) = (sem("w_" + n) for n in names)
        BS = layer * SEQS
        US = layer * (SEQS * PAIRS2)
        norms4 = inv_norm[:].rearrange("p (i t h) -> p i t h", i=2, t=TPS)

        with nc.Block() as block:
            @block.vector
            def _(dve):
                for i in range(2):
                    s = slice(i * LEN, (i + 1) * LEN)
                    nc.vector.tensor_scalar(cos_t[:, s], tables[:, 0, i], qk_scale[:, i:i + 1], None, ALU.mult)
                    nc.vector.tensor_scalar(sin_t[:, s], tables[:, 1, i], qk_scale[:, 2 + i:3 + i], None, ALU.mult)
                nc.vector.memset(xT[:], 0.0)
                nc.vector.memset(k[:], 0.0)

            @block.gpsimd
            def _(pool):
                nc.gpsimd.memset(prob[:], 0.0)
                nc.gpsimd.memset(prevT[:], 0.0)

        with nc.Block() as block:
            @block.tensor
            def _(pe):
                def project(b, hp):
                    u, a = US + b * PAIRS2 + hp, 2 * (hp % 2)
                    if hp >= 2:
                        pe.wait_ge(squared, u - 1)
                        pe.wait_ge(sin_done, u - 1)
                    for n in range(4):
                        mm = pe.matmul(bank[a + n % 2][:, n // 2 * LEN:(n // 2 + 1) * LEN], w[:, n, hp * P:(hp + 1) * P],
                                       xT[:, 0:LEN], start=True, stop=True)
                    mm.then_inc(qk_made, 1)

                def sums(b, hp):
                    pe.wait_ge(squared, US + b * PAIRS2 + hp + 1)
                    for i in range(2):
                        for t in range(TPS):
                            o = (i * TPS + t) * HEADS2 + 2 * hp
                            mm = pe.matmul(bank[5][:, o:o + 2], square[:, hp % 2, i * LEN + t * P:i * LEN + (t + 1) * P],
                                           head_ones[:], start=True, stop=True)
                    mm.then_inc(sums_made, 1)

                def spread(b, hp):
                    if hp == 0:
                        pe.wait_ge(k_spread, BS + b + 1)
                    for t in range(TPS):
                        mm = pe.transpose(bank[5][:, t * P:(t + 1) * P],
                                          k_inv[:, t, 2 * hp:2 * hp + 2, :].rearrange("p h f -> p (h f)"), core.ident[:])
                    mm.then_inc(k_turned, 1)

                def scores(b, hp):
                    u = US + b * PAIRS2 + hp
                    pe.wait_ge(k_ready, u + 1)
                    if hp >= 2:
                        pe.wait_ge(expd, u - 1)
                    for h in range(2):
                        pe.matmul(bank[2 * (hp % 2) + h][:, 0:TPS * WINDOW_KEYS], core.ident_bf[:],
                                  masks[:].rearrange("p t k -> p (t k)"), start=True, stop=False)
                    for t in range(TPS):
                        for h in range(2):
                            mm = pe.matmul(bank[2 * (hp % 2) + h][:, t * WINDOW_KEYS:(t + 1) * WINDOW_KEYS],
                                           rope[HD2 * h:HD2 * (h + 1), hp, t * P:(t + 1) * P],
                                           k[HD2 * h:HD2 * (h + 1), hp % 2, t * P:t * P + WINDOW_KEYS], start=False, stop=t == TPS - 1)
                    mm.then_inc(scored, 1)

                def flip(b, hp):
                    u, a = US + b * PAIRS2 + hp, hp % 2
                    pe.wait_ge(expd, u + 1)
                    if hp >= 1:
                        pe.wait_ge(att_ready, u)
                    for j in range(4):
                        pe.transpose(bank[4][:, j * P:(j + 1) * P], prob[:, a, j, P:2 * P], core.ident[:])
                    for h in range(2):
                        mm = pe.transpose(bank[6][:, h * WINDOW:(h + 1) * WINDOW], prob[0:WINDOW, a, 2 + h, 0:P],
                                          core.ident[0:WINDOW, 0:WINDOW])
                    mm.then_inc(flipped, 1)

                def attend(b, hp):
                    u, a = US + b * PAIRS2 + hp, hp % 2
                    pe.wait_ge(probT_ready, u + 1)
                    pe.wait_ge(prevT_ready, u + 1)
                    for t in range(TPS):
                        for h in range(2):
                            j = 2 * t + h
                            out = bank[6][:, P + j * HD2:P + (j + 1) * HD2]
                            hs = slice((2 * hp + h) * HD2, (2 * hp + h + 1) * HD2)
                            mm = pe.matmul(out, probT[:, a, j * P:(j + 1) * P], v[:, t, hs], start=True, stop=t == 0)
                            if t == 1:
                                mm = pe.matmul(out, prevT[:, a, h, :], v[:, 0, hs], start=False, stop=True)
                    mm.then_inc(attended, 1)

                def turn_att(b, hp):
                    u, a = US + b * PAIRS2 + hp, hp % 2
                    pe.wait_ge(att_ready, u + 1)
                    if hp + 3 < PAIRS2:
                        pe.wait_ge(k_ready, u + 4)
                    for t in range(TPS):
                        mm = pe.transpose(bank[5][:, LEN + t * P:LEN + (t + 1) * P], att[:, a, t * P:(t + 1) * P], core.ident[:])
                    mm.then_inc(att_turned, 1)

                def output(b, hp):
                    pe.wait_ge(attT_ready, US + b * PAIRS2 + hp + 1)
                    for t in range(TPS):
                        mm = pe.matmul(bank[7][:, t * D:(t + 1) * D], attT[:, hp % 2, t * P:(t + 1) * P], wo[:, hp, :],
                                       start=hp == 0 and t == 0, stop=hp == PAIRS2 - 1, skip_group_check=True)
                    if hp == PAIRS2 - 1:
                        mm.then_inc(out_made, 1)

                with pe.Fori(0, SEQS) as b:
                    pe.wait_ge(staged, BS + b + 1)
                    for t in range(TPS):
                        mm = pe.transpose(bank[4][:, t * P:(t + 1) * P], stage[:, t * P:(t + 1) * P], core.ident[:])
                    mm.then_inc(turned, 1)
                    pe.wait_ge(xT_ready, BS + b + 1)
                    for t in range(TPS):
                        for n in range(2):
                            mm = pe.matmul(bank[2 * t + n], xT[:, t * P:(t + 1) * P], w[:, 4, n * H2:(n + 1) * H2],
                                           start=True, stop=True)
                        mm.then_inc(v_made, 1)
                    for s in range(PAIRS2 + 1):
                        if s == 0:
                            pe.wait_ge(v_low, BS + b + 1)
                        if s == 1:
                            pe.wait_ge(v_high, BS + b + 1)
                        if s < PAIRS2:
                            project(b, s)
                        if s >= 1:
                            sums(b, s - 1)
                    pe.wait_ge(rooted, BS + b + 1)
                    pe.wait_ge(sin_done, US + b * PAIRS2 + PAIRS2)
                    spread(b, 0)
                    for s in range(PAIRS2 + 3):
                        if s < PAIRS2:
                            scores(b, s)
                        if 2 <= s < PAIRS2 + 2:
                            attend(b, s - 2)
                        if s >= 3:
                            output(b, s - 3)
                        if s + 1 < PAIRS2:
                            spread(b, s + 1)
                        if 1 <= s <= PAIRS2:
                            flip(b, s - 1)
                        if 2 <= s < PAIRS2 + 2:
                            turn_att(b, s - 2)

            @block.vector
            def _(dve):
                with dve.Fori(0, SEQS) as b:
                    nc.vector.tensor_copy(stage[:], x[:, tile(TPS * b, TPS), :].rearrange("p t d -> p (t d)")).then_inc(staged, 1)
                    dve.wait_ge(v_made, TPS * (BS + b) + 2)
                    nc.vector.tensor_copy(v[:, 1, :].rearrange("p (a n) -> p a n", a=2), core.banks[:, 2:4, :]).then_inc(v_high, 1)
                    for hp in range(PAIRS2):
                        u, a = US + b * PAIRS2 + hp, hp % 2
                        dve.wait_ge(qk_made, u + 1)
                        if hp >= 2:
                            dve.wait_ge(roped, u - 1)
                        nc.vector.tensor_tensor(by_cos[:, a, :], bank[2 * a], cos_t[:], ALU.mult).then_inc(cos_done, 1)
                        nc.vector.tensor_tensor(by_sin[:, a, :], bank[2 * a + 1], sin_t[:], ALU.mult).then_inc(sin_done, 1)
                    dve.wait_ge(rooted, BS + b + 1)
                    nc.vector.tensor_scalar(norm[:], norm[:], 1e-12, None, ALU.max).then_inc(norms_ready, 1)
                    dve.wait_ge(norms_ready, 2 * (BS + b) + 1)
                    nc.vector.reciprocal(inv_norm[:], norm[:]).then_inc(norms_ready, 1)
                    for s in range(-1, PAIRS2 + 2):
                        if 0 <= s < PAIRS2:
                            u, a = US + b * PAIRS2 + s, s % 2
                            dve.wait_ge(scored, u + 1)
                            nc.vector.tensor_reduce(top[:, a, :].rearrange("p (t h) -> p t h", t=2),
                                                    core.banks[:, 2 * a:2 * a + 2, 0:2 * WINDOW_KEYS]
                                                    .rearrange("p h (t c) -> p t h c", t=2), AX.X, ALU.max, negate=True)\
                                .then_inc(topped, 1)
                            dve.wait_ge(topped, 2 * u + 1)
                            if s == 0:
                                dve.wait_ge(norms_ready, 2 * (BS + b) + 2)
                            nc.vector.tensor_tensor(neg_top[:, a, :].rearrange("p (t h) -> p t h", t=2),
                                                    top[:, a, :].rearrange("p (t h) -> p t h", t=2),
                                                    norms4[:, 0, :, 2 * s:2 * s + 2], ALU.mult).then_inc(topped, 1)
                        if s >= 2:
                            hp = s - 2
                            u, a = US + b * PAIRS2 + hp, hp % 2
                            dve.wait_ge(inverted, u + 1)
                            dve.wait_ge(attended, u + 1)
                            if hp >= 2:
                                dve.wait_ge(att_turned, u - 1)
                            nc.vector.tensor_tensor(att[:, a, :].rearrange("p (j f) -> p j f", j=4),
                                                    bank[6][:, P:P + 4 * HD2].rearrange("p (j f) -> p j f", j=4),
                                                    inv[:, hp % 4, :, None].to_broadcast([P, 4, HD2]), ALU.mult).then_inc(att_ready, 1)
                        if s + 1 < PAIRS2:
                            hp = s + 1
                            u = US + b * PAIRS2 + hp
                            dve.wait_ge(k_turned, u + 1)
                            dve.wait_ge(roped, u + 1)
                            if hp >= 2:
                                dve.wait_ge(scored, u - 1)
                            nc.vector.tensor_tensor(k[:, hp % 2, WINDOW:], rope[:, hp, LEN:2 * LEN], bank[5][:, 0:LEN], ALU.mult)\
                                .then_inc(k_ready, 1)
                        if 1 <= s <= PAIRS2:
                            hp = s - 1
                            u, a = US + b * PAIRS2 + hp, hp % 2
                            dve.wait_ge(flipped, u + 1)
                            if hp >= 2:
                                dve.wait_ge(attended, u - 1)
                            nc.vector.tensor_copy(prevT[:, a, :, 0:WINDOW],
                                                  bank[6][:, 0:2 * WINDOW].rearrange("p (h q) -> p h q", h=2)).then_inc(prevT_ready, 1)
                            nc.vector.reciprocal(inv[:, hp % 4, :], total[:, hp % 4, :]).then_inc(inverted, 1)
                    dve.wait_ge(out_made, BS + b + 1)
                    xs = x[:, tile(TPS * b, TPS), :]
                    nc.vector.tensor_tensor(xs, xs, bank[7][:, 0:LEN].rearrange("p (t d) -> p t d", t=TPS), ALU.add)

            @block.gpsimd
            def _(pool):
                with pool.Fori(0, SEQS) as b:
                    for hp in range(PAIRS2):
                        pool.wait_ge(sin_done, US + b * PAIRS2 + hp + 1)
                        nc.gpsimd.tensor_tensor(rope[:, hp, :], by_cos[:, hp % 2, :], by_sin[:, hp % 2, :], ALU.add).then_inc(roped, 1)
                    pool.wait_ge(norms_ready, 2 * (BS + b) + 2)
                    pool.sem_inc(core.passed, 1)
                    nc.gpsimd.tensor_copy(k_inv[:], norms4[:, 1, :, :, None].to_broadcast([P, TPS, HEADS2, HD2])).then_inc(k_spread, 1)

            @block.scalar
            def _(act):
                with act.Fori(0, SEQS) as b:
                    act.wait_ge(turned, BS + b + 1)
                    nc.scalar.copy(xT[0:HD2, 0:LEN], bank[4][0:HD2, 0:LEN])
                    nc.scalar.copy(xT[HD2:P, 1:LEN + 1], bank[4][HD2:P, 0:LEN]).then_inc(xT_ready, 1)
                    act.wait_ge(v_made, TPS * (BS + b) + 1)
                    nc.scalar.copy(v[:, 0, :].rearrange("p (a n) -> p a n", a=2), core.banks[:, 0:2, :]).then_inc(v_low, 1)
                    for hp in range(PAIRS2):
                        u, a = US + b * PAIRS2 + hp, hp % 2
                        act.wait_ge(cos_done, u + 1)
                        if hp >= 2:
                            act.wait_ge(sums_made, u - 1)
                        nc.scalar.activation(square[:, a, :], bank[2 * a], ACT.Square).then_inc(squared, 1)
                    act.wait_ge(sums_made, US + b * PAIRS2 + PAIRS2)
                    nc.scalar.activation(norm[:], bank[5][:, 0:NORMS], ACT.Sqrt).then_inc(rooted, 1)
                    for s in range(PAIRS2 + 3):
                        if s >= 3:
                            hp = s - 3
                            u, a = US + b * PAIRS2 + hp, hp % 2
                            act.wait_ge(att_turned, u + 1)
                            nc.scalar.copy(attT[:, a, :], bank[5][:, LEN:2 * LEN]).then_inc(attT_ready, 1)
                        if s < PAIRS2:
                            u, a = US + b * PAIRS2 + s, s % 2
                            act.wait_ge(topped, 2 * u + 2)
                            if s >= 2:
                                act.wait_ge(flipped, u - 1)
                            for j in range(4):
                                t, h = j // 2, j % 2
                                e = nc.scalar.activation(prob[:, a, j, P - WINDOW:2 * P],
                                                         bank[2 * a + h][:, t * WINDOW_KEYS:(t + 1) * WINDOW_KEYS], ACT.Exp,
                                                         bias=neg_top[:, a, j:j + 1], scale=norms4[:, 0, t, 2 * s + h:2 * s + h + 1],
                                                         accum_out=total[:, s % 4, j:j + 1])
                            e.then_inc(expd, 1)
                        if 1 <= s <= PAIRS2:
                            hp = s - 1
                            act.wait_ge(flipped, US + b * PAIRS2 + hp + 1)
                            nc.scalar.copy(probT[:, hp % 2, :], bank[4]).then_inc(probT_ready, 1)


def gated_feedforward(core, layer):
    nc, x, bank, dram = core.nc, core.x, core.bank, core.dram
    C = 3
    HALF = D // 2
    with ExitStack() as stack:
        sb, sem = scratch(core, stack)
        w1, w2 = sb("g_w1", [D, 2 * C, P]), sb("g_w2", [P, C, D])
        ln_g, ln_b, b1, b2 = sb("g_ln_g", [D, 1]), sb("g_ln_b", [D, 1]), sb("g_b1", [P, 2 * C]), sb("g_b2", [P, D])
        shifted = sb("g_shifted", [P, TILES, D])
        by_seq = [a.rearrange("p (s t) d -> p s t d", t=TPS) for a in (x[:], shifted[:])]
        shift_zeroed, shift_landed = sem("g_shift_zeroed"), sem("g_shift_landed")
        moves = [(shifted[:, :, 0:HALF], x[:, :, 0:HALF]),
                 (shifted[1:P, :, HALF:D], x[0:P - 1, :, HALF:D]),
                 (by_seq[1][0:1, :, 1, HALF:D], by_seq[0][P - 1:P, :, 0, HALF:D])]
        load_layer(core, "g", [(w1[:].rearrange("p a n -> p (a n)"), flat2(dram["g_w1"][tile(layer)])),
                               (w2[:].rearrange("p a n -> p (a n)"), flat2(dram["g_w2"][tile(layer)])),
                               (ln_g[:], flat2(dram["g_ln_g"][tile(layer)])), (ln_b[:], flat2(dram["g_ln_b"][tile(layer)])),
                               (b1[:], flat2(dram["g_b1"][tile(layer)])), (b2[:], flat2(dram["g_b2"][tile(layer)]))] + moves, layer)
        made, summed = sem("g_made"), sem("g_summed")
        bias = sb("g_bias", [P, 2 * C])
        with nc.Block() as block:
            @block.tensor
            def _(pe):
                for n in range(2 * C):
                    mm = pe.matmul(bank[0][:, n:n + 1], w1[:, n, :], ln_b[:], start=True, stop=True)
                mm.then_inc(summed, 1)

            @block.vector
            def _(dve):
                nc.vector.memset(by_seq[1][0:1, :, 0, HALF:D], 0.0)
                dve.wait_ge(summed, layer + 1)
                nc.vector.tensor_tensor(bias[:], bank[0][:, 0:2 * C], b1[:], ALU.add)
                nc.vector.tensor_scalar(w1[:], w1[:], ln_g[:, 0:1], None, ALU.mult)

        stats_block(core, "gs", shifted, LN_EPS, layer=layer)

        stage, xT = sb("g_stage", [P, TPS, D]), sb("g_xT", [D, LEN])
        gate, hid = sb("g_gate", [P, C, LEN]), sb("g_hid", [P, C, LEN])
        staged, turned, xT_ready, made, bent, gated, out_made, added = (
            sem("g_" + n) for n in ("staged", "turned", "xT_ready", "hid_made", "bent", "gated", "out_made", "added"))
        BS = layer * SEQS
        with nc.Block() as block:
            @block.vector
            def _(dve):
                with dve.Fori(0, SEQS) as b:
                    for t in range(TPS):
                        i = TPS * b + t
                        nc.vector.tensor_scalar(stage[:, t, :], flat(shifted[:, tile(i), :]), core.mean[:, tile(i)],
                                                core.rstd[:, tile(i)], ALU.subtract, ALU.mult).then_inc(staged, 1)
                    xs = x[:, tile(TPS * b, TPS), :]
                    nc.vector.tensor_tensor(xs, xs, b2[:, None, :].to_broadcast([P, TPS, D]), ALU.add).then_inc(added, 1)
                    for c in range(C):
                        dve.wait_ge(bent, C * (BS + b) + c + 1)
                        nc.vector.scalar_tensor_tensor(hid[:, c, :], bank[1 + c][:, 0:LEN], bias[:, c:c + 1], gate[:, c, :],
                                                       ALU.add, ALU.mult).then_inc(gated, 1)
                    dve.wait_ge(out_made, BS + b + 1)
                    dve.wait_ge(added, BS + b + 1)
                    nc.vector.tensor_tensor(xs, xs, bank[4][:, 0:LEN].rearrange("p (t d) -> p t d", t=TPS), ALU.add)

            @block.tensor
            def _(pe):
                with pe.Fori(0, SEQS) as b:
                    pe.wait_ge(staged, TPS * (BS + b) + TPS)
                    for t in range(TPS):
                        mm = pe.transpose(bank[0][:, t * P:(t + 1) * P], stage[:, t, :], core.ident[:])
                    mm.then_inc(turned, 1)
                    pe.wait_ge(xT_ready, BS + b + 1)
                    for c in range(C):
                        pe.matmul(bank[1 + c][:, 0:LEN], w1[:, c, :], xT[:], start=True, stop=True)
                        pe.matmul(bank[1 + c][:, LEN:2 * LEN], w1[:, C + c, :], xT[:], start=True, stop=True).then_inc(made, 1)
                    pe.wait_ge(gated, C * (BS + b) + C)
                    for t in range(TPS):
                        for c in range(C):
                            mm = pe.matmul(bank[4][:, t * D:(t + 1) * D], hid[:, c, t * P:(t + 1) * P], w2[:, c, :],
                                           start=c == 0, stop=c == C - 1)
                    mm.then_inc(out_made, 1)

            @block.scalar
            def _(act):
                with act.Fori(0, SEQS) as b:
                    act.wait_ge(turned, BS + b + 1)
                    nc.scalar.copy(xT[:], bank[0][:, 0:LEN]).then_inc(xT_ready, 1)
                    for c in range(C):
                        act.wait_ge(made, C * (BS + b) + c + 1)
                        nc.scalar.activation(gate[:, c, :], bank[1 + c][:, LEN:2 * LEN], ACT.Gelu, bias=bias[:, C + c:C + c + 1])\
                            .then_inc(bent, 1)


def flat2(ap):
    return ap.rearrange("a p n -> (a p) n")


def l3_attention(core):
    nc, x, bank, dram = core.nc, core.x, core.bank, core.dram
    with ExitStack() as stack:
        sb, sem = scratch(core, stack)
        w, bqk, bv = sb("a3_w", [D, 3 * D]), sb("a3_bqk", [D, 2]), sb("a3_bv", [P, D])
        decay = sb("a3_decay", [P, 3, P])
        load_block(core, "a3", [(w[:], dram["L3_wqkv"]), (bqk[:], dram["L3_bqk"]), (bv[:], dram["L3_bv"]),
                                (decay[:], dram["L3_decay"])])
        stats_block(core, "a3s", x, LN_EPS)
        stage, xT = sb("a3_stage", [P, TPS, D]), sb("a3_xT", [D, LEN])
        qk, v, score = sb("a3_qk", [D, 2, LEN]), sb("a3_v", [P, TPS, D]), sb("a3_score", [P, 3, P])
        staged, turned, xT_ready, made, qk_ready, v_ready, scored, decayed, out_made, added = (
            sem("a3_" + n) for n in ("staged", "turned", "xT_ready", "made", "qk_ready", "v_ready", "scored", "decayed",
                                     "out_made", "added"))
        with nc.Block() as block:
            @block.vector
            def _(dve):
                with dve.Fori(0, SEQS) as b:
                    put_normalized(core, dve, b, stage, staged)
                    dve.wait_ge(made, b + 1)
                    nc.vector.tensor_tensor(v[:], bank[2][:, 0:LEN].rearrange("p (t d) -> p t d", t=TPS),
                                            bv[:, None, :].to_broadcast([P, TPS, D]), ALU.add).then_inc(v_ready, 1)
                    dve.wait_ge(scored, b + 1)
                    nc.vector.tensor_tensor(score[:], bank[3][:, 0:3 * P].rearrange("p (n q) -> p n q", n=3), decay[:], ALU.mult)\
                        .then_inc(decayed, 1)
                    dve.wait_ge(out_made, b + 1)
                    xs = x[:, tile(TPS * b, TPS), :]
                    nc.vector.tensor_tensor(xs, xs, bank[4][:, 0:LEN].rearrange("p (t d) -> p t d", t=TPS), ALU.add)

            @block.tensor
            def _(pe):
                with pe.Fori(0, SEQS) as b:
                    pe.wait_ge(staged, TPS * b + TPS)
                    for t in range(TPS):
                        mm = pe.transpose(bank[0][:, t * P:(t + 1) * P], stage[:, t, :], core.ident[:])
                    mm.then_inc(turned, 1)
                    pe.wait_ge(xT_ready, b + 1)
                    for n in range(2):
                        pe.matmul(bank[1][:, n * LEN:(n + 1) * LEN], w[:, n * D:(n + 1) * D], xT[:], start=True, stop=True)
                    for t in range(TPS):
                        mm = pe.matmul(bank[2][:, t * D:(t + 1) * D], xT[:, t * P:(t + 1) * P], w[:, 2 * D:3 * D], start=True, stop=True)
                    mm.then_inc(made, 1)
                    pe.wait_ge(qk_ready, b + 1)
                    pe.matmul(bank[3][:, 0:LEN], qk[:, 1, 0:P], qk[:, 0, :], start=True, stop=True)
                    pe.matmul(bank[3][:, LEN:LEN + P], qk[:, 1, P:LEN], qk[:, 0, P:LEN], start=True, stop=True).then_inc(scored, 1)
                    pe.wait_ge(v_ready, b + 1)
                    pe.wait_ge(decayed, b + 1)
                    pe.matmul(bank[4][:, 0:D], score[:, 0, :], v[:, 0, :], start=True, stop=True)
                    pe.matmul(bank[4][:, D:2 * D], score[:, 1, :], v[:, 0, :], start=True, stop=False)
                    pe.matmul(bank[4][:, D:2 * D], score[:, 2, :], v[:, 1, :], start=False, stop=True).then_inc(out_made, 1)

            @block.scalar
            def _(act):
                with act.Fori(0, SEQS) as b:
                    act.wait_ge(turned, b + 1)
                    nc.scalar.copy(xT[:], bank[0][:, 0:LEN]).then_inc(xT_ready, 1)
                    act.wait_ge(made, b + 1)
                    for n in range(2):
                        ins = nc.scalar.activation(qk[:, n, :], bank[1][:, n * LEN:(n + 1) * LEN], ACT.Identity, bias=bqk[:, n:n + 1])
                    ins.then_inc(qk_ready, 1)


def l3_feedforward(core):
    nc, x, bank, dram = core.nc, core.x, core.bank, core.dram
    LAYERS, E, H = 4, 4, 512
    C = H // P
    with ExitStack() as stack:
        sb, sem = scratch(core, stack)
        w1, w2 = sb("m_w1", [D, E, H]), sb("m_w2", [P, E * C, D])
        g, b_ln, b1, b2 = sb("m_g", [D, E]), sb("m_b_ln", [D, E]), sb("m_b1", [P, E * C]), sb("m_b2", [P, E, D])
        rw, rb, earlier = sb("m_rw", [D, E]), sb("m_rb", [P, E]), sb("m_earlier", [P, E, E])
        load_block(core, "m0", [(earlier[:].rearrange("p a b -> p (a b)"), dram["m_earlier"])])
        bias = sb("m_bias", [P, E * C])
        stage, xT = sb("m_stage", [P, TPS, D]), sb("m_xT", [D, LEN])
        logit, top, comb, rank, kept = (sb("m_" + n, s) for n, s in (
            ("logit", [P, TILES, E]), ("top", [P, TILES]), ("comb", [P, TILES, E]), ("rank", [P, TILES, E]), ("kept", [P, TILES])))
        above, equal = sb("m_above", [P, TILES, E, E]), sb("m_equal", [P, TILES, E, E])
        hid = sb("m_hid", [P, 2, C, LEN])
        names = ("summed", "r_staged", "r_turned", "r_xT_ready", "routed", "r_logits", "route", "spread", "staged", "turned",
                 "xT_ready", "hidden", "bent", "projected", "added", "based")
        (summed, r_staged, r_turned, r_xT_ready, routed, r_logits, route, spread, staged, turned, xT_ready, hidden, bent,
         projected, added, based) = (sem("m_" + n) for n in names)
        saved = sb("m_saved", [P, TILES, D])
        enter_stream(core, "ms0", saved)
        with nc.Fori(0, LAYERS) as layer:
            BS = layer * SEQS
            load_layer(core, "m", [(w1[:].rearrange("p e h -> p (e h)"), flat2(dram["m_w1"][tile(layer)])),
                                   (w2[:].rearrange("p n d -> p (n d)"), flat2(dram["m_w2"][tile(layer)])),
                                   (g[:], flat2(dram["m_g"][tile(layer)])), (b_ln[:], flat2(dram["m_b_ln"][tile(layer)])),
                                   (b1[:], flat2(dram["m_b1"][tile(layer)])),
                                   (b2[:].rearrange("p e d -> p (e d)"), flat2(dram["m_b2"][tile(layer)])),
                                   (rw[:], flat2(dram["m_rw"][tile(layer)])), (rb[:], flat2(dram["m_rb"][tile(layer)]))], layer)

            with nc.Block() as block:
                @block.tensor
                def _(pe):
                    for e in range(E):
                        for c in range(C):
                            n = e * C + c
                            mm = pe.matmul(bank[2][:, n:n + 1], w1[:, e, c * P:(c + 1) * P], b_ln[:, e:e + 1], start=True, stop=True)
                    mm.then_inc(summed, 1)
                    with pe.Fori(0, SEQS) as b:
                        pe.wait_ge(r_staged, BS + b + 1)
                        for t in range(TPS):
                            mm = pe.transpose(bank[0][:, t * P:(t + 1) * P], stage[:, t, :], core.ident[:])
                        mm.then_inc(r_turned, 1)
                        pe.wait_ge(r_xT_ready, BS + b + 1)
                        for t in range(TPS):
                            mm = pe.matmul(bank[1][:, t * E:(t + 1) * E], xT[:, t * P:(t + 1) * P], rw[:], start=True, stop=True)
                        mm.then_inc(routed, 1)

                @block.vector
                def _(dve):
                    dve.wait_ge(summed, layer + 1)
                    nc.vector.tensor_tensor(bias[:], bank[2][:, 0:E * C], b1[:], ALU.add)
                    for e in range(E):
                        nc.vector.tensor_scalar(w1[:, e, :], w1[:, e, :], g[:, e:e + 1], None, ALU.mult)
                    with dve.Fori(0, SEQS) as b:
                        nc.vector.tensor_copy(stage[:], x[:, tile(TPS * b, TPS), :]).then_inc(r_staged, 1)
                        dve.wait_ge(routed, BS + b + 1)
                        nc.vector.tensor_tensor(logit[:, tile(TPS * b, TPS), :],
                                                bank[1][:, 0:TPS * E].rearrange("p (t e) -> p t e", t=TPS),
                                                rb[:, None, :].to_broadcast([P, TPS, E]), ALU.add).then_inc(r_logits, 1)

                @block.scalar
                def _(act):
                    with act.Fori(0, SEQS) as b:
                        act.wait_ge(r_turned, BS + b + 1)
                        nc.scalar.copy(xT[:], bank[0][:, 0:LEN]).then_inc(r_xT_ready, 1)

            STEPS = 9
            with nc.Block() as block:
                @block.vector
                def _(dve):
                    then = Chain(dve, route, layer * STEPS)
                    then(nc.vector.tensor_reduce(top[:], logit[:], AX.X, ALU.max))
                    then(nc.vector.tensor_tensor(logit[:], logit[:], top[:, :, None].to_broadcast([P, TILES, E]), ALU.subtract))
                    dve.wait_ge(spread, layer + 1)
                    other = logit[:, :, None, :].to_broadcast([P, TILES, E, E])
                    own = logit[:, :, :, None].to_broadcast([P, TILES, E, E])
                    nc.vector.tensor_tensor(above[:], other, own, ALU.is_gt)
                    then(nc.vector.tensor_tensor(equal[:], other, own, ALU.is_equal))
                    then(nc.vector.tensor_tensor(equal[:], equal[:], earlier[:, None, :, :].to_broadcast([P, TILES, E, E]), ALU.mult))
                    then(nc.vector.tensor_tensor(above[:], above[:], equal[:], ALU.add))
                    then(nc.vector.tensor_reduce(rank[:], above[:], AX.X, ALU.add))
                    then(nc.vector.scalar_tensor_tensor(comb[:], rank[:], 1.5, logit[:], ALU.is_lt, ALU.mult))
                    then(nc.vector.tensor_reduce(kept[:], comb[:], AX.X, ALU.add))
                    then(nc.vector.reciprocal(top[:], kept[:]))
                    nc.vector.tensor_tensor(comb[:], comb[:], top[:, :, None].to_broadcast([P, TILES, E]), ALU.mult)
                    assert then.n == STEPS, then.n

                @block.scalar
                def _(act):
                    act.wait_ge(route, layer * STEPS + 2)
                    nc.scalar.activation(logit[:], logit[:], ACT.Exp).then_inc(spread, 1)

            stats_block(core, "ms", x, LN_EPS, layer=layer)

            with nc.Block() as block:
                @block.tensor
                def _(pe):
                    def up(b, e):
                        if e >= 2:
                            pe.wait_ge(bent, C * (E * (BS + b) + e - 1))
                        for c in range(C):
                            pe.matmul(bank[1 + 2 * (e % 2) + c // 2][:, c % 2 * LEN:(c % 2 + 1) * LEN],
                                      w1[:, e, c * P:(c + 1) * P], xT[:], start=True, stop=True).then_inc(hidden, 1)

                    def down(b, e):
                        pe.wait_ge(bent, C * (E * (BS + b) + e + 1))
                        if e >= 2:
                            pe.wait_ge(added, TPS * (E * (BS + b) + e - 1))
                        for t in range(TPS):
                            for c in range(C):
                                mm = pe.matmul(bank[5 + e % 2][:, t * D:(t + 1) * D], hid[:, e % 2, c, t * P:(t + 1) * P],
                                               w2[:, e * C + c, :], start=c == 0, stop=c == C - 1)
                        mm.then_inc(projected, 1)

                    with pe.Fori(0, SEQS) as b:
                        pe.wait_ge(staged, TPS * (BS + b) + TPS)
                        for t in range(TPS):
                            mm = pe.transpose(bank[0][:, t * P:(t + 1) * P], stage[:, t, :], core.ident[:])
                        mm.then_inc(turned, 1)
                        pe.wait_ge(xT_ready, BS + b + 1)
                        for e in range(E + 1):
                            if e < E:
                                up(b, e)
                            if e >= 1:
                                down(b, e - 1)

                @block.scalar
                def _(act):
                    with act.Fori(0, SEQS) as b:
                        act.wait_ge(turned, BS + b + 1)
                        nc.scalar.copy(xT[:], bank[0][:, 0:LEN]).then_inc(xT_ready, 1)
                        for e in range(E):
                            if e >= 2:
                                act.wait_ge(projected, E * (BS + b) + e - 1)
                            for c in range(C):
                                act.wait_ge(hidden, C * (E * (BS + b) + e) + c // 2 * 2 + 2)
                                nc.scalar.activation(hid[:, e % 2, c, :],
                                                     bank[1 + 2 * (e % 2) + c // 2][:, c % 2 * LEN:(c % 2 + 1) * LEN],
                                                     ACT.Gelu, bias=bias[:, e * C + c:e * C + c + 1]).then_inc(bent, 1)

                @block.vector
                def _(dve):
                    with dve.Fori(0, SEQS) as b:
                        put_normalized(core, dve, b, stage, staged)
                        for e in range(E):
                            for t in range(TPS):
                                i = TPS * b + t
                                xs = flat(x[:, tile(i), :])
                                weight = comb[:, tile(i), e:e + 1].rearrange("p a c -> p (a c)")
                                n = E * (BS + b) + e
                                if e >= 1:
                                    dve.wait_ge(added, TPS * n - 1 + t)
                                else:
                                    dve.wait_ge(staged, TPS * (BS + b) + TPS)
                                nc.vector.scalar_tensor_tensor(xs, b2[:, e, :], weight, xs, ALU.mult, ALU.add).then_inc(based, 1)
                            dve.wait_ge(projected, E * (BS + b) + e + 1)
                            for t in range(TPS):
                                i = TPS * b + t
                                xs = flat(x[:, tile(i), :])
                                weight = comb[:, tile(i), e:e + 1].rearrange("p a c -> p (a c)")
                                dve.wait_ge(based, TPS * (E * (BS + b) + e) + t + 1)
                                nc.vector.scalar_tensor_tensor(xs, bank[5 + e % 2][:, t * D:(t + 1) * D], weight, xs,
                                                               ALU.mult, ALU.add).then_inc(added, 1)
        leave_stream(core, saved)


def build(nc, dram, out, sublayers):
    with ExitStack() as ctx:
        core = Core(nc, dram, ctx)
        landed, stored = (ctx.enter_context(nc.semaphore(name)) for name in ("x_landed", "x_stored"))
        token_major = "s (t p) d -> p (s t) d"
        with nc.Block() as block:
            @block.sync
            def _(sp):
                sp.dma_start(core.x[:], dram["x"].rearrange(token_major, p=P)).then_inc(landed, 16)
                sp.dma_start(core.ident[:], dram["ident"]).then_inc(landed, 16)
                sp.wait_ge(landed, 32)

            @block.vector
            def _(dve):
                dve.wait_ge(landed, 32)
                nc.vector.tensor_copy(core.ident_bf[:], core.ident[:])
        for sublayer in sublayers:
            core.run(sublayer)
        with nc.Block() as block:
            @block.sync
            def _(sp):
                sp.dma_start(out.rearrange(token_major, p=P), core.x[:]).then_inc(stored, 16)
                sp.wait_ge(stored, 16)


def kernel(**inputs):
    import numpy as np
    import concourse.bacc as bacc
    from concourse.bass_utils import run_bass_kernel_spmd

    def rows(v):
        v = np.asarray(v).reshape(-1)
        return np.ascontiguousarray(np.broadcast_to(v[None, :], (P, v.size)))

    inputs = {k: np.asarray(v) for k, v in inputs.items()}
    arrays = {}
    arrays["x"] = inputs["L0_attn_embeddings"]
    arrays["ident"] = np.eye(P, dtype=np.float32)
    arrays["L0_wqkv"] = np.concatenate([inputs["L0_attn_Wq"], inputs["L0_attn_Wk"], inputs["L0_attn_Wv"]], 0).T
    arrays["L0_bqkv"] = rows(np.concatenate([inputs["L0_attn_bq"], inputs["L0_attn_bk"], inputs["L0_attn_bv"]]))
    arrays["L0_fc"] = inputs["L0_ffn_w_fc"]
    arrays["L0_proj"] = inputs["L0_ffn_w_proj"]
    arrays["L0_uT"] = inputs["L0_ffn_u"].T
    arrays["L0_v"] = inputs["L0_ffn_v"]
    arrays["L0_fbT"] = inputs["L0_ffn_fast_b"].T
    arrays["L0_gate"] = rows(inputs["L0_ffn_gate"])

    def heads_apart(w):
        w = w.reshape(-1, 4, 4, 8)
        out = np.zeros((w.shape[0], 4, 4, 32), np.float32)
        out[..., 0:8] = w
        return out.reshape(-1, 4, 128)

    arrays["L1_wq"] = inputs["L1_attn_Wq"]
    arrays["L1_wkv"] = np.concatenate([inputs["L1_attn_Wk"], inputs["L1_attn_Wv"]], 1)
    arrays["L1_wo"] = inputs["L1_attn_Wo"]
    arrays["L1_blocks"] = np.kron(np.eye(16), np.ones((8, 8))).astype(np.float32)
    arrays["L1_bq"] = inputs["L1_attn_bq"].reshape(D, 1)
    arrays["L1_bkv"] = rows(np.concatenate([inputs["L1_attn_bk"], inputs["L1_attn_bv"]]))
    arrays["L1_bo"] = rows(inputs["L1_attn_bo"])
    arrays["L1_gamma"] = rows(inputs["L1_attn_gamma"])
    arrays["L1_beta"] = rows(inputs["L1_attn_beta"])
    arrays["L1_fc"] = inputs["L1_ffn_W_fc"]
    arrays["L1_proj"] = inputs["L1_ffn_W_proj"]
    arrays["L1_ln_w"] = inputs["L1_ffn_ln_w"].reshape(4, P).T
    arrays["L1_ln_b"] = inputs["L1_ffn_ln_b"].reshape(4, P).T
    wqkv, bqkv = inputs["L2_attn_Wqkv"], inputs["L2_attn_bqkv"]
    arrays["L2_wq"] = heads_apart(wqkv[:, 0:D])
    arrays["L2_wk"] = heads_apart(wqkv[:, D:2 * D])
    arrays["L2_wv"] = wqkv[:, 2 * D:3 * D]
    arrays["L2_wo"] = inputs["L2_attn_Wout"]
    arrays["L2_bo"] = rows(inputs["L2_attn_bout"])
    arrays["L2_bv"] = rows(bqkv[2 * D:3 * D])
    arrays["L2_bq"] = heads_apart(bqkv[None, 0:D])[0].T
    arrays["L2_bk"] = heads_apart(bqkv[None, D:2 * D])[0].T
    pos = np.arange(LEN)
    arrays["L2_apart"] = np.abs(pos[:, None] - pos[None, :]).astype(np.float32).reshape(TPS, P, LEN).transpose(1, 0, 2)
    arrays["L2_slopes"] = rows(np.array([value for _, value in SLOPE_PARTS], np.float32))

    half = np.arange(0, HD2, 2, dtype=np.float32)
    freqs = pos.astype(np.float32)[:, None] * (1.0 / np.float32(10000.0) ** (half / np.float32(HD2)))[None, :]
    spread = (half + np.float32(0.4 * HD2)) / np.float32(1.4 * HD2)
    power = (pos.astype(np.float32) - LEN // 2) / np.float32(WINDOW // 2)
    scale = spread[None, :] ** power[:, None]
    freqs, scale = (np.concatenate([a, a], 1).astype(np.float32) for a in (freqs, scale))
    sign = np.where(np.arange(HD2) < HD2 // 2, -1.0, 1.0).astype(np.float32)
    qk_factor = 8.0
    one = np.array([[np.cos(freqs) * scale * qk_factor, np.cos(freqs) / scale],
                    [np.sin(freqs) * scale * sign * qk_factor, np.sin(freqs) / scale * sign]], np.float32)
    arrays["r_tables"] = np.concatenate([one, one], 3).transpose(3, 0, 1, 2)
    key = np.arange(WINDOW_KEYS)[None, :] - WINDOW
    query = np.arange(P)[:, None]
    seen = (key <= query) & (query <= key + WINDOW)
    arrays["r_masks"] = np.stack([np.where(seen & (key >= 0), 0.0, -1e30), np.where(seen, 0.0, -1e30)], 1).astype(np.float32)
    arrays["r_head_ones"] = np.kron(np.eye(2), np.ones((HD2, 1))).astype(np.float32)
    swap = (np.arange(HD2) + HD2 // 2) % HD2
    w = inputs["L2_ffn_Wqkv"].reshape(-1, D, 3, HEADS2, HD2)
    arrays["r_w"] = np.stack([w[:, :, 0], w[:, :, 0][..., swap], w[:, :, 1], w[:, :, 1][..., swap], w[:, :, 2]], 2)\
        .reshape(-1, D, 5 * HEADS2 * HD2)
    arrays["r_wo"] = inputs["L2_ffn_Wo"].reshape(-1, PAIRS2, P, D).transpose(0, 2, 1, 3).reshape(-1, P, PAIRS2 * D)
    qs, ks = inputs["L2_ffn_q_scale"], inputs["L2_ffn_k_scale"]
    scales = np.stack([qs, ks, qs[:, swap], ks[:, swap]], 2)
    arrays["r_qk_scale"] = np.concatenate([scales, scales], 1)
    w1, b1, w2 = inputs["L2_ffn_W1"], inputs["L2_ffn_b1"], inputs["L2_ffn_W2"]
    depth, width = w1.shape[0], w2.shape[1]
    filled = 3 * P
    w1p, b1p, w2p = (np.zeros(s, np.float32) for s in ((depth, D, 2, filled), (depth, 2, filled), (depth, filled, D)))
    w1p[..., 0:width] = w1.reshape(depth, D, 2, width)
    b1p[..., 0:width] = b1.reshape(depth, 2, width)
    w2p[:, 0:width] = w2
    arrays["g_w1"] = w1p.reshape(depth, D, 2 * filled)
    arrays["g_b1"] = b1p.reshape(depth, 6, P).transpose(0, 2, 1)
    arrays["g_w2"] = w2p.reshape(depth, 3, P, D).transpose(0, 2, 1, 3).reshape(depth, P, 3 * D)
    arrays["g_b2"] = np.broadcast_to(inputs["L2_ffn_b2"][:, None, :], (depth, P, D))
    arrays["g_ln_g"] = inputs["L2_ffn_ln_g"][:, :, None]
    arrays["g_ln_b"] = inputs["L2_ffn_ln_b"][:, :, None]
    arrays["L3_wqkv"] = inputs["L3_attn_W_qkv"].T
    arrays["L3_bqk"] = inputs["L3_attn_b_qkv"][0:2 * D].reshape(2, D).T
    arrays["L3_bv"] = rows(inputs["L3_attn_b_qkv"][2 * D:])
    gap = (pos[None, :] - pos[:, None]).astype(np.float32)
    decay = (np.where(gap >= 0, np.float32(0.99) ** gap, 0.0) / np.sqrt(np.float32(D))).astype(np.float32)
    arrays["L3_decay"] = np.stack([decay[0:P, 0:P], decay[0:P, P:LEN], decay[P:LEN, P:LEN]], 1)
    layers = inputs["L3_ffn_w1"].shape[0]
    arrays["m_w1"] = inputs["L3_ffn_w1"].transpose(0, 2, 1, 3).reshape(layers, D, 4 * 512)
    arrays["m_w2"] = inputs["L3_ffn_w2"].reshape(layers, 16, P, D).transpose(0, 2, 1, 3).reshape(layers, P, 16 * D)
    arrays["m_g"] = inputs["L3_ffn_ln_g"].transpose(0, 2, 1)
    arrays["m_b_ln"] = inputs["L3_ffn_ln_b"].transpose(0, 2, 1)
    arrays["m_b1"] = inputs["L3_ffn_b1"].reshape(layers, 16, P).transpose(0, 2, 1)
    arrays["m_b2"] = np.broadcast_to(inputs["L3_ffn_b2"].reshape(layers, 1, 4 * D), (layers, P, 4 * D))
    arrays["m_rw"] = inputs["L3_ffn_router_w"]
    arrays["m_rb"] = np.broadcast_to(inputs["L3_ffn_router_b"][:, None, :], (layers, P, 4))
    arrays["m_earlier"] = rows(np.tril(np.ones((4, 4), np.float32), -1))
    nc = bacc.Bacc("TRN2", target_bir_lowering=False, num_devices=1)
    arrays = {f"in_{k}": np.ascontiguousarray(v) for k, v in arrays.items()}
    dram = {k[3:]: nc.dram_tensor(k, v.shape, F32, kind="ExternalInput").ap() for k, v in arrays.items()}
    out = nc.dram_tensor("out_x", (SEQS, LEN, D), F32, kind="ExternalOutput").ap()
    build(nc, dram, out, [l0_attention, l0_feedforward, l1_attention, l1_feedforward, l2_attention, l2_feedforward, l3_attention, l3_feedforward])
    result = run_bass_kernel_spmd(nc, [arrays], core_ids=[0])
    return result.results[0]["out_x"]
```

```python
import math
from contextlib import ExitStack

import concourse.bass as bass
from concourse import mybir

F32 = mybir.dt.float32
BF16 = mybir.dt.bfloat16
ALU = mybir.AluOpType
ACT = mybir.ActivationFunctionType
AX = mybir.AxisListType

P = 128
D = 128
SEQS = 16
LEN = 256
TPS = LEN // P
TILES = SEQS * TPS
LN_EPS = 1e-5


def slope_parts(heads=16):
    import numpy as np
    out = []
    for h in range(heads):
        rest = np.float32((2.0 ** (-2.0 ** (-(math.log2(heads) - 3)))) ** h)
        while rest:
            bits = np.array([rest], np.float32).view(np.uint32)
            bits = (bits + np.uint32(0x7FFF) + ((bits >> np.uint32(16)) & np.uint32(1))) & np.uint32(0xFFFF0000)
            part = bits.view(np.float32)[0]
            out.append((h, -float(part)))
            rest = np.float32(rest - part)
    return out


SLOPE_PARTS = slope_parts()


class Core:

    def __init__(self, nc, dram, ctx):
        self.nc = nc
        self.dram = dram
        self.ctx = ctx
        self.x = self.sb("x", [P, TILES, D])
        self.ident = self.sb("ident", [P, P])
        self.ident_bf = self.sb("ident_bf", [P, P], BF16)
        self.mean = self.sb("mean", [P, TILES])
        self.rstd = self.sb("rstd", [P, TILES])
        self.banks = ctx.enter_context(nc.psum_tensor("banks", [P, 8, 512], F32))
        self.passed = ctx.enter_context(nc.semaphore("passed"))
        self.bank = [self.banks[:, i, :] for i in range(8)]

    def sb(self, name, shape, dt=F32):
        return self.ctx.enter_context(self.nc.sbuf_tensor(name, shape, dt))

    def sem(self, name):
        handle = self.sublayer.enter_context(self.nc.semaphore(name))
        self.sems.append(handle)
        return handle

    def run(self, sublayer):
        nc = self.nc
        with ExitStack() as self.sublayer:
            self.sems = []
            sublayer(self)
            with nc.Block() as block:
                @block.gpsimd
                def _(pool):
                    for handle in self.sems:
                        nc.gpsimd.sem_clear(handle)


class Chain:

    def __init__(self, eng, sem, base=0):
        self.eng, self.sem, self.base, self.n = eng, sem, base, 0

    def __call__(self, instruction):
        self.n += 1
        instruction.then_inc(self.sem, 1)
        self.eng.wait_ge(self.sem, self.base + self.n)


def scratch(core, stack):
    def sb(name, shape, dt=F32):
        return stack.enter_context(core.nc.sbuf_tensor(name, shape, dt))
    return sb, core.sem


def load_block(core, name, loads):
    nc = core.nc
    landed = core.sem(f"{name}_landed")
    with nc.Block() as block:
        @block.sync
        def _(sp):
            for dst, src in loads:
                sp.dma_start(dst, src).then_inc(landed, 16)
            sp.wait_ge(landed, 16 * len(loads))


def load_layer(core, name, loads, layer):
    nc = core.nc
    landed = core.sem(f"{name}_landed")
    with nc.Block() as block:
        @block.sync
        def _(sp):
            for dst, src in loads:
                sp.dma_start(dst, src).then_inc(landed, 16)
            sp.wait_ge(landed, layer * (16 * len(loads)) + 16 * len(loads))
            sp.sem_inc(core.passed, 1)


def stats_block(core, name, src, eps, layer=None, width=D):
    nc = core.nc
    U = 4
    with ExitStack() as stack:
        sb, sem = scratch(core, stack)
        raw = sb(f"{name}_raw", [P, TILES, 6])
        eps_col = sb(f"{name}_eps", [P, 1])
        gap = sb(f"{name}_gap", [P, TILES])
        var = sb(f"{name}_var", [P, TILES])
        std = sb(f"{name}_std", [P, TILES])
        gathered, merged, eps_set, rooted = (sem(f"{name}_{n}") for n in ("gathered", "merged", "eps_set", "rooted"))
        n = 0 if layer is None else layer
        MERGES = 5
        with nc.Block() as block:
            @block.vector
            def _(dve):
                nc.vector.memset(eps_col[:], eps).then_inc(eps_set, 1)
                with dve.Fori(0, TILES // U) as i:
                    for k in range(U):
                        nc.vector.bn_stats(flat(raw[:, tile(U * i + k), :]), flat(src[:, tile(U * i + k), :])).then_inc(gathered, 1)
                dve.wait_ge(gathered, n * TILES + TILES)
                then = Chain(dve, merged, n * MERGES)
                nc.vector.tensor_tensor(core.mean[:], raw[:, :, 1], raw[:, :, 4], ALU.add)
                nc.vector.tensor_tensor(var[:], raw[:, :, 2], raw[:, :, 5], ALU.add)
                then(nc.vector.tensor_tensor(gap[:], raw[:, :, 1], raw[:, :, 4], ALU.subtract))
                then(nc.vector.tensor_tensor(gap[:], gap[:], gap[:], ALU.mult))
                then(nc.vector.tensor_scalar(gap[:], gap[:], 0.25, None, ALU.mult))
                then(nc.vector.scalar_tensor_tensor(var[:], var[:], 1.0 / width, gap[:], ALU.mult, ALU.add))
                then(nc.vector.tensor_scalar(core.mean[:], core.mean[:], 0.5, None, ALU.mult))
                dve.wait_ge(rooted, n + 1)
                nc.vector.reciprocal(core.rstd[:], std[:])

            @block.scalar
            def _(act):
                act.wait_ge(eps_set, n + 1)
                act.wait_ge(merged, n * MERGES + MERGES)
                nc.scalar.activation(std[:], var[:], ACT.Sqrt, bias=eps_col[:]).then_inc(rooted, 1)


def tile(t, k=1):
    return bass.ds(t, k)


def flat(ap):
    return ap.rearrange("p a d -> p (a d)")


def l0_attention(core):
    nc, x, bank, dram = core.nc, core.x, core.bank, core.dram
    HD = 8
    SCALE = float(D) ** -0.5
    PAIRS = [(0, 0), (0, 1), (1, 0), (1, 1), (0, 2), (2, 0), (1, 2), (2, 1)]
    KQ = HD * len(PAIRS)
    with ExitStack() as stack:
        sb, sem = scratch(core, stack)
        w = sb("a0_w", [D, 3 * HD])
        bias = sb("a0_bias", [P, 3 * HD])
        load_block(core, "a0", [(w[:], dram["L0_wqkv"]), (bias[:], dram["L0_bqkv"])])
        stats_block(core, "a0s", x, LN_EPS)

        stage = sb("a0_stage", [P, TPS, D])
        xT = sb("a0_xT", [D, LEN])
        qkv = sb("a0_qkv", [P, TILES, 3 * HD])
        v1 = sb("a0_v1", [P, TILES, HD + 1])
        staged, turned, xT_ready, projected, biased = (sem("a0_" + n) for n in
                                                       ("staged", "turned", "xT_ready", "projected", "biased"))
        with nc.Block() as block:
            @block.vector
            def _(dve):
                with dve.Fori(0, SEQS) as b:
                    for t in range(TPS):
                        i = 2 * b + t
                        nc.vector.tensor_scalar(stage[:, t, :], flat(x[:, tile(i), :]), core.mean[:, tile(i)],
                                                core.rstd[:, tile(i)], ALU.subtract, ALU.mult).then_inc(staged, 1)
                    dve.wait_ge(projected, b + 1)
                    nc.vector.tensor_tensor(qkv[:, tile(2 * b, 2), :],
                                            bank[1][:, 0:2 * 3 * HD].rearrange("p (t c) -> p t c", t=TPS),
                                            bias[:, None, :].to_broadcast([P, TPS, 3 * HD]), ALU.add).then_inc(biased, 1)

            @block.tensor
            def _(pe):
                with pe.Fori(0, SEQS) as b:
                    pe.wait_ge(staged, 2 * b + 2)
                    for t in range(TPS):
                        mm = pe.transpose(bank[0][:, t * P:(t + 1) * P], stage[:, t, :], core.ident[:])
                    mm.then_inc(turned, 1)
                    pe.wait_ge(xT_ready, b + 1)
                    for t in range(TPS):
                        mm = pe.matmul(bank[1][:, t * 3 * HD:(t + 1) * 3 * HD], xT[:, t * P:(t + 1) * P], w[:],
                                       start=True, stop=True)
                    mm.then_inc(projected, 1)

            @block.scalar
            def _(act):
                with act.Fori(0, SEQS) as b:
                    act.wait_ge(turned, b + 1)
                    nc.scalar.copy(xT[:], bank[0][:, 0:LEN]).then_inc(xT_ready, 1)

        parts = sb("a0_parts", [P, 3, TILES, 2 * HD], BF16)
        rest = sb("a0_rest", [P, 2, TILES, 2 * HD])
        q_rows = sb("a0_q_rows", [P, TILES, P], BF16)
        k_rows = sb("a0_k_rows", [P, TILES, P], BF16)
        split, laid = sem("a0_split"), sem("a0_laid")
        with nc.Block() as block:
            @block.vector
            def _(dve):
                then = Chain(dve, split)
                qk = qkv[:, :, 0:2 * HD]
                then(nc.vector.tensor_copy(parts[:, 0], qk))
                then(nc.vector.tensor_tensor(rest[:, 0], qk, parts[:, 0], ALU.subtract))
                then(nc.vector.tensor_copy(parts[:, 1], rest[:, 0]))
                then(nc.vector.tensor_tensor(rest[:, 1], rest[:, 0], parts[:, 1], ALU.subtract))
                then(nc.vector.tensor_copy(parts[:, 2], rest[:, 1]))
                nc.vector.memset(v1[:, :, HD:HD + 1], 1.0)
                nc.vector.tensor_copy(v1[:, :, 0:HD], qkv[:, :, 2 * HD:3 * HD])
                nc.vector.memset(q_rows[:, :, KQ:P], 0.0)
                nc.vector.memset(k_rows[:, :, KQ:P], 1.0)
                for n, (a, b) in enumerate(PAIRS):
                    nc.vector.tensor_copy(q_rows[:, :, n * HD:(n + 1) * HD], parts[:, a, :, 0:HD])
                    nc.vector.tensor_copy(k_rows[:, :, n * HD:(n + 1) * HD], parts[:, b, :, HD:2 * HD])

        qT = sb("a0_qT", [P, TILES, P], BF16)
        kT = sb("a0_kT", [P, TILES, P], BF16)

        def turn_rows(name, jobs):
            G = 8
            turned_g, copied = sem(f"a0_turned_{name}"), sem(f"a0_copied_{name}")
            steps = [(dst, src, g) for dst, src in jobs for g in range(TILES // G)]
            with nc.Block() as block:
                @block.tensor
                def _(pe):
                    for n, (dst, src, g) in enumerate(steps):
                        if n >= 2:
                            pe.wait_ge(copied, n - 1)
                        out = bank[n % 2].bitcast(BF16)
                        for k in range(G):
                            mm = pe.transpose(out[:, k * P:(k + 1) * P], src[:, g * G + k, :], core.ident_bf[:])
                        mm.then_inc(turned_g, 1)

                @block.vector
                def _(dve):
                    for n, (dst, src, g) in enumerate(steps):
                        dve.wait_ge(turned_g, n + 1)
                        nc.vector.tensor_copy(flat(dst[:, g * G:(g + 1) * G, :]), bank[n % 2].bitcast(BF16)).then_inc(copied, 1)

        turn_rows("qk", [(qT, q_rows), (kT, k_rows)])

        top = sb("a0_top", [P, TILES, 2])
        scored, halved = sem("a0_scored"), sem("a0_halved")
        HALF = TILES * P // 2
        with nc.Block() as block:
            @block.tensor
            def _(pe):
                with pe.Fori(0, TILES) as t:
                    for h in range(2):
                        pe.wait_ge(halved, 2 * t + h + 1)
                        for c in range(4):
                            mm = pe.matmul(bank[4 * h + c], flat(qT[:, tile(t), :]),
                                           kT[:, 16 * h + 4 * c:16 * h + 4 * c + 4, :].rearrange("p a d -> p (a d)"),
                                           start=True, stop=True)
                        mm.then_inc(scored, 1)

            @block.vector
            def _(dve):
                dve.sem_inc(halved, 2)
                with dve.Fori(0, TILES) as t:
                    for h in range(2):
                        dve.wait_ge(scored, 2 * t + h + 1)
                        nc.vector.tensor_reduce(top[:, tile(t), h:h + 1].rearrange("p a c -> p (a c)"),
                                                core.banks[:, 4 * h:4 * h + 4, :], AX.XY, ALU.max).then_inc(halved, 1)

        low = sb("a0_low", [P, 3, TILES])
        cut = sem("a0_cut")
        with nc.Block() as block:
            @block.vector
            def _(dve):
                then = Chain(dve, cut)
                m = [q_rows[:, :, KQ + c:KQ + c + 1].rearrange("p t a -> p (t a)") for c in range(3)]
                then(nc.vector.tensor_tensor(low[:, 0], top[:, :, 0], top[:, :, 1], ALU.max))
                then(nc.vector.tensor_scalar(low[:, 0], low[:, 0], -1.0, None, ALU.mult))
                then(nc.vector.tensor_copy(m[0], low[:, 0]))
                then(nc.vector.tensor_tensor(low[:, 1], low[:, 0], m[0], ALU.subtract))
                then(nc.vector.tensor_copy(m[1], low[:, 1]))
                then(nc.vector.tensor_tensor(low[:, 2], low[:, 1], m[1], ALU.subtract))
                nc.vector.tensor_copy(m[2], low[:, 2])

        turn_rows("m", [(qT, q_rows)])

        QC = 4
        CHUNKS = TILES // QC
        expd = sb("a0_expd", [P, 2, 2, QC * P])
        inv = sb("a0_inv", [P, QC])
        y = sb("a0_y", [P, QC, HD])
        paired, expd_ready, expd_used, sums_read, inverted = (
            sem("a0_" + n) for n in ("paired", "expd_ready", "expd_used", "sums_read", "inverted"))
        KPAIRS = TILES // 2
        acc = bank[4][:, 0:QC * (HD + 1)].rearrange("p (s c) -> p s c", s=QC)
        with nc.Block() as block:
            @block.tensor
            def _(pe):
                def scores(c, kt, n, par):
                    pe.wait_ge(expd_ready, n + 1)
                    for h in range(2):
                        mm = pe.matmul(bank[2 * par + h], flat(kT[:, tile(kt + h), :]),
                                       qT[:, tile(c * QC, QC), :].rearrange("p a d -> p (a d)"), start=True, stop=True)
                    mm.then_inc(paired, 1)

                def sums(kt, n, par, first, last):
                    pe.wait_ge(expd_ready, n + 3)
                    for h in range(2):
                        for s in range(QC):
                            mm = pe.matmul(acc[:, s, :], expd[:, par, h, s * P:(s + 1) * P], flat(v1[:, tile(kt + h), :]),
                                           start=first and h == 0 and s == 0, stop=last and h == 1, skip_group_check=True)
                    mm.then_inc(expd_used, 1)

                with pe.Fori(0, CHUNKS) as c:
                    scores(c, 0, c * KPAIRS, 0)
                    scores(c, 2, c * KPAIRS + 1, 1)
                    pe.wait_ge(sums_read, c + 1)
                    sums(0, c * KPAIRS, 0, True, False)
                    scores(c, 4, c * KPAIRS + 2, 0)
                    sums(2, c * KPAIRS + 1, 1, False, False)
                    scores(c, 6, c * KPAIRS + 3, 1)
                    with pe.Fori(1, KPAIRS // 2 - 1) as k:
                        for par in range(2):
                            sums(4 * k + 2 * par, c * KPAIRS + 2 * k + par, par, False, False)
                            scores(c, 4 * k + 2 * par + 4, c * KPAIRS + 2 * k + par + 2, par)
                    for par in range(2):
                        sums(TILES - 4 + 2 * par, c * KPAIRS + KPAIRS - 2 + par, par, False, par == 1)

            @block.scalar
            def _(act):
                act.sem_inc(expd_ready, 2)
                with act.Fori(0, CHUNKS * KPAIRS // 2) as k:
                    for par in range(2):
                        act.wait_ge(paired, 2 * k + par + 1)
                        act.wait_ge(expd_used, 2 * k + par + 1)
                        nc.scalar.activation(expd[:, par], core.banks[:, 2 * par:2 * par + 2, :], ACT.Exp, scale=SCALE)\
                            .then_inc(expd_ready, 1)

            @block.vector
            def _(dve):
                dve.sem_inc(sums_read, 1)
                dve.sem_inc(expd_used, 2)
                with dve.Fori(0, CHUNKS) as c:
                    dve.wait_ge(expd_used, c * KPAIRS + KPAIRS + 2)
                    nc.vector.reciprocal(inv[:], acc[:, :, HD]).then_inc(inverted, 1)
                    dve.wait_ge(inverted, c + 1)
                    nc.vector.tensor_tensor(y[:], acc[:, :, 0:HD], inv[:, :, None].to_broadcast([P, QC, HD]), ALU.mult)\
                        .then_inc(sums_read, 1)
                    dve.wait_ge(sums_read, c + 2)
                    for s in range(QC):
                        xs = flat(x[:, tile(c * QC + s), :]).rearrange("p (r f) -> p r f", f=HD)
                        nc.vector.tensor_tensor(xs, xs, y[:, s, None, :].to_broadcast([P, D // HD, HD]), ALU.add)


def l0_feedforward(core):
    nc, x, bank, dram = core.nc, core.x, core.bank, core.dram
    H = 512
    C = H // P
    R = 16
    with ExitStack() as stack:
        sb, sem = scratch(core, stack)
        fc = sb("f0_fc", [P, C, D])
        proj = sb("f0_proj", [P, H])
        uT = sb("f0_uT", [R, H])
        v = sb("f0_v", [R, D])
        fbT = sb("f0_fbT", [R, R])
        gate = sb("f0_gate", [P, 1])
        load_block(core, "f0", [(fc[:], dram["L0_fc"].rearrange("(c p) d -> p c d", p=P)), (proj[:], dram["L0_proj"]),
                                (uT[:], dram["L0_uT"]), (v[:], dram["L0_v"]), (fbT[:], dram["L0_fbT"]), (gate[:], dram["L0_gate"])])
        stats_block(core, "f0s", x, LN_EPS)

        w1 = sb("f0_w1", [D, H])
        w2 = sb("f0_w2", [P, C, D])
        fbv = sb("f0_fbv", [R, D])
        scale = sb("f0_scale", [P, C + 1])
        edge = sb("f0_edge", [P, 2, C + 1])
        tern = sb("f0_tern", [P, 2, C, D])
        below = sb("f0_below", [P, 2, C, D])
        made, small, turned = sem("f0_made"), sem("f0_small"), sem("f0_turned")
        with nc.Block() as block:
            @block.vector
            def _(dve):
                then = Chain(dve, made)
                then(nc.vector.tensor_reduce(scale[:, 0:C], fc[:], AX.X, ALU.add, apply_absolute_value=True))
                then(nc.vector.tensor_reduce(scale[:, C:C + 1], proj[:], AX.X, ALU.add, apply_absolute_value=True))
                then(nc.vector.tensor_scalar(scale[:, 0:C], scale[:, 0:C], 1.0 / D, 1e-5, ALU.mult, ALU.max))
                then(nc.vector.tensor_scalar(scale[:, C:C + 1], scale[:, C:C + 1], 1.0 / H, 1e-5, ALU.mult, ALU.max))
                then(nc.vector.tensor_scalar(edge[:, 0], scale[:], 0.5, None, ALU.mult))
                then(nc.vector.tensor_scalar(edge[:, 1], scale[:], -0.5, None, ALU.mult))
                for c in range(C):
                    for m, src, e in ((0, fc[:, c, :], c), (1, proj[:, c * P:(c + 1) * P], C)):
                        then(nc.vector.tensor_scalar(below[:, m, c], src, edge[:, 1, e:e + 1], None, ALU.is_lt))
                        then(nc.vector.scalar_tensor_tensor(tern[:, m, c], src, edge[:, 0, e:e + 1], below[:, m, c],
                                                            ALU.is_gt, ALU.subtract))
                        then(nc.vector.tensor_scalar(tern[:, m, c], tern[:, m, c], scale[:, e:e + 1], None, ALU.mult))
                dve.wait_ge(small, 1)
                then(nc.vector.tensor_copy(fbv[:], bank[0][0:R, 0:D]))
                dve.wait_ge(small, 2)
                then(nc.vector.scalar_tensor_tensor(tern[:, 0], bank[1].rearrange("p (c d) -> p c d", c=C), gate[:, 0:1],
                                                    tern[:, 0], ALU.mult, ALU.add))
                dve.wait_ge(turned, 1)
                then(nc.vector.tensor_copy(w1[:], bank[2]))
                then(nc.vector.tensor_copy(w2[:].rearrange("p c d -> p (c d)"), bank[3]))

            @block.tensor
            def _(pe):
                pe.matmul(bank[0][0:R, 0:D], fbT[:], v[:], start=True, stop=True).then_inc(small, 1)
                FBV = 6 + 3 * 2 * C + 1
                pe.wait_ge(made, FBV)
                for c in range(C):
                    mm = pe.matmul(bank[1][:, c * D:(c + 1) * D], uT[:, c * P:(c + 1) * P], fbv[:], start=True, stop=True)
                mm.then_inc(small, 1)
                pe.wait_ge(made, FBV + 1)
                for c in range(C):
                    pe.transpose(bank[2][:, c * P:(c + 1) * P], tern[:, 0, c, :], core.ident[:])
                    mm = pe.transpose(bank[3][:, c * P:(c + 1) * P], tern[:, 1, c, :], core.ident[:])
                mm.then_inc(turned, 1)

        stage = sb("f0_stage", [P, TPS, D])
        xT = sb("f0_xT", [D, LEN])
        relu = sb("f0_relu", [P, C * LEN])
        hid = sb("f0_hid", [P, C, LEN])
        staged, turned_x, xT_ready, hidden, clipped, squared, projected, added = (
            sem("f0_" + n) for n in ("staged", "turned_x", "xT_ready", "hidden", "clipped", "squared", "projected", "added"))
        with nc.Block() as block:
            @block.vector
            def _(dve):
                def put(b):
                    for t in range(TPS):
                        i = 2 * b + t
                        nc.vector.tensor_scalar(stage[:, t, :], flat(x[:, tile(i), :]), core.mean[:, tile(i)],
                                                core.rstd[:, tile(i)], ALU.subtract, ALU.mult).then_inc(staged, 1)
                with dve.Fori(0, SEQS) as b:
                    put(b)
                    dve.wait_ge(clipped, b + 1)
                    nc.vector.tensor_tensor(hid[:].rearrange("p c t -> p (c t)"), relu[:], relu[:], ALU.mult).then_inc(squared, 1)
                    dve.wait_ge(projected, b + 1)
                    nc.vector.tensor_tensor(x[:, tile(2 * b, 2), :], x[:, tile(2 * b, 2), :],
                                            bank[4][:, 0:LEN].rearrange("p (t d) -> p t d", t=TPS), ALU.add)

            @block.tensor
            def _(pe):
                with pe.Fori(0, SEQS) as b:
                    pe.wait_ge(staged, 2 * b + 2)
                    for t in range(TPS):
                        mm = pe.transpose(bank[0][:, t * P:(t + 1) * P], stage[:, t, :], core.ident[:])
                    mm.then_inc(turned_x, 1)
                    pe.wait_ge(xT_ready, b + 1)
                    for c in range(C):
                        mm = pe.matmul(bank[2 + c // 2][:, (c % 2) * LEN:(c % 2 + 1) * LEN], w1[:, c * P:(c + 1) * P], xT[:],
                                       start=True, stop=True)
                    mm.then_inc(hidden, 1)
                    pe.wait_ge(squared, b + 1)
                    for t in range(TPS):
                        for c in range(C):
                            mm = pe.matmul(bank[4][:, t * D:(t + 1) * D], hid[:, c, t * P:(t + 1) * P], w2[:, c, :],
                                           start=c == 0, stop=c == C - 1)
                    mm.then_inc(projected, 1)

            @block.scalar
            def _(act):
                with act.Fori(0, SEQS) as b:
                    act.wait_ge(turned_x, b + 1)
                    nc.scalar.copy(xT[:], bank[0][:, 0:LEN]).then_inc(xT_ready, 1)
                    act.wait_ge(hidden, b + 1)
                    nc.scalar.activation(relu[:].rearrange("p (a f) -> p a f", a=2), core.banks[:, 2:4, :], ACT.Relu).then_inc(clipped, 1)


def put_normalized(core, dve, b, stage, staged):
    nc = core.nc
    for t in range(TPS):
        i = TPS * b + t
        nc.vector.tensor_scalar(stage[:, t, :], flat(core.x[:, tile(i), :]), core.mean[:, tile(i)], core.rstd[:, tile(i)],
                                ALU.subtract, ALU.mult).then_inc(staged, 1)


def enter_stream(core, name, saved):
    nc = core.nc
    stats_block(core, name, core.x, LN_EPS)
    kept = core.sem(f"{name}_kept")
    with nc.Block() as block:
        @block.vector
        def _(dve):
            nc.vector.tensor_copy(saved[:], core.x[:]).then_inc(kept, 1)
            dve.wait_ge(kept, 1)
            for t in range(TILES):
                nc.vector.tensor_scalar(core.x[:, t, :], saved[:, t, :], core.mean[:, t:t + 1], core.rstd[:, t:t + 1],
                                        ALU.subtract, ALU.mult)


def leave_stream(core, saved):
    nc = core.nc
    with nc.Block() as block:
        @block.vector
        def _(dve):
            nc.vector.tensor_tensor(core.x[:], core.x[:], saved[:], ALU.add)


def l1_attention(core):
    nc, x, bank, dram = core.nc, core.x, core.bank, core.dram
    HEADS, HD = 16, 8
    EPS = 1e-6
    with ExitStack() as stack:
        sb, sem = scratch(core, stack)
        wq, wkv, wo, blocks = sb("a1_wq", [D, D]), sb("a1_wkv", [D, 2 * D]), sb("a1_wo", [D, D]), sb("a1_blocks", [D, D])
        bq, bkv, bo = sb("a1_bq", [D, 1]), sb("a1_bkv", [P, 2 * D]), sb("a1_bo", [P, D])
        gamma, beta = sb("a1_gamma", [P, D]), sb("a1_beta", [P, D])
        load_block(core, "a1", [(wq[:], dram["L1_wq"]), (wkv[:], dram["L1_wkv"]), (wo[:], dram["L1_wo"]),
                                (blocks[:], dram["L1_blocks"]), (bq[:], dram["L1_bq"]), (bkv[:], dram["L1_bkv"]),
                                (bo[:], dram["L1_bo"]), (gamma[:], dram["L1_gamma"]), (beta[:], dram["L1_beta"])])
        stats_block(core, "a1s", x, LN_EPS)
        stage = sb("a1_stage", [P, TPS, D])
        xT = sb("a1_xT", [D, LEN])
        q_raw, q_exp, q_lin, q = (sb("a1_" + n, [D, LEN]) for n in ("q_raw", "q_exp", "q_lin", "q"))
        kv = sb("a1_kv", [P, TPS, 2 * D])
        k_exp, k_lin, k_sq = (sb("a1_" + n, [P, TPS, D]) for n in ("k_exp", "k_lin", "k_sq"))
        k_sum, k_norm, k_inv = (sb("a1_" + n, [P, TPS * HEADS]) for n in ("k_sum", "k_norm", "k_inv"))
        vk, m = sb("a1_vk", [D, D]), sb("a1_m", [D, D])
        y = sb("a1_y", [P, TPS, D])
        raw, mv, std, inv = sb("a1_raw", [P, TPS, 6]), sb("a1_mv", [P, TPS, 2]), sb("a1_std", [P, TPS]), sb("a1_inv", [P, TPS])
        eps_col = sb("a1_eps_col", [P, 1])
        (eps_set, staged, turned, xT_ready, q_made, q_biased, kv_made, q_exp_ready, kv_ready, k_exp_ready, k_summed, k_rooted,
         q_ready, k_ready, vk_made, vk_ready, m_made, m_ready, y_made, y_varied, y_rooted, chain) = (
            sem("a1_" + n) for n in (
                "eps_set", "staged", "turned", "xT_ready", "q_made", "q_biased", "kv_made", "q_exp_ready", "kv_ready", "k_exp_ready",
                "k_summed", "k_rooted", "q_ready", "k_ready", "vk_made", "vk_ready", "m_made", "m_ready", "y_made",
                "y_varied", "y_rooted", "chain"))
        CHAIN = 12
        with nc.Block() as block:
            @block.vector
            def _(dve):
                nc.vector.memset(eps_col[:], EPS).then_inc(eps_set, 1)
                with dve.Fori(0, SEQS) as b:
                    then = Chain(dve, chain, b * CHAIN)
                    put_normalized(core, dve, b, stage, staged)
                    dve.wait_ge(q_made, b + 1)
                    nc.vector.tensor_scalar(q_raw[:], bank[1][:, 0:LEN], bq[:, 0:1], None, ALU.add).then_inc(q_biased, 1)
                    dve.wait_ge(q_biased, b + 1)
                    then(nc.vector.tensor_scalar(q_lin[:], q_raw[:], 0.0, None, ALU.max))
                    dve.wait_ge(q_exp_ready, b + 1)
                    nc.vector.scalar_tensor_tensor(q[:], q_exp[:], 1.0, q_lin[:], ALU.min, ALU.add).then_inc(q_ready, 1)
                    dve.wait_ge(kv_made, b + 1)
                    nc.vector.tensor_tensor(kv[:], bank[2].rearrange("p (t c) -> p t c", t=TPS),
                                            bkv[:, None, :].to_broadcast([P, TPS, 2 * D]), ALU.add).then_inc(kv_ready, 1)
                    dve.wait_ge(kv_ready, b + 1)
                    then(nc.vector.tensor_scalar(k_lin[:], kv[:, :, 0:D], 0.0, None, ALU.max))
                    dve.wait_ge(k_exp_ready, b + 1)
                    then(nc.vector.scalar_tensor_tensor(k_lin[:], k_exp[:], 1.0, k_lin[:], ALU.min, ALU.add))
                    then(nc.vector.tensor_tensor(k_sq[:], k_lin[:], k_lin[:], ALU.mult))
                    nc.vector.tensor_reduce(k_sum[:], k_sq[:].rearrange("p t (h f) -> p (t h) f", f=HD), AX.X, ALU.add)\
                        .then_inc(k_summed, 1)
                    dve.wait_ge(k_rooted, b + 1)
                    then(nc.vector.reciprocal(k_inv[:], k_norm[:]))
                    nc.vector.tensor_tensor(k_sq[:].rearrange("p t (h f) -> p (t h) f", f=HD),
                                            k_lin[:].rearrange("p t (h f) -> p (t h) f", f=HD),
                                            k_inv[:, :, None].to_broadcast([P, TPS * HEADS, HD]), ALU.mult).then_inc(k_ready, 1)
                    dve.wait_ge(vk_made, b + 1)
                    nc.vector.tensor_tensor(vk[:], bank[3][:, 0:D], blocks[:], ALU.mult).then_inc(vk_ready, 1)
                    dve.wait_ge(y_made, b + 1)
                    then(nc.vector.tensor_tensor(y[:], bank[5][:, 0:LEN].rearrange("p (t d) -> p t d", t=TPS),
                                                 bo[:, None, :].to_broadcast([P, TPS, D]), ALU.add))
                    then(nc.vector.tensor_tensor(y[:], y[:], stage[:], ALU.add))
                    nc.vector.bn_stats(raw[:, 0, :], y[:, 0, :])
                    then(nc.vector.bn_stats(raw[:, 1, :], y[:, 1, :]))
                    xs = x[:, tile(TPS * b, TPS), :]
                    nc.vector.tensor_tensor(xs, xs, beta[:, None, :].to_broadcast([P, TPS, D]), ALU.add)
                    nc.vector.bn_aggr(mv[:, 0, :], raw[:, 0, :])
                    nc.vector.bn_aggr(mv[:, 1, :], raw[:, 1, :]).then_inc(y_varied, 1)
                    dve.wait_ge(y_rooted, b + 1)
                    then(nc.vector.reciprocal(inv[:], std[:]))
                    for t in range(TPS):
                        ins = nc.vector.tensor_scalar(y[:, t, :], y[:, t, :], mv[:, t, 0:1], inv[:, t:t + 1],
                                                      ALU.subtract, ALU.mult)
                    then(ins)
                    then(nc.vector.tensor_tensor(y[:], y[:], gamma[:, None, :].to_broadcast([P, TPS, D]), ALU.mult))
                    then(nc.vector.tensor_tensor(xs, xs, y[:], ALU.add))
                    assert then.n == CHAIN, then.n

            @block.tensor
            def _(pe):
                with pe.Fori(0, SEQS) as b:
                    pe.wait_ge(staged, TPS * b + TPS)
                    for t in range(TPS):
                        mm = pe.transpose(bank[0][:, t * P:(t + 1) * P], stage[:, t, :], core.ident[:])
                    mm.then_inc(turned, 1)
                    pe.wait_ge(xT_ready, b + 1)
                    pe.matmul(bank[1][:, 0:LEN], wq[:], xT[:], start=True, stop=True).then_inc(q_made, 1)
                    for t in range(TPS):
                        mm = pe.matmul(bank[2][:, t * 2 * D:(t + 1) * 2 * D], xT[:, t * P:(t + 1) * P], wkv[:],
                                       start=True, stop=True)
                    mm.then_inc(kv_made, 1)
                    pe.wait_ge(k_ready, b + 1)
                    for t in range(TPS):
                        mm = pe.matmul(bank[3][:, 0:D], kv[:, t, D:2 * D], k_sq[:, t, :], start=t == 0, stop=t == TPS - 1)
                    mm.then_inc(vk_made, 1)
                    pe.wait_ge(vk_ready, b + 1)
                    pe.matmul(bank[4][:, 0:D], vk[:], wo[:], start=True, stop=True).then_inc(m_made, 1)
                    pe.wait_ge(m_ready, b + 1)
                    pe.wait_ge(q_ready, b + 1)
                    for t in range(TPS):
                        mm = pe.matmul(bank[5][:, t * D:(t + 1) * D], q[:, t * P:(t + 1) * P], m[:], start=True, stop=True)
                    mm.then_inc(y_made, 1)

            @block.scalar
            def _(act):
                act.wait_ge(eps_set, 1)
                with act.Fori(0, SEQS) as b:
                    act.wait_ge(turned, b + 1)
                    nc.scalar.copy(xT[:], bank[0][:, 0:LEN]).then_inc(xT_ready, 1)
                    act.wait_ge(q_biased, b + 1)
                    nc.scalar.activation(q_exp[:], q_raw[:], ACT.Exp).then_inc(q_exp_ready, 1)
                    act.wait_ge(kv_ready, b + 1)
                    nc.scalar.activation(k_exp[:], kv[:, :, 0:D], ACT.Exp).then_inc(k_exp_ready, 1)
                    act.wait_ge(k_summed, b + 1)
                    nc.scalar.activation(k_norm[:], k_sum[:], ACT.Sqrt, bias=eps_col[:]).then_inc(k_rooted, 1)
                    act.wait_ge(m_made, b + 1)
                    nc.scalar.copy(m[:], bank[4][:, 0:D]).then_inc(m_ready, 1)
                    act.wait_ge(y_varied, b + 1)
                    nc.scalar.activation(std[:], mv[:, :, 1], ACT.Sqrt, bias=eps_col[:]).then_inc(y_rooted, 1)


def l1_feedforward(core):
    nc, x, bank, dram = core.nc, core.x, core.bank, core.dram
    H = 512
    C = H // P
    with ExitStack() as stack:
        sb, sem = scratch(core, stack)
        fc, proj = sb("f1_fc", [P, C, D]), sb("f1_proj", [P, H])
        ln_w, ln_b = sb("f1_ln_w", [P, C]), sb("f1_ln_b", [P, C])
        load_block(core, "f1", [(fc[:], dram["L1_fc"].rearrange("(c p) d -> p c d", p=P)), (proj[:], dram["L1_proj"]),
                                (ln_w[:], dram["L1_ln_w"]), (ln_b[:], dram["L1_ln_b"])])
        stats_block(core, "f1s", x, LN_EPS)

        ones = sb("f1_ones", [P, P])
        total, edge = sb("f1_total", [P, 2]), sb("f1_edge", [P, 2, 2])
        tern, below = sb("f1_tern", [P, 2, H]), sb("f1_below", [P, 2, H])
        w1, w2, w2_plain = sb("f1_w1", [D, H]), sb("f1_w2", [P, C, D]), sb("f1_w2_plain", [P, C, D])
        b_rows, shift = sb("f1_b_rows", [P, C, P]), sb("f1_shift", [P, D])
        made, product = sem("f1_made"), sem("f1_product")
        with nc.Block() as block:
            @block.vector
            def _(dve):
                then = Chain(dve, made)
                nc.vector.memset(ones[:], 1.0)
                nc.vector.tensor_reduce(total[:, 0:1], fc[:].rearrange("p c d -> p (c d)"), AX.X, ALU.add, apply_absolute_value=True)
                then(nc.vector.tensor_reduce(total[:, 1:2], proj[:], AX.X, ALU.add, apply_absolute_value=True))
                dve.wait_ge(product, 1)
                then(nc.vector.tensor_scalar(edge[:, 0], bank[0][:, 0:2], 1.0 / (H * D), 1e-6, ALU.mult, ALU.add))
                then(nc.vector.tensor_scalar(edge[:, 1], edge[:, 0], -0.5, None, ALU.mult))
                then(nc.vector.tensor_scalar(edge[:, 0], edge[:, 0], 0.5, None, ALU.mult))
                for n, src in ((0, fc[:].rearrange("p c d -> p (c d)")), (1, proj[:])):
                    then(nc.vector.tensor_scalar(below[:, n], src, edge[:, 1, n:n + 1], None, ALU.is_lt))
                    then(nc.vector.scalar_tensor_tensor(tern[:, n], src, edge[:, 0, n:n + 1], below[:, n],
                                                        ALU.is_gt, ALU.subtract))
                for c in range(C):
                    nc.vector.tensor_copy(b_rows[:, c, :], ln_b[:, c:c + 1].to_broadcast([P, P]))
                dve.wait_ge(product, 2)
                nc.vector.tensor_copy(w1[:], bank[1])
                for c in range(C):
                    nc.vector.tensor_scalar(w2[:, c, :], bank[2][:, c * D:(c + 1) * D], ln_w[:, c:c + 1], None, ALU.mult)
                then(nc.vector.tensor_copy(w2_plain[:].rearrange("p c d -> p (c d)"), bank[2]))
                dve.wait_ge(product, 3)
                nc.vector.tensor_copy(shift[:], bank[3][:, 0:D])

            @block.tensor
            def _(pe):
                pe.wait_ge(made, 1)
                pe.matmul(bank[0][:, 0:2], ones[:], total[:], start=True, stop=True).then_inc(product, 1)
                pe.wait_ge(made, 8)
                for c in range(C):
                    pe.transpose(bank[1][:, c * P:(c + 1) * P], tern[:, 0, c * P:(c + 1) * P], core.ident[:])
                    mm = pe.transpose(bank[2][:, c * P:(c + 1) * P], tern[:, 1, c * P:(c + 1) * P], core.ident[:])
                mm.then_inc(product, 1)
                pe.wait_ge(made, 9)
                for c in range(C):
                    mm = pe.matmul(bank[3][:, 0:D], b_rows[:, c, :], w2_plain[:, c, :], start=c == 0, stop=c == C - 1)
                mm.then_inc(product, 1)

        hid = sb("f1_hid", [P, TILES, H])
        stage, xT = sb("f1_stage", [P, TPS, D]), sb("f1_xT", [D, LEN])
        staged, turned, xT_ready, hidden, bent = (sem("f1_" + n) for n in ("staged", "turned", "xT_ready", "hidden", "bent"))
        with nc.Block() as block:
            @block.vector
            def _(dve):
                dve.sem_inc(turned, 1)
                with dve.Fori(0, SEQS) as b:
                    dve.wait_ge(turned, b + 1)
                    put_normalized(core, dve, b, stage, staged)

            @block.tensor
            def _(pe):
                with pe.Fori(0, SEQS) as b:
                    pe.wait_ge(staged, TPS * b + TPS)
                    for t in range(TPS):
                        mm = pe.transpose(bank[0][:, t * P:(t + 1) * P], stage[:, t, :], core.ident[:])
                    mm.then_inc(turned, 1)
                    pe.wait_ge(xT_ready, b + 1)
                    for t in range(TPS):
                        mm = pe.matmul(bank[1 + t], xT[:, t * P:(t + 1) * P], w1[:], start=True, stop=True)
                    mm.then_inc(hidden, 1)

            @block.scalar
            def _(act):
                with act.Fori(0, SEQS) as b:
                    act.wait_ge(turned, b + 2)
                    nc.scalar.copy(xT[:], bank[0][:, 0:LEN]).then_inc(xT_ready, 1)
                    act.wait_ge(hidden, b + 1)
                    nc.scalar.activation(hid[:, tile(TPS * b, TPS), :], core.banks[:, 1:3, :], ACT.Gelu).then_inc(bent, 1)

        stats_block(core, "f1h", hid, LN_EPS, width=H)

        norm, normT = sb("f1_norm", [P, TPS, H]), sb("f1_normT", [P, TPS, H])
        normed, flipped, normT_ready, projected, added = (sem("f1_" + n) for n in
                                                          ("normed", "flipped", "normT_ready", "projected", "added"))
        with nc.Block() as block:
            @block.vector
            def _(dve):
                with dve.Fori(0, SEQS) as b:
                    for t in range(TPS):
                        i = TPS * b + t
                        nc.vector.tensor_scalar(norm[:, t, :], flat(hid[:, tile(i), :]), core.mean[:, tile(i)],
                                                core.rstd[:, tile(i)], ALU.subtract, ALU.mult).then_inc(normed, 1)
                    dve.wait_ge(projected, b + 1)
                    xs = x[:, tile(TPS * b, TPS), :]
                    nc.vector.tensor_tensor(xs, xs, bank[3][:, 0:LEN].rearrange("p (t d) -> p t d", t=TPS), ALU.add)\
                        .then_inc(added, 1)
                    dve.wait_ge(added, 2 * b + 1)
                    nc.vector.tensor_tensor(xs, xs, shift[:, None, :].to_broadcast([P, TPS, D]), ALU.add).then_inc(added, 1)

            @block.tensor
            def _(pe):
                with pe.Fori(0, SEQS) as b:
                    for t in range(TPS):
                        pe.wait_ge(normed, TPS * b + t + 1)
                        for c in range(C):
                            mm = pe.transpose(bank[1 + t][:, c * P:(c + 1) * P], norm[:, t, c * P:(c + 1) * P], core.ident[:])
                        mm.then_inc(flipped, 1)
                    for t in range(TPS):
                        pe.wait_ge(normT_ready, TPS * b + t + 1)
                        for c in range(C):
                            mm = pe.matmul(bank[3][:, t * D:(t + 1) * D], normT[:, t, c * P:(c + 1) * P], w2[:, c, :],
                                           start=c == 0, stop=c == C - 1)
                    mm.then_inc(projected, 1)

            @block.scalar
            def _(act):
                with act.Fori(0, SEQS) as b:
                    for t in range(TPS):
                        act.wait_ge(flipped, TPS * b + t + 1)
                        nc.scalar.copy(normT[:, t, :], bank[1 + t]).then_inc(normT_ready, 1)


def l2_attention(core):
    nc, x, bank, dram = core.nc, core.x, core.bank, core.dram
    HEADS, HD, G = 16, 8, 4
    R = P // G
    with ExitStack() as stack:
        sb, sem = scratch(core, stack)
        wq, wk, wv = sb("a2_wq", [D, G, P]), sb("a2_wk", [D, G, P]), sb("a2_wv", [D, D])
        wo, bo, bv = sb("a2_wo", [D, D]), sb("a2_bo", [P, D]), sb("a2_bv", [P, D])
        bq, bk = sb("a2_bq", [P, G]), sb("a2_bk", [P, G])
        apart_f = sb("a2_apart_f", [P, TPS, LEN])
        slopes = sb("a2_slopes", [P, len(SLOPE_PARTS)])
        load_block(core, "a2", [(wq[:], dram["L2_wq"]), (wk[:], dram["L2_wk"]), (wv[:], dram["L2_wv"]), (wo[:], dram["L2_wo"]),
                                (bo[:], dram["L2_bo"]), (bv[:], dram["L2_bv"]), (bq[:], dram["L2_bq"]), (bk[:], dram["L2_bk"]),
                                (apart_f[:], dram["L2_apart"]), (slopes[:], dram["L2_slopes"])])
        stats_block(core, "a2s", x, LN_EPS)
        apart = sb("a2_apart", [P, TPS, LEN], BF16)
        diag = sb("a2_diag", [P, len(SLOPE_PARTS), P], BF16)
        first_part = [sum(1 for h, _ in SLOPE_PARTS if h < n) for n in range(HEADS + 1)]
        with nc.Block() as block:
            @block.vector
            def _(dve):
                nc.vector.tensor_copy(apart[:], apart_f[:])
                for n in range(len(SLOPE_PARTS)):
                    nc.vector.tensor_scalar(diag[:, n, :], core.ident[:], slopes[:, n:n + 1], None, ALU.mult)

        stage, xT = sb("a2_stage", [P, TPS, D]), sb("a2_xT", [D, LEN])
        q, k, v = sb("a2_q", [P, G, LEN]), sb("a2_k", [P, G, LEN]), sb("a2_v", [P, TPS, D])
        neg_top, total, inv = sb("a2_neg_top", [P, 2, TPS]), sb("a2_total", [P, TPS, HEADS]), sb("a2_inv", [P, TPS, HEADS])
        prob, probT = sb("a2_prob", [P, 2, TPS, LEN]), sb("a2_probT", [P, 2, 2 * LEN])
        att, attT = sb("a2_att", [P, TPS, D]), sb("a2_attT", [D, LEN])
        (staged, turned, xT_ready, projected, q_ready, k_ready, v_ready, scored, topped, expd, flipped, probT_ready, summed,
         inverted, att_ready, att_turned, attT_ready, out_made, added) = (
            sem("a2_" + n) for n in (
                "staged", "turned", "xT_ready", "projected", "q_ready", "k_ready", "v_ready", "scored", "topped", "expd",
                "flipped", "probT_ready", "summed", "inverted", "att_ready", "att_turned", "attT_ready", "out_made", "added"))
        with nc.Block() as block:
            @block.vector
            def _(dve):
                with dve.Fori(0, SEQS) as b:
                    put_normalized(core, dve, b, stage, staged)
                    dve.wait_ge(projected, b + 1)
                    for g in range(G):
                        nc.vector.tensor_scalar(q[:, g, :], bank[g // 2][:, g % 2 * LEN:(g % 2 + 1) * LEN], bq[:, g:g + 1],
                                                float(HD) ** -0.5, ALU.add, ALU.mult).then_inc(q_ready, 1)
                    nc.vector.tensor_tensor(v[:], bank[4][:, 0:LEN].rearrange("p (t d) -> p t d", t=TPS),
                                            bv[:, None, :].to_broadcast([P, TPS, D]), ALU.add).then_inc(v_ready, 1)
                    for h in range(HEADS + 1):
                        if h < HEADS:
                            dve.wait_ge(scored, b * HEADS + h + 1)
                            nc.vector.tensor_reduce(neg_top[:, h % 2, :], bank[h % 2].rearrange("p (t k) -> p t k", t=TPS),
                                                    AX.X, ALU.max, negate=True).then_inc(topped, 1)
                        if h >= 1:
                            u = h - 1
                            dve.wait_ge(flipped, b * HEADS + u + 1)
                            if u >= 2:
                                dve.wait_ge(summed, b * HEADS + u - 1)
                            nc.vector.tensor_copy(probT[:, u % 2, :], bank[2 + u % 2]).then_inc(probT_ready, 1)
                    nc.vector.reciprocal(inv[:], total[:]).then_inc(inverted, 1)
                    dve.wait_ge(inverted, b + 1)
                    dve.wait_ge(summed, b * HEADS + HEADS)
                    nc.vector.tensor_tensor(att[:].rearrange("p t (h f) -> p (t h) f", f=HD),
                                            bank[5][:, 0:LEN].rearrange("p (a f) -> p a f", f=HD),
                                            inv[:].rearrange("p t h -> p (t h)")[:, :, None].to_broadcast([P, TPS * HEADS, HD]),
                                            ALU.mult).then_inc(att_ready, 1)
                    dve.wait_ge(out_made, b + 1)
                    xs = x[:, tile(TPS * b, TPS), :]
                    nc.vector.tensor_tensor(xs, xs, bank[7][:, 0:LEN].rearrange("p (t d) -> p t d", t=TPS), ALU.add)\
                        .then_inc(added, 1)
                    dve.wait_ge(added, 2 * b + 1)
                    nc.vector.tensor_tensor(xs, xs, bo[:, None, :].to_broadcast([P, TPS, D]), ALU.add).then_inc(added, 1)

            @block.tensor
            def _(pe):
                def scores(b, h):
                    g, r = h // G, h % G * R
                    if h >= 2:
                        pe.wait_ge(expd, b * HEADS + h - 1)
                    for t in range(TPS):
                        out = bank[h % 2][:, t * LEN:(t + 1) * LEN]
                        for n in range(first_part[h], first_part[h + 1]):
                            pe.matmul(out, diag[:, n, :], apart[:, t, :], start=n == first_part[h], stop=False)
                        mm = pe.matmul(out, q[r:r + R, g, t * P:(t + 1) * P], k[r:r + R, g, :], start=False, stop=True)
                    mm.then_inc(scored, 1)

                def attend(b, h):
                    pe.wait_ge(expd, b * HEADS + h + 1)
                    for t in range(TPS):
                        for c in range(TPS):
                            mm = pe.transpose(bank[2 + h % 2][:, (t * TPS + c) * P:(t * TPS + c + 1) * P],
                                              prob[:, h % 2, t, c * P:(c + 1) * P], core.ident[:])
                    mm.then_inc(flipped, 1)

                def values(b, h):
                    pe.wait_ge(probT_ready, b * HEADS + h + 1)
                    for t in range(TPS):
                        for c in range(TPS):
                            o = t * D + h * HD
                            mm = pe.matmul(bank[5][:, o:o + HD], probT[:, h % 2, (t * TPS + c) * P:(t * TPS + c + 1) * P],
                                           v[:, c, h * HD:(h + 1) * HD], start=c == 0, stop=c == TPS - 1)
                    mm.then_inc(summed, 1)

                with pe.Fori(0, SEQS) as b:
                    pe.wait_ge(staged, TPS * b + TPS)
                    for t in range(TPS):
                        mm = pe.transpose(bank[6][:, t * P:(t + 1) * P], stage[:, t, :], core.ident[:])
                    mm.then_inc(turned, 1)
                    pe.wait_ge(xT_ready, b + 1)
                    for g in range(G):
                        pe.matmul(bank[g // 2][:, g % 2 * LEN:(g % 2 + 1) * LEN], wq[:, g, :], xT[:], start=True, stop=True)
                        pe.matmul(bank[2 + g // 2][:, g % 2 * LEN:(g % 2 + 1) * LEN], wk[:, g, :], xT[:], start=True, stop=True)
                    for t in range(TPS):
                        mm = pe.matmul(bank[4][:, t * D:(t + 1) * D], xT[:, t * P:(t + 1) * P], wv[:], start=True, stop=True)
                    mm.then_inc(projected, 1)
                    pe.wait_ge(q_ready, b * G + G)
                    pe.wait_ge(k_ready, b * G + G)
                    pe.wait_ge(v_ready, b + 1)
                    for h in range(HEADS + 2):
                        if h < HEADS:
                            scores(b, h)
                        if h >= 2:
                            values(b, h - 2)
                        if 1 <= h <= HEADS:
                            attend(b, h - 1)
                    pe.wait_ge(att_ready, b + 1)
                    for t in range(TPS):
                        mm = pe.transpose(bank[6][:, t * P:(t + 1) * P], att[:, t, :], core.ident[:])
                    mm.then_inc(att_turned, 1)
                    pe.wait_ge(attT_ready, b + 1)
                    for t in range(TPS):
                        mm = pe.matmul(bank[7][:, t * D:(t + 1) * D], attT[:, t * P:(t + 1) * P], wo[:], start=True, stop=True)
                    mm.then_inc(out_made, 1)

            @block.scalar
            def _(act):
                with act.Fori(0, SEQS) as b:
                    act.wait_ge(turned, b + 1)
                    nc.scalar.copy(xT[:], bank[6][:, 0:LEN]).then_inc(xT_ready, 1)
                    act.wait_ge(projected, b + 1)
                    for g in range(G):
                        nc.scalar.activation(k[:, g, :], bank[2 + g // 2][:, g % 2 * LEN:(g % 2 + 1) * LEN], ACT.Identity,
                                             bias=bk[:, g:g + 1]).then_inc(k_ready, 1)
                    for h in range(HEADS):
                        act.wait_ge(topped, b * HEADS + h + 1)
                        if h >= 2:
                            act.wait_ge(flipped, b * HEADS + h - 1)
                        for t in range(TPS):
                            e = nc.scalar.activation(prob[:, h % 2, t, :], bank[h % 2][:, t * LEN:(t + 1) * LEN], ACT.Exp,
                                                     bias=neg_top[:, h % 2, t:t + 1], accum_out=total[:, t, h:h + 1])
                        e.then_inc(expd, 1)
                    act.wait_ge(att_turned, b + 1)
                    nc.scalar.copy(attT[:], bank[6][:, 0:LEN]).then_inc(attT_ready, 1)


def l2_feedforward(core):
    nc, dram = core.nc, core.dram
    DEPTH = 6
    with ExitStack() as stack:
        sb, sem = scratch(core, stack)
        tables = sb("r_tables", [P, 2, 2, LEN])
        masks_f = sb("r_masks_f", [P, TPS, WINDOW_KEYS])
        masks = sb("r_masks", [P, TPS, WINDOW_KEYS], BF16)
        head_ones = sb("r_head_ones", [P, 2])
        load_block(core, "r", [(tables[:], dram["r_tables"]), (masks_f[:], dram["r_masks"]), (head_ones[:], dram["r_head_ones"])])
        with nc.Block() as block:
            @block.vector
            def _(dve):
                nc.vector.tensor_copy(masks[:], masks_f[:])

        saved = sb("r_saved", [P, TILES, D])
        enter_stream(core, "rs", saved)
        w = sb("w_w", [D, 5, HEADS2 * HD2])
        wo = sb("w_wo", [P, PAIRS2, D])
        qk_scale = sb("w_qk_scale", [P, 4])
        w1, w2 = sb("g_w1", [D, 6, P]), sb("g_w2", [P, 3, D])
        ln_g, ln_b, b1, b2 = sb("g_ln_g", [D, 1]), sb("g_ln_b", [D, 1]), sb("g_b1", [P, 6]), sb("g_b2", [P, D])

        def attention_loads(n):
            return [(w[:].rearrange("p a n -> p (a n)"), flat2(dram["r_w"][tile(n)])),
                    (wo[:].rearrange("p a n -> p (a n)"), flat2(dram["r_wo"][tile(n)])),
                    (qk_scale[:], flat2(dram["r_qk_scale"][tile(n)]))]

        def feedforward_loads(n):
            return [(w1[:].rearrange("p a n -> p (a n)"), flat2(dram["g_w1"][tile(n)])),
                    (w2[:].rearrange("p a n -> p (a n)"), flat2(dram["g_w2"][tile(n)])),
                    (ln_g[:], flat2(dram["g_ln_g"][tile(n)])), (ln_b[:], flat2(dram["g_ln_b"][tile(n)])),
                    (b1[:], flat2(dram["g_b1"][tile(n)])), (b2[:], flat2(dram["g_b2"][tile(n)]))]

        load_block(core, "w0", attention_loads(0))
        with nc.Fori(0, DEPTH) as layer:
            windowed_attention(core, layer, tables, masks, head_ones, w, wo, qk_scale, feedforward_loads(layer))
            gated_feedforward(core, layer, w1, w2, ln_g, ln_b, b1, b2, attention_loads(layer + 1))
        leave_stream(core, saved)


HEADS2, HD2 = 16, 64
WINDOW = 32
PAIRS2 = HEADS2 // 2
WINDOW_KEYS = WINDOW + P


def start_loads(core, block, name, loads, layer):
    landed = core.sem(f"{name}_landed")

    @block.sync
    def _(sp):
        for dst, src in loads:
            sp.dma_start(dst, src).then_inc(landed, 16)
        sp.wait_ge(landed, layer * (16 * len(loads)) + 16 * len(loads))
        sp.sem_inc(core.passed, 1)


def windowed_attention(core, layer, tables, masks, head_ones, w, wo, qk_scale, next_loads):
    nc, x, bank, dram = core.nc, core.x, core.bank, core.dram
    INNER = HEADS2 * HD2
    H2 = INNER // 2
    with ExitStack() as stack:
        sb, sem = scratch(core, stack)
        cos_t, sin_t = sb("w_cos", [P, 2 * LEN]), sb("w_sin", [P, 2 * LEN])
        stage, xT = sb("w_stage", [P, LEN]), sb("w_xT", [D, LEN + 1])
        v = sb("w_v", [P, 2, TPS, INNER])
        by_cos, by_sin, square = (sb("w_" + n, [P, 2, 2 * LEN]) for n in ("by_cos", "by_sin", "square"))
        rope = sb("w_rope", [P, PAIRS2, 2 * LEN])
        NORMS = 2 * TPS * HEADS2
        norm, inv_norm = sb("w_norm", [P, NORMS]), sb("w_inv_norm", [P, NORMS])
        k_inv = sb("w_k_inv", [P, TPS, HEADS2, HD2])
        k = sb("w_k", [P, 2, WINDOW + LEN])
        top, neg_top = (sb("w_" + n, [P, 2, 4]) for n in ("top", "neg_top"))
        total, inv = sb("w_total", [P, 4, 4]), sb("w_inv", [P, 4, 4])
        prob = sb("w_prob", [P, 2, 4, 2 * P])
        probT = sb("w_probT", [P, 2, 4 * P])
        prevT = sb("w_prevT", [P, 2, 2, P])
        att, attT = sb("w_att", [P, 2, TPS * P]), sb("w_attT", [P, 2, LEN])
        names = ("staged", "turned", "xT_ready", "v_made", "v_ready", "qk_made", "cos_done",
                 "squared", "roped", "sums_made", "rooted", "norms_ready", "k_spread", "k_turned", "k_ready", "scored",
                 "topped", "expd", "flipped", "probT_ready", "prevT_ready", "attended", "att_ready", "att_turned",
                 "attT_ready", "out_made", "added", "inverted")
        (staged, turned, xT_ready, v_made, v_ready, qk_made, cos_done, squared, roped, sums_made,
         rooted, norms_ready, k_spread, k_turned, k_ready, scored, topped, expd, flipped, probT_ready, prevT_ready, attended,
         att_ready, att_turned, attT_ready, out_made, added, inverted) = (sem("w_" + n) for n in names)
        BS = layer * SEQS
        US = layer * (SEQS * PAIRS2)
        norms4 = inv_norm[:].rearrange("p (i t h) -> p i t h", i=2, t=TPS)

        with nc.Block() as block:
            @block.vector
            def _(dve):
                for i in range(2):
                    s = slice(i * LEN, (i + 1) * LEN)
                    nc.vector.tensor_scalar(cos_t[:, s], tables[:, 0, i], qk_scale[:, i:i + 1], None, ALU.mult)
                    nc.vector.tensor_scalar(sin_t[:, s], tables[:, 1, i], qk_scale[:, 2 + i:3 + i], None, ALU.mult)
                nc.vector.memset(xT[:], 0.0)
                nc.vector.memset(k[:], 0.0)

            @block.gpsimd
            def _(pool):
                nc.gpsimd.memset(prob[:], 0.0)
                nc.gpsimd.memset(prevT[:], 0.0)

        SUMS = TPS * WINDOW_KEYS

        def over_sequences(eng, sequence):
            sequence(-1, 0, before=False, now=False, following=True)
            sequence(0, 1, before=False, now=True, following=True)
            with eng.Fori(0, (SEQS - 2) // 2) as i:
                for k in range(2):
                    sequence(2 * i + 1 + k, k, before=True, now=True, following=True)
            sequence(SEQS - 1, 0, before=True, now=True, following=False)
            sequence(SEQS, 1, before=True, now=False, following=False)

        with nc.Block() as block:
            start_loads(core, block, "g", next_loads, layer)

            @block.tensor
            def _(pe):
                def sums(u, hp, wait_scores):
                    pe.wait_ge(squared, u + PAIRS2)
                    if wait_scores:
                        pe.wait_ge(expd, u)
                    for i in range(2):
                        for t in range(TPS):
                            o = SUMS + (i * TPS + t) * HEADS2 + 2 * hp
                            mm = pe.matmul(bank[0][:, o:o + 2], square[:, hp % 2, i * LEN + t * P:i * LEN + (t + 1) * P],
                                           head_ones[:], start=True, stop=True)
                    mm.then_inc(sums_made, 1)

                def project(u, hp, wait_last):
                    if wait_last:
                        pe.wait_ge(cos_done, u + PAIRS2)
                    for n in range(4):
                        mm = pe.matmul(bank[2 + n % 2][:, n // 2 * LEN:(n // 2 + 1) * LEN], w[:, n, hp * P:(hp + 1) * P],
                                       xT[:, 0:LEN], start=True, stop=True)
                    mm.then_inc(qk_made, 1)

                def values(u, hp, wait_last, outputs):
                    if wait_last:
                        pe.wait_ge(v_ready, u + PAIRS2)
                    if outputs is not None:
                        pe.wait_ge(added, outputs)
                    for t in range(TPS):
                        mm = pe.matmul(bank[7][:, LEN + t * P:LEN + (t + 1) * P], xT[:, t * P:(t + 1) * P],
                                       w[:, 4, hp * P:(hp + 1) * P], start=True, stop=True)
                    mm.then_inc(v_made, 1)

                def spread(u, hp):
                    pe.wait_ge(k_spread, u + 1)
                    for t in range(TPS):
                        mm = pe.transpose(bank[5][:, t * P:(t + 1) * P],
                                          k_inv[:, t, 2 * hp:2 * hp + 2, :].rearrange("p h f -> p (h f)"), core.ident[:])
                    mm.then_inc(k_turned, 1)

                def scores(u, hp, wait_last):
                    pe.wait_ge(k_ready, u + 1)
                    if wait_last:
                        pe.wait_ge(expd, u)
                    for h in range(2):
                        pe.matmul(bank[h][:, 0:TPS * WINDOW_KEYS], core.ident_bf[:],
                                  masks[:].rearrange("p t k -> p (t k)"), start=True, stop=False)
                    for t in range(TPS):
                        for h in range(2):
                            mm = pe.matmul(bank[h][:, t * WINDOW_KEYS:(t + 1) * WINDOW_KEYS],
                                           rope[HD2 * h:HD2 * (h + 1), hp, t * P:(t + 1) * P],
                                           k[HD2 * h:HD2 * (h + 1), hp % 2, t * P:t * P + WINDOW_KEYS], start=False, stop=t == TPS - 1)
                    mm.then_inc(scored, 1)

                def flip(u, hp, wait_last):
                    a = hp % 2
                    pe.wait_ge(expd, u + 1)
                    if wait_last:
                        pe.wait_ge(att_ready, u)
                    for j in range(4):
                        pe.transpose(bank[4][:, j * P:(j + 1) * P], prob[:, a, j, P:2 * P], core.ident[:])
                    for h in range(2):
                        mm = pe.transpose(bank[6][:, h * WINDOW:(h + 1) * WINDOW], prob[0:WINDOW, a, 2 + h, 0:P],
                                          core.ident[0:WINDOW, 0:WINDOW])
                    mm.then_inc(flipped, 1)

                def attend(u, hp, half):
                    a = hp % 2
                    pe.wait_ge(probT_ready, u + 1)
                    pe.wait_ge(prevT_ready, u + 1)
                    for t in range(TPS):
                        for h in range(2):
                            j = 2 * t + h
                            out = bank[6][:, P + j * HD2:P + (j + 1) * HD2]
                            hs = slice((2 * hp + h) * HD2, (2 * hp + h + 1) * HD2)
                            mm = pe.matmul(out, probT[:, a, j * P:(j + 1) * P], v[:, half, t, hs], start=True, stop=t == 0)
                            if t == 1:
                                mm = pe.matmul(out, prevT[:, a, h, :], v[:, half, 0, hs], start=False, stop=True)
                    mm.then_inc(attended, 1)

                def turn_att(u, hp, wait_k):
                    pe.wait_ge(att_ready, u + 1)
                    if wait_k:
                        pe.wait_ge(k_ready, u + 4)
                    for t in range(TPS):
                        mm = pe.transpose(bank[5][:, LEN + t * P:LEN + (t + 1) * P], att[:, hp % 2, t * P:(t + 1) * P], core.ident[:])
                    mm.then_inc(att_turned, 1)

                def output(u, hp, taken, wait_last):
                    pe.wait_ge(attT_ready, u + 1)
                    if taken is not None:
                        pe.wait_ge(v_ready, taken)
                    if wait_last:
                        pe.wait_ge(added, u)
                    for t in range(TPS):
                        mm = pe.matmul(bank[7][:, t * D:(t + 1) * D], attT[:, hp % 2, t * P:(t + 1) * P], wo[:, hp, :],
                                       start=True, stop=True)
                    mm.then_inc(out_made, 1)

                def sequence(b, NEXT, before, now, following):
                    def has(s, back):
                        return now if s >= back else before

                    for s in range(PAIRS2):
                        u = US + b * PAIRS2 + s
                        if s == 0:
                            if before:
                                attend(u - 2, PAIRS2 - 2, NEXT)
                            if now:
                                sums(u, PAIRS2 - 1, before)
                            if before:
                                output(u - 3, PAIRS2 - 3, u + PAIRS2 if now else None, True)
                            if following:
                                if now:
                                    pe.wait_ge(cos_done, u + PAIRS2)
                                pe.wait_ge(staged, BS + b + 2)
                                for t in range(TPS):
                                    mm = pe.transpose(bank[2][:, t * P:(t + 1) * P], stage[:, t * P:(t + 1) * P], core.ident[:])
                                mm.then_inc(turned, 1)
                            if before:
                                flip(u - 1, PAIRS2 - 1, True)
                                turn_att(u - 2, PAIRS2 - 2, False)
                            if following:
                                pe.wait_ge(xT_ready, BS + b + 2)
                                project(u, 0, now)
                            if now:
                                if before:
                                    pe.wait_ge(attT_ready, u - 1)
                                spread(u, 0)
                                scores(u, 0, before)
                                spread(u + 1, 1)
                            if following:
                                values(u, 0, now, u - 2 if before else None)
                        else:
                            if following:
                                project(u, s, True)
                                values(u, s, True, u - 3 if has(s, 4) else None)
                                sums(u, s - 1, now)
                            if now:
                                scores(u, s, True)
                            if has(s, 2):
                                attend(u - 2, (s - 2) % PAIRS2, NEXT if s < 2 else 1 - NEXT)
                            if has(s, 3):
                                output(u - 3, (s - 3) % PAIRS2, u + PAIRS2 + 1 if following else None, has(s, 4))
                            if now and s + 1 < PAIRS2:
                                spread(u + 1, s + 1)
                            if now:
                                flip(u - 1, s - 1, has(s, 2))
                            if has(s, 2):
                                turn_att(u - 2, (s - 2) % PAIRS2, now and s + 1 < PAIRS2)

                over_sequences(pe, sequence)

            @block.vector
            def _(dve):
                def reduce_scores(u, s):
                    a = s % 2
                    dve.wait_ge(scored, u + 1)
                    nc.vector.tensor_reduce(top[:, a, :].rearrange("p (t h) -> p t h", t=2),
                                            core.banks[:, 0:2, 0:TPS * WINDOW_KEYS].rearrange("p h (t c) -> p t h c", t=2),
                                            AX.X, ALU.max, negate=True).then_inc(topped, 1)
                    dve.wait_ge(topped, 2 * u + 1)
                    nc.vector.tensor_tensor(neg_top[:, a, :].rearrange("p (t h) -> p t h", t=2),
                                            top[:, a, :].rearrange("p (t h) -> p t h", t=2),
                                            norms4[:, 0, :, 2 * s:2 * s + 2], ALU.mult).then_inc(topped, 1)

                def divide(u, hp):
                    dve.wait_ge(inverted, u + 1)
                    dve.wait_ge(attended, u + 1)
                    nc.vector.tensor_tensor(att[:, hp % 2, :].rearrange("p (j f) -> p j f", j=4),
                                            bank[6][:, P:P + 4 * HD2].rearrange("p (j f) -> p j f", j=4),
                                            inv[:, hp % 4, :, None].to_broadcast([P, 4, HD2]), ALU.mult).then_inc(att_ready, 1)

                def add_output(u, b):
                    dve.wait_ge(out_made, u + 1)
                    xs = x[:, tile(TPS * b, TPS), :]
                    nc.vector.tensor_tensor(xs, xs, bank[7][:, 0:LEN].rearrange("p (t d) -> p t d", t=TPS), ALU.add)\
                        .then_inc(added, 1)

                def scale_keys(u, hp):
                    dve.wait_ge(k_turned, u + 1)
                    dve.wait_ge(roped, u + 1)
                    nc.vector.tensor_tensor(k[:, hp % 2, WINDOW:], rope[:, hp, LEN:2 * LEN], bank[5][:, 0:LEN], ALU.mult)\
                        .then_inc(k_ready, 1)

                def rotate(u, hp, wait_buffer):
                    a = hp % 2
                    dve.wait_ge(qk_made, u + PAIRS2 + 1)
                    if wait_buffer:
                        dve.wait_ge(roped, u + PAIRS2 - 1)
                    nc.vector.tensor_tensor(by_sin[:, a, :], bank[3], sin_t[:], ALU.mult)
                    dve.wait_ge(squared, u + PAIRS2 + 1)
                    nc.vector.tensor_tensor(by_cos[:, a, :], bank[2], cos_t[:], ALU.mult).then_inc(cos_done, 1)

                def take_flipped(u, hp):
                    dve.wait_ge(flipped, u + 1)
                    nc.vector.tensor_copy(prevT[:, hp % 2, :, 0:WINDOW],
                                          bank[6][:, 0:2 * WINDOW].rearrange("p (h q) -> p h q", h=2)).then_inc(prevT_ready, 1)
                    nc.vector.reciprocal(inv[:, hp % 4, :], total[:, hp % 4, :]).then_inc(inverted, 1)

                def sequence(b, NEXT, before, now, following):
                    def has(s, back):
                        return now if s >= back else before

                    if following:
                        if now:
                            dve.wait_ge(qk_made, US + b * PAIRS2 + PAIRS2)
                        nc.vector.tensor_copy(stage[:], x[:, tile(TPS * b + TPS, TPS), :].rearrange("p t d -> p (t d)"))\
                            .then_inc(staged, 1)
                    for s in range(PAIRS2):
                        u = US + b * PAIRS2 + s
                        if s >= 1 and following:
                            rotate(u, s, s >= 2 or now)
                        if s >= 1 and now:
                            reduce_scores(u, s)
                        if has(s, 2):
                            divide(u - 2, (s - 2) % PAIRS2)
                        if s == 0 and now:
                            dve.wait_ge(rooted, BS + b + 1)
                            nc.vector.tensor_scalar(norm[:], norm[:], 1e-12, None, ALU.max).then_inc(norms_ready, 1)
                            dve.wait_ge(norms_ready, 2 * (BS + b) + 1)
                            nc.vector.reciprocal(inv_norm[:], norm[:]).then_inc(norms_ready, 1)
                        if has(s, 3):
                            add_output(u - 3, b if s >= 3 else b - 1)
                        if s >= 1 and now and s + 1 < PAIRS2:
                            scale_keys(u + 1, s + 1)
                        if has(s, 1):
                            take_flipped(u - 1, (s - 1) % PAIRS2)
                        if s == 0:
                            if now:
                                scale_keys(u, 0)
                            if following:
                                rotate(u, 0, now)
                            if now:
                                dve.wait_ge(norms_ready, 2 * (BS + b) + 2)
                                reduce_scores(u, 0)
                                scale_keys(u + 1, 1)

                over_sequences(dve, sequence)

            @block.gpsimd
            def _(pool):
                def sequence(b, NEXT, before, now, following):
                    for s in range(PAIRS2):
                        u = US + b * PAIRS2 + s
                        if now:
                            if s == 0:
                                pool.wait_ge(norms_ready, 2 * (BS + b) + 2)
                                pool.sem_inc(core.passed, 1)
                            for hp in range(3) if s == 0 else range(s + 2, s + 3):
                                if hp < PAIRS2:
                                    hs = slice(2 * hp, 2 * hp + 2)
                                    nc.gpsimd.tensor_copy(k_inv[:, :, hs, :],
                                                          norms4[:, 1, :, hs, None].to_broadcast([P, TPS, 2, HD2])).then_inc(k_spread, 1)
                        if following:
                            if now:
                                pool.wait_ge(scored, u + 1)
                            pool.wait_ge(cos_done, u + PAIRS2 + 1)
                            nc.gpsimd.tensor_tensor(rope[:, s, :], by_cos[:, s % 2, :], by_sin[:, s % 2, :], ALU.add).then_inc(roped, 1)

                over_sequences(pool, sequence)

            @block.scalar
            def _(act):
                def exponentials(u, s):
                    a = s % 2
                    act.wait_ge(topped, 2 * u + 2)
                    for j in range(4):
                        t, h = j // 2, j % 2
                        e = nc.scalar.activation(prob[:, a, j, P - WINDOW:2 * P],
                                                 bank[h][:, t * WINDOW_KEYS:(t + 1) * WINDOW_KEYS], ACT.Exp,
                                                 bias=neg_top[:, a, j:j + 1], scale=norms4[:, 0, t, 2 * s + h:2 * s + h + 1],
                                                 accum_out=total[:, s % 4, j:j + 1])
                    e.then_inc(expd, 1)

                def squares(u, hp, wait_buffer):
                    act.wait_ge(qk_made, u + PAIRS2 + 1)
                    if wait_buffer:
                        act.wait_ge(sums_made, u + PAIRS2 - 1)
                    nc.scalar.activation(square[:, hp % 2, :], bank[2], ACT.Square).then_inc(squared, 1)

                def take_values(u, hp, half):
                    act.wait_ge(v_made, u + PAIRS2 + 1)
                    nc.scalar.copy(v[:, half, :, hp * P:(hp + 1) * P], bank[7][:, LEN:2 * LEN].rearrange("p (t n) -> p t n", t=TPS))\
                        .then_inc(v_ready, 1)

                def take_flipped(u, hp):
                    act.wait_ge(flipped, u + 1)
                    nc.scalar.copy(probT[:, hp % 2, :], bank[4]).then_inc(probT_ready, 1)

                def take_turned(u, hp, wait_buffer):
                    act.wait_ge(att_turned, u + 1)
                    if wait_buffer:
                        act.wait_ge(out_made, u - 1)
                    nc.scalar.copy(attT[:, hp % 2, :], bank[5][:, LEN:2 * LEN]).then_inc(attT_ready, 1)

                def sequence(b, NEXT, before, now, following):
                    def has(s, back):
                        return now if s >= back else before

                    for s in range(PAIRS2):
                        u = US + b * PAIRS2 + s
                        if s == 0:
                            if now:
                                act.wait_ge(sums_made, u + PAIRS2)
                                nc.scalar.activation(norm[:], bank[0][:, SUMS:SUMS + NORMS], ACT.Sqrt).then_inc(rooted, 1)
                            if following:
                                act.wait_ge(turned, BS + b + 2)
                                nc.scalar.copy(xT[0:HD2, 0:LEN], bank[2][0:HD2, 0:LEN])
                                nc.scalar.copy(xT[HD2:P, 1:LEN + 1], bank[2][HD2:P, 0:LEN]).then_inc(xT_ready, 1)
                        else:
                            if following:
                                squares(u, s, s >= 2 or now)
                                take_values(u, s, NEXT)
                            if now:
                                exponentials(u, s)
                        if has(s, 1):
                            take_flipped(u - 1, (s - 1) % PAIRS2)
                        if has(s, 2):
                            take_turned(u - 2, (s - 2) % PAIRS2, has(s, 4))
                        if s == 0:
                            if following:
                                squares(u, 0, now)
                            if now:
                                exponentials(u, 0)
                            if following:
                                take_values(u, 0, NEXT)

                over_sequences(act, sequence)


def gated_feedforward(core, layer, w1, w2, ln_g, ln_b, b1, b2, next_loads):
    nc, x, bank, dram = core.nc, core.x, core.bank, core.dram
    C = 3
    HALF = D // 2
    with ExitStack() as stack:
        sb, sem = scratch(core, stack)
        shifted = sb("g_shifted", [P, TILES, D])
        by_seq = [a.rearrange("p (s t) d -> p s t d", t=TPS) for a in (x[:], shifted[:])]
        moves = [(shifted[:, :, 0:HALF], x[:, :, 0:HALF]),
                 (shifted[1:P, :, HALF:D], x[0:P - 1, :, HALF:D]),
                 (by_seq[1][0:1, :, 1, HALF:D], by_seq[0][P - 1:P, :, 0, HALF:D])]
        summed = sem("g_summed")
        bias = sb("g_bias", [P, 2 * C])
        with nc.Block() as block:
            start_loads(core, block, "gs", moves, layer)

            @block.tensor
            def _(pe):
                for n in range(2 * C):
                    mm = pe.matmul(bank[0][:, n:n + 1], w1[:, n, :], ln_b[:], start=True, stop=True)
                mm.then_inc(summed, 1)

            @block.vector
            def _(dve):
                nc.vector.memset(by_seq[1][0:1, :, 0, HALF:D], 0.0)
                dve.wait_ge(summed, layer + 1)
                nc.vector.tensor_tensor(bias[:], bank[0][:, 0:2 * C], b1[:], ALU.add)
                nc.vector.tensor_scalar(w1[:], w1[:], ln_g[:, 0:1], None, ALU.mult)

        stats_block(core, "gs", shifted, LN_EPS, layer=layer)

        stage, xT = sb("g_stage", [P, 2, TPS, D]), sb("g_xT", [D, 2, LEN])
        gate, hid = sb("g_gate", [P, C, LEN]), sb("g_hid", [P, 2, C, LEN])
        staged, turned, xT_ready, made, bent, gated, out_made, added, based = (
            sem("g_" + n) for n in ("staged", "turned", "xT_ready", "hid_made", "bent", "gated", "out_made", "added", "based"))
        BS = layer * SEQS

        def first_of_all(b):
            return isinstance(b, int) and b == 1

        def over_sequences(eng, turn):
            turn(-1, 1, finish=False, now=False, front=True)
            turn(0, 0, finish=False, now=True, front=True)
            turn(1, 1, finish=True, now=True, front=True)
            with eng.Fori(0, (SEQS - 4) // 2) as i:
                for k in range(2):
                    turn(2 * i + 2 + k, k, finish=True, now=True, front=True)
            turn(SEQS - 2, 0, finish=True, now=True, front=True)
            turn(SEQS - 1, 1, finish=True, now=True, front=False)
            turn(SEQS, 0, finish=True, now=False, front=False)

        with nc.Block() as block:
            start_loads(core, block, "w", next_loads, layer)

            @block.vector
            def _(dve):
                def turn(b, half, finish, now, front):
                    if front:
                        if finish:
                            dve.wait_ge(turned, BS + b)
                        for t in range(TPS):
                            i = TPS * b + TPS + t
                            nc.vector.tensor_scalar(stage[:, 1 - half, t, :], flat(shifted[:, tile(i), :]), core.mean[:, tile(i)],
                                                    core.rstd[:, tile(i)], ALU.subtract, ALU.mult).then_inc(staged, 1)
                    if now:
                        for c in range(C):
                            dve.wait_ge(bent, C * (BS + b) + c + 1)
                            nc.vector.scalar_tensor_tensor(hid[:, half, c, :], bank[1 + C * half + c][:, 0:LEN], bias[:, c:c + 1],
                                                           gate[:, c, :], ALU.add, ALU.mult).then_inc(gated, 1)
                    if finish:
                        dve.wait_ge(out_made, BS + b)
                        dve.wait_ge(based, BS + b)
                        xs = x[:, tile(TPS * b - TPS, TPS), :]
                        nc.vector.tensor_tensor(xs, xs, bank[7][:, 0:LEN].rearrange("p (t d) -> p t d", t=TPS), ALU.add)\
                            .then_inc(added, 1)

                over_sequences(dve, turn)

            @block.gpsimd
            def _(pool):
                with pool.Fori(0, SEQS) as b:
                    xs = x[:, tile(TPS * b, TPS), :]
                    nc.gpsimd.tensor_tensor(xs, xs, b2[:, None, :].to_broadcast([P, TPS, D]), ALU.add).then_inc(based, 1)

            @block.tensor
            def _(pe):
                def turn(b, half, finish, now, front):
                    if now:
                        pe.wait_ge(xT_ready, BS + b + 1)
                        for c in range(C):
                            pe.matmul(bank[1 + C * half + c][:, 0:LEN], w1[:, c, :], xT[:, half, :], start=True, stop=True)
                            pe.matmul(bank[1 + C * half + c][:, LEN:2 * LEN], w1[:, C + c, :], xT[:, half, :],
                                      start=True, stop=True).then_inc(made, 1)
                    if front:
                        pe.wait_ge(staged, TPS * (BS + b) + 2 * TPS)
                        for t in range(TPS):
                            mm = pe.transpose(bank[0][:, t * P:(t + 1) * P], stage[:, 1 - half, t, :], core.ident[:])
                        mm.then_inc(turned, 1)
                    if finish:
                        pe.wait_ge(gated, C * (BS + b))
                        if not first_of_all(b):
                            pe.wait_ge(added, BS + b - 1)
                        for t in range(TPS):
                            for c in range(C):
                                mm = pe.matmul(bank[7][:, t * D:(t + 1) * D], hid[:, 1 - half, c, t * P:(t + 1) * P], w2[:, c, :],
                                               start=c == 0, stop=c == C - 1)
                        mm.then_inc(out_made, 1)

                over_sequences(pe, turn)

            @block.scalar
            def _(act):
                def turn(b, half, finish, now, front):
                    if now:
                        for c in range(C):
                            act.wait_ge(made, C * (BS + b) + c + 1)
                            if finish:
                                act.wait_ge(gated, C * (BS + b) - C + c + 1)
                            nc.scalar.activation(gate[:, c, :], bank[1 + C * half + c][:, LEN:2 * LEN], ACT.Gelu,
                                                 bias=bias[:, C + c:C + c + 1]).then_inc(bent, 1)
                    if front:
                        act.wait_ge(turned, BS + b + 2)
                        nc.scalar.copy(xT[:, 1 - half, :], bank[0][:, 0:LEN]).then_inc(xT_ready, 1)

                over_sequences(act, turn)


def flat2(ap):
    return ap.rearrange("a p n -> (a p) n")


def l3_attention(core):
    nc, x, bank, dram = core.nc, core.x, core.bank, core.dram
    with ExitStack() as stack:
        sb, sem = scratch(core, stack)
        w, bqk, bv = sb("a3_w", [D, 3 * D]), sb("a3_bqk", [D, 2]), sb("a3_bv", [P, D])
        decay = sb("a3_decay", [P, 3, P])
        load_block(core, "a3", [(w[:], dram["L3_wqkv"]), (bqk[:], dram["L3_bqk"]), (bv[:], dram["L3_bv"]),
                                (decay[:], dram["L3_decay"])])
        stats_block(core, "a3s", x, LN_EPS)
        stage, xT = sb("a3_stage", [P, TPS, D]), sb("a3_xT", [D, LEN])
        qk, v, score = sb("a3_qk", [D, 2, LEN]), sb("a3_v", [P, TPS, D]), sb("a3_score", [P, 3, P])
        staged, turned, xT_ready, made, qk_ready, v_ready, scored, decayed, out_made, added = (
            sem("a3_" + n) for n in ("staged", "turned", "xT_ready", "made", "qk_ready", "v_ready", "scored", "decayed",
                                     "out_made", "added"))
        with nc.Block() as block:
            @block.vector
            def _(dve):
                with dve.Fori(0, SEQS) as b:
                    put_normalized(core, dve, b, stage, staged)
                    dve.wait_ge(made, b + 1)
                    nc.vector.tensor_tensor(v[:], bank[2][:, 0:LEN].rearrange("p (t d) -> p t d", t=TPS),
                                            bv[:, None, :].to_broadcast([P, TPS, D]), ALU.add).then_inc(v_ready, 1)
                    dve.wait_ge(scored, b + 1)
                    nc.vector.tensor_tensor(score[:], bank[3][:, 0:3 * P].rearrange("p (n q) -> p n q", n=3), decay[:], ALU.mult)\
                        .then_inc(decayed, 1)
                    dve.wait_ge(out_made, b + 1)
                    xs = x[:, tile(TPS * b, TPS), :]
                    nc.vector.tensor_tensor(xs, xs, bank[4][:, 0:LEN].rearrange("p (t d) -> p t d", t=TPS), ALU.add)

            @block.tensor
            def _(pe):
                with pe.Fori(0, SEQS) as b:
                    pe.wait_ge(staged, TPS * b + TPS)
                    for t in range(TPS):
                        mm = pe.transpose(bank[0][:, t * P:(t + 1) * P], stage[:, t, :], core.ident[:])
                    mm.then_inc(turned, 1)
                    pe.wait_ge(xT_ready, b + 1)
                    for n in range(2):
                        pe.matmul(bank[1][:, n * LEN:(n + 1) * LEN], w[:, n * D:(n + 1) * D], xT[:], start=True, stop=True)
                    for t in range(TPS):
                        mm = pe.matmul(bank[2][:, t * D:(t + 1) * D], xT[:, t * P:(t + 1) * P], w[:, 2 * D:3 * D], start=True, stop=True)
                    mm.then_inc(made, 1)
                    pe.wait_ge(qk_ready, b + 1)
                    pe.matmul(bank[3][:, 0:LEN], qk[:, 1, 0:P], qk[:, 0, :], start=True, stop=True)
                    pe.matmul(bank[3][:, LEN:LEN + P], qk[:, 1, P:LEN], qk[:, 0, P:LEN], start=True, stop=True).then_inc(scored, 1)
                    pe.wait_ge(v_ready, b + 1)
                    pe.wait_ge(decayed, b + 1)
                    pe.matmul(bank[4][:, 0:D], score[:, 0, :], v[:, 0, :], start=True, stop=True)
                    pe.matmul(bank[4][:, D:2 * D], score[:, 1, :], v[:, 0, :], start=True, stop=False)
                    pe.matmul(bank[4][:, D:2 * D], score[:, 2, :], v[:, 1, :], start=False, stop=True).then_inc(out_made, 1)

            @block.scalar
            def _(act):
                with act.Fori(0, SEQS) as b:
                    act.wait_ge(turned, b + 1)
                    nc.scalar.copy(xT[:], bank[0][:, 0:LEN]).then_inc(xT_ready, 1)
                    act.wait_ge(made, b + 1)
                    for n in range(2):
                        ins = nc.scalar.activation(qk[:, n, :], bank[1][:, n * LEN:(n + 1) * LEN], ACT.Identity, bias=bqk[:, n:n + 1])
                    ins.then_inc(qk_ready, 1)


def l3_feedforward(core):
    nc, x, bank, dram = core.nc, core.x, core.bank, core.dram
    LAYERS, E, H = 4, 4, 512
    C = H // P
    with ExitStack() as stack:
        sb, sem = scratch(core, stack)
        w1, w2 = sb("m_w1", [D, E, H]), sb("m_w2", [P, E * C, D])
        g, b_ln, b1, b2 = sb("m_g", [D, E]), sb("m_b_ln", [D, E]), sb("m_b1", [P, E * C]), sb("m_b2", [P, E, D])
        rw, rb, earlier = sb("m_rw", [D, E]), sb("m_rb", [P, E]), sb("m_earlier", [P, E, E])
        load_block(core, "m0", [(earlier[:].rearrange("p a b -> p (a b)"), dram["m_earlier"])])
        bias = sb("m_bias", [P, E * C])
        stage, xT = sb("m_stage", [P, TPS, D]), sb("m_xT", [D, LEN])
        logit, top, comb, rank, kept = (sb("m_" + n, s) for n, s in (
            ("logit", [P, TILES, E]), ("top", [P, TILES]), ("comb", [P, TILES, E]), ("rank", [P, TILES, E]), ("kept", [P, TILES])))
        above, equal = sb("m_above", [P, TILES, E, E]), sb("m_equal", [P, TILES, E, E])
        hid = sb("m_hid", [P, 2, C, LEN])
        names = ("summed", "r_staged", "r_turned", "r_xT_ready", "routed", "r_logits", "route", "spread", "staged", "turned",
                 "xT_ready", "hidden", "bent", "projected", "added", "based")
        (summed, r_staged, r_turned, r_xT_ready, routed, r_logits, route, spread, staged, turned, xT_ready, hidden, bent,
         projected, added, based) = (sem("m_" + n) for n in names)
        saved = sb("m_saved", [P, TILES, D])
        enter_stream(core, "ms0", saved)
        with nc.Fori(0, LAYERS) as layer:
            BS = layer * SEQS
            load_layer(core, "m", [(w1[:].rearrange("p e h -> p (e h)"), flat2(dram["m_w1"][tile(layer)])),
                                   (w2[:].rearrange("p n d -> p (n d)"), flat2(dram["m_w2"][tile(layer)])),
                                   (g[:], flat2(dram["m_g"][tile(layer)])), (b_ln[:], flat2(dram["m_b_ln"][tile(layer)])),
                                   (b1[:], flat2(dram["m_b1"][tile(layer)])),
                                   (b2[:].rearrange("p e d -> p (e d)"), flat2(dram["m_b2"][tile(layer)])),
                                   (rw[:], flat2(dram["m_rw"][tile(layer)])), (rb[:], flat2(dram["m_rb"][tile(layer)]))], layer)

            with nc.Block() as block:
                @block.tensor
                def _(pe):
                    for e in range(E):
                        for c in range(C):
                            n = e * C + c
                            mm = pe.matmul(bank[2][:, n:n + 1], w1[:, e, c * P:(c + 1) * P], b_ln[:, e:e + 1], start=True, stop=True)
                    mm.then_inc(summed, 1)
                    with pe.Fori(0, SEQS) as b:
                        pe.wait_ge(r_staged, BS + b + 1)
                        for t in range(TPS):
                            mm = pe.transpose(bank[0][:, t * P:(t + 1) * P], stage[:, t, :], core.ident[:])
                        mm.then_inc(r_turned, 1)
                        pe.wait_ge(r_xT_ready, BS + b + 1)
                        for t in range(TPS):
                            mm = pe.matmul(bank[1][:, t * E:(t + 1) * E], xT[:, t * P:(t + 1) * P], rw[:], start=True, stop=True)
                        mm.then_inc(routed, 1)

                @block.vector
                def _(dve):
                    dve.wait_ge(summed, layer + 1)
                    nc.vector.tensor_tensor(bias[:], bank[2][:, 0:E * C], b1[:], ALU.add)
                    for e in range(E):
                        nc.vector.tensor_scalar(w1[:, e, :], w1[:, e, :], g[:, e:e + 1], None, ALU.mult)
                    with dve.Fori(0, SEQS) as b:
                        nc.vector.tensor_copy(stage[:], x[:, tile(TPS * b, TPS), :]).then_inc(r_staged, 1)
                        dve.wait_ge(routed, BS + b + 1)
                        nc.vector.tensor_tensor(logit[:, tile(TPS * b, TPS), :],
                                                bank[1][:, 0:TPS * E].rearrange("p (t e) -> p t e", t=TPS),
                                                rb[:, None, :].to_broadcast([P, TPS, E]), ALU.add).then_inc(r_logits, 1)

                @block.scalar
                def _(act):
                    with act.Fori(0, SEQS) as b:
                        act.wait_ge(r_turned, BS + b + 1)
                        nc.scalar.copy(xT[:], bank[0][:, 0:LEN]).then_inc(r_xT_ready, 1)

            STEPS = 9
            with nc.Block() as block:
                @block.vector
                def _(dve):
                    then = Chain(dve, route, layer * STEPS)
                    then(nc.vector.tensor_reduce(top[:], logit[:], AX.X, ALU.max))
                    then(nc.vector.tensor_tensor(logit[:], logit[:], top[:, :, None].to_broadcast([P, TILES, E]), ALU.subtract))
                    dve.wait_ge(spread, layer + 1)
                    other = logit[:, :, None, :].to_broadcast([P, TILES, E, E])
                    own = logit[:, :, :, None].to_broadcast([P, TILES, E, E])
                    nc.vector.tensor_tensor(above[:], other, own, ALU.is_gt)
                    then(nc.vector.tensor_tensor(equal[:], other, own, ALU.is_equal))
                    then(nc.vector.tensor_tensor(equal[:], equal[:], earlier[:, None, :, :].to_broadcast([P, TILES, E, E]), ALU.mult))
                    then(nc.vector.tensor_tensor(above[:], above[:], equal[:], ALU.add))
                    then(nc.vector.tensor_reduce(rank[:], above[:], AX.X, ALU.add))
                    then(nc.vector.scalar_tensor_tensor(comb[:], rank[:], 1.5, logit[:], ALU.is_lt, ALU.mult))
                    then(nc.vector.tensor_reduce(kept[:], comb[:], AX.X, ALU.add))
                    then(nc.vector.reciprocal(top[:], kept[:]))
                    nc.vector.tensor_tensor(comb[:], comb[:], top[:, :, None].to_broadcast([P, TILES, E]), ALU.mult)
                    assert then.n == STEPS, then.n

                @block.scalar
                def _(act):
                    act.wait_ge(route, layer * STEPS + 2)
                    nc.scalar.activation(logit[:], logit[:], ACT.Exp).then_inc(spread, 1)

            stats_block(core, "ms", x, LN_EPS, layer=layer)

            with nc.Block() as block:
                @block.tensor
                def _(pe):
                    def up(b, e):
                        if e >= 2:
                            pe.wait_ge(bent, C * (E * (BS + b) + e - 1))
                        for c in range(C):
                            pe.matmul(bank[1 + 2 * (e % 2) + c // 2][:, c % 2 * LEN:(c % 2 + 1) * LEN],
                                      w1[:, e, c * P:(c + 1) * P], xT[:], start=True, stop=True).then_inc(hidden, 1)

                    def down(b, e):
                        pe.wait_ge(bent, C * (E * (BS + b) + e + 1))
                        if e >= 2:
                            pe.wait_ge(added, TPS * (E * (BS + b) + e - 1))
                        for t in range(TPS):
                            for c in range(C):
                                mm = pe.matmul(bank[5 + e % 2][:, t * D:(t + 1) * D], hid[:, e % 2, c, t * P:(t + 1) * P],
                                               w2[:, e * C + c, :], start=c == 0, stop=c == C - 1)
                        mm.then_inc(projected, 1)

                    with pe.Fori(0, SEQS) as b:
                        pe.wait_ge(staged, TPS * (BS + b) + TPS)
                        for t in range(TPS):
                            mm = pe.transpose(bank[0][:, t * P:(t + 1) * P], stage[:, t, :], core.ident[:])
                        mm.then_inc(turned, 1)
                        pe.wait_ge(xT_ready, BS + b + 1)
                        for e in range(E + 1):
                            if e < E:
                                up(b, e)
                            if e >= 1:
                                down(b, e - 1)

                @block.scalar
                def _(act):
                    with act.Fori(0, SEQS) as b:
                        act.wait_ge(turned, BS + b + 1)
                        nc.scalar.copy(xT[:], bank[0][:, 0:LEN]).then_inc(xT_ready, 1)
                        for e in range(E):
                            if e >= 2:
                                act.wait_ge(projected, E * (BS + b) + e - 1)
                            for c in range(C):
                                act.wait_ge(hidden, C * (E * (BS + b) + e) + c // 2 * 2 + 2)
                                nc.scalar.activation(hid[:, e % 2, c, :],
                                                     bank[1 + 2 * (e % 2) + c // 2][:, c % 2 * LEN:(c % 2 + 1) * LEN],
                                                     ACT.Gelu, bias=bias[:, e * C + c:e * C + c + 1]).then_inc(bent, 1)

                @block.vector
                def _(dve):
                    with dve.Fori(0, SEQS) as b:
                        put_normalized(core, dve, b, stage, staged)
                        for e in range(E):
                            for t in range(TPS):
                                i = TPS * b + t
                                xs = flat(x[:, tile(i), :])
                                weight = comb[:, tile(i), e:e + 1].rearrange("p a c -> p (a c)")
                                n = E * (BS + b) + e
                                if e >= 1:
                                    dve.wait_ge(added, TPS * n - 1 + t)
                                else:
                                    dve.wait_ge(staged, TPS * (BS + b) + TPS)
                                nc.vector.scalar_tensor_tensor(xs, b2[:, e, :], weight, xs, ALU.mult, ALU.add).then_inc(based, 1)
                            dve.wait_ge(projected, E * (BS + b) + e + 1)
                            for t in range(TPS):
                                i = TPS * b + t
                                xs = flat(x[:, tile(i), :])
                                weight = comb[:, tile(i), e:e + 1].rearrange("p a c -> p (a c)")
                                dve.wait_ge(based, TPS * (E * (BS + b) + e) + t + 1)
                                nc.vector.scalar_tensor_tensor(xs, bank[5 + e % 2][:, t * D:(t + 1) * D], weight, xs,
                                                               ALU.mult, ALU.add).then_inc(added, 1)
        leave_stream(core, saved)


def build(nc, dram, out, sublayers):
    with ExitStack() as ctx:
        core = Core(nc, dram, ctx)
        landed, stored = (ctx.enter_context(nc.semaphore(name)) for name in ("x_landed", "x_stored"))
        token_major = "s (t p) d -> p (s t) d"
        with nc.Block() as block:
            @block.sync
            def _(sp):
                sp.dma_start(core.x[:], dram["x"].rearrange(token_major, p=P)).then_inc(landed, 16)
                sp.dma_start(core.ident[:], dram["ident"]).then_inc(landed, 16)
                sp.wait_ge(landed, 32)

            @block.vector
            def _(dve):
                dve.wait_ge(landed, 32)
                nc.vector.tensor_copy(core.ident_bf[:], core.ident[:])
        for sublayer in sublayers:
            core.run(sublayer)
        with nc.Block() as block:
            @block.sync
            def _(sp):
                sp.dma_start(out.rearrange(token_major, p=P), core.x[:]).then_inc(stored, 16)
                sp.wait_ge(stored, 16)


def kernel(**inputs):
    import numpy as np
    import concourse.bacc as bacc
    from concourse.bass_utils import run_bass_kernel_spmd

    def rows(v):
        v = np.asarray(v).reshape(-1)
        return np.ascontiguousarray(np.broadcast_to(v[None, :], (P, v.size)))

    inputs = {k: np.asarray(v) for k, v in inputs.items()}
    arrays = {}
    arrays["x"] = inputs["L0_attn_embeddings"]
    arrays["ident"] = np.eye(P, dtype=np.float32)
    arrays["L0_wqkv"] = np.concatenate([inputs["L0_attn_Wq"], inputs["L0_attn_Wk"], inputs["L0_attn_Wv"]], 0).T
    arrays["L0_bqkv"] = rows(np.concatenate([inputs["L0_attn_bq"], inputs["L0_attn_bk"], inputs["L0_attn_bv"]]))
    arrays["L0_fc"] = inputs["L0_ffn_w_fc"]
    arrays["L0_proj"] = inputs["L0_ffn_w_proj"]
    arrays["L0_uT"] = inputs["L0_ffn_u"].T
    arrays["L0_v"] = inputs["L0_ffn_v"]
    arrays["L0_fbT"] = inputs["L0_ffn_fast_b"].T
    arrays["L0_gate"] = rows(inputs["L0_ffn_gate"])

    def heads_apart(w):
        w = w.reshape(-1, 4, 4, 8)
        out = np.zeros((w.shape[0], 4, 4, 32), np.float32)
        out[..., 0:8] = w
        return out.reshape(-1, 4, 128)

    arrays["L1_wq"] = inputs["L1_attn_Wq"]
    arrays["L1_wkv"] = np.concatenate([inputs["L1_attn_Wk"], inputs["L1_attn_Wv"]], 1)
    arrays["L1_wo"] = inputs["L1_attn_Wo"]
    arrays["L1_blocks"] = np.kron(np.eye(16), np.ones((8, 8))).astype(np.float32)
    arrays["L1_bq"] = inputs["L1_attn_bq"].reshape(D, 1)
    arrays["L1_bkv"] = rows(np.concatenate([inputs["L1_attn_bk"], inputs["L1_attn_bv"]]))
    arrays["L1_bo"] = rows(inputs["L1_attn_bo"])
    arrays["L1_gamma"] = rows(inputs["L1_attn_gamma"])
    arrays["L1_beta"] = rows(inputs["L1_attn_beta"])
    arrays["L1_fc"] = inputs["L1_ffn_W_fc"]
    arrays["L1_proj"] = inputs["L1_ffn_W_proj"]
    arrays["L1_ln_w"] = inputs["L1_ffn_ln_w"].reshape(4, P).T
    arrays["L1_ln_b"] = inputs["L1_ffn_ln_b"].reshape(4, P).T
    wqkv, bqkv = inputs["L2_attn_Wqkv"], inputs["L2_attn_bqkv"]
    arrays["L2_wq"] = heads_apart(wqkv[:, 0:D])
    arrays["L2_wk"] = heads_apart(wqkv[:, D:2 * D])
    arrays["L2_wv"] = wqkv[:, 2 * D:3 * D]
    arrays["L2_wo"] = inputs["L2_attn_Wout"]
    arrays["L2_bo"] = rows(inputs["L2_attn_bout"])
    arrays["L2_bv"] = rows(bqkv[2 * D:3 * D])
    arrays["L2_bq"] = heads_apart(bqkv[None, 0:D])[0].T
    arrays["L2_bk"] = heads_apart(bqkv[None, D:2 * D])[0].T
    pos = np.arange(LEN)
    arrays["L2_apart"] = np.abs(pos[:, None] - pos[None, :]).astype(np.float32).reshape(TPS, P, LEN).transpose(1, 0, 2)
    arrays["L2_slopes"] = rows(np.array([value for _, value in SLOPE_PARTS], np.float32))

    half = np.arange(0, HD2, 2, dtype=np.float32)
    freqs = pos.astype(np.float32)[:, None] * (1.0 / np.float32(10000.0) ** (half / np.float32(HD2)))[None, :]
    spread = (half + np.float32(0.4 * HD2)) / np.float32(1.4 * HD2)
    power = (pos.astype(np.float32) - LEN // 2) / np.float32(WINDOW // 2)
    scale = spread[None, :] ** power[:, None]
    freqs, scale = (np.concatenate([a, a], 1).astype(np.float32) for a in (freqs, scale))
    sign = np.where(np.arange(HD2) < HD2 // 2, -1.0, 1.0).astype(np.float32)
    qk_factor = 8.0
    one = np.array([[np.cos(freqs) * scale * qk_factor, np.cos(freqs) / scale],
                    [np.sin(freqs) * scale * sign * qk_factor, np.sin(freqs) / scale * sign]], np.float32)
    arrays["r_tables"] = np.concatenate([one, one], 3).transpose(3, 0, 1, 2)
    key = np.arange(WINDOW_KEYS)[None, :] - WINDOW
    query = np.arange(P)[:, None]
    seen = (key <= query) & (query <= key + WINDOW)
    arrays["r_masks"] = np.stack([np.where(seen & (key >= 0), 0.0, -1e30), np.where(seen, 0.0, -1e30)], 1).astype(np.float32)
    arrays["r_head_ones"] = np.kron(np.eye(2), np.ones((HD2, 1))).astype(np.float32)
    swap = (np.arange(HD2) + HD2 // 2) % HD2
    w = inputs["L2_ffn_Wqkv"].reshape(-1, D, 3, HEADS2, HD2)
    arrays["r_w"] = np.stack([w[:, :, 0], w[:, :, 0][..., swap], w[:, :, 1], w[:, :, 1][..., swap], w[:, :, 2]], 2)\
        .reshape(-1, D, 5 * HEADS2 * HD2)
    arrays["r_wo"] = inputs["L2_ffn_Wo"].reshape(-1, PAIRS2, P, D).transpose(0, 2, 1, 3).reshape(-1, P, PAIRS2 * D)
    qs, ks = inputs["L2_ffn_q_scale"], inputs["L2_ffn_k_scale"]
    scales = np.stack([qs, ks, qs[:, swap], ks[:, swap]], 2)
    arrays["r_qk_scale"] = np.concatenate([scales, scales], 1)
    w1, b1, w2 = inputs["L2_ffn_W1"], inputs["L2_ffn_b1"], inputs["L2_ffn_W2"]
    depth, width = w1.shape[0], w2.shape[1]
    filled = 3 * P
    w1p, b1p, w2p = (np.zeros(s, np.float32) for s in ((depth, D, 2, filled), (depth, 2, filled), (depth, filled, D)))
    w1p[..., 0:width] = w1.reshape(depth, D, 2, width)
    b1p[..., 0:width] = b1.reshape(depth, 2, width)
    w2p[:, 0:width] = w2
    arrays["g_w1"] = w1p.reshape(depth, D, 2 * filled)
    arrays["g_b1"] = b1p.reshape(depth, 6, P).transpose(0, 2, 1)
    arrays["g_w2"] = w2p.reshape(depth, 3, P, D).transpose(0, 2, 1, 3).reshape(depth, P, 3 * D)
    arrays["g_b2"] = np.broadcast_to(inputs["L2_ffn_b2"][:, None, :], (depth, P, D))
    arrays["g_ln_g"] = inputs["L2_ffn_ln_g"][:, :, None]
    arrays["g_ln_b"] = inputs["L2_ffn_ln_b"][:, :, None]
    for name in ("r_w", "r_wo", "r_qk_scale"):
        arrays[name] = np.concatenate([arrays[name], arrays[name][0:1]], 0)
    arrays["L3_wqkv"] = inputs["L3_attn_W_qkv"].T
    arrays["L3_bqk"] = inputs["L3_attn_b_qkv"][0:2 * D].reshape(2, D).T
    arrays["L3_bv"] = rows(inputs["L3_attn_b_qkv"][2 * D:])
    gap = (pos[None, :] - pos[:, None]).astype(np.float32)
    decay = (np.where(gap >= 0, np.float32(0.99) ** gap, 0.0) / np.sqrt(np.float32(D))).astype(np.float32)
    arrays["L3_decay"] = np.stack([decay[0:P, 0:P], decay[0:P, P:LEN], decay[P:LEN, P:LEN]], 1)
    layers = inputs["L3_ffn_w1"].shape[0]
    arrays["m_w1"] = inputs["L3_ffn_w1"].transpose(0, 2, 1, 3).reshape(layers, D, 4 * 512)
    arrays["m_w2"] = inputs["L3_ffn_w2"].reshape(layers, 16, P, D).transpose(0, 2, 1, 3).reshape(layers, P, 16 * D)
    arrays["m_g"] = inputs["L3_ffn_ln_g"].transpose(0, 2, 1)
    arrays["m_b_ln"] = inputs["L3_ffn_ln_b"].transpose(0, 2, 1)
    arrays["m_b1"] = inputs["L3_ffn_b1"].reshape(layers, 16, P).transpose(0, 2, 1)
    arrays["m_b2"] = np.broadcast_to(inputs["L3_ffn_b2"].reshape(layers, 1, 4 * D), (layers, P, 4 * D))
    arrays["m_rw"] = inputs["L3_ffn_router_w"]
    arrays["m_rb"] = np.broadcast_to(inputs["L3_ffn_router_b"][:, None, :], (layers, P, 4))
    arrays["m_earlier"] = rows(np.tril(np.ones((4, 4), np.float32), -1))
    nc = bacc.Bacc("TRN2", target_bir_lowering=False, num_devices=1)
    arrays = {f"in_{k}": np.ascontiguousarray(v) for k, v in arrays.items()}
    dram = {k[3:]: nc.dram_tensor(k, v.shape, F32, kind="ExternalInput").ap() for k, v in arrays.items()}
    out = nc.dram_tensor("out_x", (SEQS, LEN, D), F32, kind="ExternalOutput").ap()
    build(nc, dram, out, [l0_attention, l0_feedforward, l1_attention, l1_feedforward, l2_attention, l2_feedforward, l3_attention, l3_feedforward])
    result = run_bass_kernel_spmd(nc, [arrays], core_ids=[0])
    return result.results[0]["out_x"]
```

```python
import math
from contextlib import ExitStack

import concourse.bass as bass
from concourse import mybir

F32 = mybir.dt.float32
BF16 = mybir.dt.bfloat16
ALU = mybir.AluOpType
ACT = mybir.ActivationFunctionType
AX = mybir.AxisListType

P = 128
D = 128
SEQS = 16
LEN = 256
TPS = LEN // P
TILES = SEQS * TPS
LN_EPS = 1e-5


def slope_parts(heads=16):
    import numpy as np
    out = []
    for h in range(heads):
        rest = np.float32((2.0 ** (-2.0 ** (-(math.log2(heads) - 3)))) ** h)
        while rest:
            bits = np.array([rest], np.float32).view(np.uint32)
            bits = (bits + np.uint32(0x7FFF) + ((bits >> np.uint32(16)) & np.uint32(1))) & np.uint32(0xFFFF0000)
            part = bits.view(np.float32)[0]
            out.append((h, -float(part)))
            rest = np.float32(rest - part)
    return out


SLOPE_PARTS = slope_parts()


class Core:

    def __init__(self, nc, dram, ctx):
        self.nc = nc
        self.dram = dram
        self.ctx = ctx
        self.x = self.sb("x", [P, TILES, D])
        self.ident = self.sb("ident", [P, P])
        self.ident_bf = self.sb("ident_bf", [P, P], BF16)
        self.mean = self.sb("mean", [P, TILES])
        self.rstd = self.sb("rstd", [P, TILES])
        self.banks = ctx.enter_context(nc.psum_tensor("banks", [P, 8, 512], F32))
        self.passed = ctx.enter_context(nc.semaphore("passed"))
        self.bank = [self.banks[:, i, :] for i in range(8)]

    def sb(self, name, shape, dt=F32):
        return self.ctx.enter_context(self.nc.sbuf_tensor(name, shape, dt))

    def sem(self, name):
        handle = self.sublayer.enter_context(self.nc.semaphore(name))
        self.sems.append(handle)
        return handle

    def run(self, sublayer):
        nc = self.nc
        with ExitStack() as self.sublayer:
            self.sems = []
            sublayer(self)
            with nc.Block() as block:
                @block.gpsimd
                def _(pool):
                    for handle in self.sems:
                        nc.gpsimd.sem_clear(handle)


class Chain:

    def __init__(self, eng, sem, base=0):
        self.eng, self.sem, self.base, self.n = eng, sem, base, 0

    def __call__(self, instruction):
        self.n += 1
        instruction.then_inc(self.sem, 1)
        self.eng.wait_ge(self.sem, self.base + self.n)


def scratch(core, stack):
    def sb(name, shape, dt=F32):
        return stack.enter_context(core.nc.sbuf_tensor(name, shape, dt))
    return sb, core.sem


def load_block(core, name, loads):
    nc = core.nc
    landed = core.sem(f"{name}_landed")
    with nc.Block() as block:
        @block.sync
        def _(sp):
            for dst, src in loads:
                sp.dma_start(dst, src).then_inc(landed, 16)
            sp.wait_ge(landed, 16 * len(loads))


def load_layer(core, name, loads, layer):
    nc = core.nc
    landed = core.sem(f"{name}_landed")
    with nc.Block() as block:
        @block.sync
        def _(sp):
            for dst, src in loads:
                sp.dma_start(dst, src).then_inc(landed, 16)
            sp.wait_ge(landed, layer * (16 * len(loads)) + 16 * len(loads))
            sp.sem_inc(core.passed, 1)


def stats_block(core, name, src, eps, layer=None, width=D, beside=None):
    nc = core.nc
    U = 4
    with ExitStack() as stack:
        sb, sem = scratch(core, stack)
        raw = sb(f"{name}_raw", [P, TILES, 6])
        eps_col = sb(f"{name}_eps", [P, 1])
        gap = sb(f"{name}_gap", [P, TILES])
        var = sb(f"{name}_var", [P, TILES])
        std = sb(f"{name}_std", [P, TILES])
        gathered, merged, eps_set, rooted = (sem(f"{name}_{n}") for n in ("gathered", "merged", "eps_set", "rooted"))
        n = 0 if layer is None else layer
        MERGES = 5
        with nc.Block() as block:
            if beside:
                @block.tensor
                def _(pe):
                    beside[0](pe)

            @block.vector
            def _(dve):
                if beside:
                    beside[2](dve)
                nc.vector.memset(eps_col[:], eps).then_inc(eps_set, 1)
                with dve.Fori(0, TILES // U) as i:
                    for k in range(U):
                        nc.vector.bn_stats(flat(raw[:, tile(U * i + k), :]), flat(src[:, tile(U * i + k), :])).then_inc(gathered, 1)
                dve.wait_ge(gathered, n * TILES + TILES)
                then = Chain(dve, merged, n * MERGES)
                nc.vector.tensor_tensor(core.mean[:], raw[:, :, 1], raw[:, :, 4], ALU.add)
                nc.vector.tensor_tensor(var[:], raw[:, :, 2], raw[:, :, 5], ALU.add)
                then(nc.vector.tensor_tensor(gap[:], raw[:, :, 1], raw[:, :, 4], ALU.subtract))
                then(nc.vector.tensor_tensor(gap[:], gap[:], gap[:], ALU.mult))
                then(nc.vector.tensor_scalar(gap[:], gap[:], 0.25, None, ALU.mult))
                then(nc.vector.scalar_tensor_tensor(var[:], var[:], 1.0 / width, gap[:], ALU.mult, ALU.add))
                then(nc.vector.tensor_scalar(core.mean[:], core.mean[:], 0.5, None, ALU.mult))
                dve.wait_ge(rooted, n + 1)
                nc.vector.reciprocal(core.rstd[:], std[:])

            @block.scalar
            def _(act):
                if beside:
                    beside[1](act)
                act.wait_ge(eps_set, n + 1)
                act.wait_ge(merged, n * MERGES + MERGES)
                nc.scalar.activation(std[:], var[:], ACT.Sqrt, bias=eps_col[:]).then_inc(rooted, 1)


def tile(t, k=1):
    return bass.ds(t, k)


def flat(ap):
    return ap.rearrange("p a d -> p (a d)")


def over_turns(eng, turn):
    turn(-1, 1, before=False, now=False, following=True, again=False)
    turn(0, 0, before=False, now=True, following=True, again=False)
    turn(1, 1, before=True, now=True, following=True, again=False)
    with eng.Fori(0, (SEQS - 4) // 2) as i:
        for n in range(2):
            turn(2 * i + 2 + n, n, before=True, now=True, following=True, again=True)
    turn(SEQS - 2, 0, before=True, now=True, following=True, again=True)
    turn(SEQS - 1, 1, before=True, now=True, following=False, again=True)
    turn(SEQS, 0, before=True, now=False, following=False, again=True)


def l0_attention(core):
    nc, x, bank, dram = core.nc, core.x, core.bank, core.dram
    HD = 8
    SCALE = float(D) ** -0.5
    PAIRS = [(0, 0), (0, 1), (1, 0), (1, 1), (0, 2), (2, 0), (1, 2), (2, 1)]
    KQ = HD * len(PAIRS)
    with ExitStack() as stack:
        sb, sem = scratch(core, stack)
        w = sb("a0_w", [D, 3 * HD])
        bias = sb("a0_bias", [P, 3 * HD])
        load_block(core, "a0", [(w[:], dram["L0_wqkv"]), (bias[:], dram["L0_bqkv"])])
        stats_block(core, "a0s", x, LN_EPS)

        stage = sb("a0_stage", [P, TPS, D])
        xT = sb("a0_xT", [D, LEN])
        qkv = sb("a0_qkv", [P, TILES, 3 * HD])
        VC = 32
        v1 = sb("a0_v1", [P, TILES, VC])
        staged, turned, xT_ready, projected, biased = (sem("a0_" + n) for n in
                                                       ("staged", "turned", "xT_ready", "projected", "biased"))
        with nc.Block() as block:
            @block.vector
            def _(dve):
                with dve.Fori(0, SEQS) as b:
                    for t in range(TPS):
                        i = 2 * b + t
                        nc.vector.tensor_scalar(stage[:, t, :], flat(x[:, tile(i), :]), core.mean[:, tile(i)],
                                                core.rstd[:, tile(i)], ALU.subtract, ALU.mult).then_inc(staged, 1)
                    dve.wait_ge(projected, b + 1)
                    nc.vector.tensor_tensor(qkv[:, tile(2 * b, 2), :],
                                            bank[1][:, 0:2 * 3 * HD].rearrange("p (t c) -> p t c", t=TPS),
                                            bias[:, None, :].to_broadcast([P, TPS, 3 * HD]), ALU.add).then_inc(biased, 1)

            @block.tensor
            def _(pe):
                with pe.Fori(0, SEQS) as b:
                    pe.wait_ge(staged, 2 * b + 2)
                    for t in range(TPS):
                        mm = pe.transpose(bank[0][:, t * P:(t + 1) * P], stage[:, t, :], core.ident[:])
                    mm.then_inc(turned, 1)
                    pe.wait_ge(xT_ready, b + 1)
                    for t in range(TPS):
                        mm = pe.matmul(bank[1][:, t * 3 * HD:(t + 1) * 3 * HD], xT[:, t * P:(t + 1) * P], w[:],
                                       start=True, stop=True)
                    mm.then_inc(projected, 1)

            @block.scalar
            def _(act):
                with act.Fori(0, SEQS) as b:
                    act.wait_ge(turned, b + 1)
                    nc.scalar.copy(xT[:], bank[0][:, 0:LEN]).then_inc(xT_ready, 1)

        parts = sb("a0_parts", [P, 3, TILES, 2 * HD], BF16)
        rest = sb("a0_rest", [P, 2, TILES, 2 * HD])
        q_rows = sb("a0_q_rows", [P, TILES, P], BF16)
        k_rows = sb("a0_k_rows", [P, TILES, P], BF16)
        split, laid = sem("a0_split"), sem("a0_laid")
        with nc.Block() as block:
            @block.vector
            def _(dve):
                then = Chain(dve, split)
                qk = qkv[:, :, 0:2 * HD]
                then(nc.vector.tensor_copy(parts[:, 0], qk))
                then(nc.vector.tensor_tensor(rest[:, 0], qk, parts[:, 0], ALU.subtract))
                then(nc.vector.tensor_copy(parts[:, 1], rest[:, 0]))
                then(nc.vector.tensor_tensor(rest[:, 1], rest[:, 0], parts[:, 1], ALU.subtract))
                then(nc.vector.tensor_copy(parts[:, 2], rest[:, 1]))
                nc.vector.memset(v1[:, :, HD:HD + 1], 1.0)
                nc.vector.memset(v1[:, :, HD + 1:VC], 0.0)
                nc.vector.tensor_copy(v1[:, :, 0:HD], qkv[:, :, 2 * HD:3 * HD])
                nc.vector.memset(q_rows[:, :, KQ:P], 0.0)
                nc.vector.memset(k_rows[:, :, KQ:P], 1.0)
                for n, (a, b) in enumerate(PAIRS):
                    nc.vector.tensor_copy(q_rows[:, :, n * HD:(n + 1) * HD], parts[:, a, :, 0:HD])
                    nc.vector.tensor_copy(k_rows[:, :, n * HD:(n + 1) * HD], parts[:, b, :, HD:2 * HD])

        qT = sb("a0_qT", [P, TILES, P], BF16)
        kT = sb("a0_kT", [P, TILES, P], BF16)

        def turn_rows(name, jobs):
            G = 8
            turned_g, copied = sem(f"a0_turned_{name}"), sem(f"a0_copied_{name}")
            steps = [(dst, src, g) for dst, src in jobs for g in range(TILES // G)]
            with nc.Block() as block:
                @block.tensor
                def _(pe):
                    for n, (dst, src, g) in enumerate(steps):
                        if n >= 2:
                            pe.wait_ge(copied, n - 1)
                        out = bank[n % 2].bitcast(BF16)
                        for k in range(G):
                            mm = pe.transpose(out[:, k * P:(k + 1) * P], src[:, g * G + k, :], core.ident_bf[:])
                        mm.then_inc(turned_g, 1)

                @block.vector
                def _(dve):
                    for n, (dst, src, g) in enumerate(steps):
                        dve.wait_ge(turned_g, n + 1)
                        nc.vector.tensor_copy(flat(dst[:, g * G:(g + 1) * G, :]), bank[n % 2].bitcast(BF16)).then_inc(copied, 1)

        turn_rows("qk", [(qT, q_rows), (kT, k_rows)])

        top = sb("a0_top", [P, TILES, 2])
        scored, halved = sem("a0_scored"), sem("a0_halved")
        HALF = TILES * P // 2
        with nc.Block() as block:
            @block.tensor
            def _(pe):
                with pe.Fori(0, TILES) as t:
                    for h in range(2):
                        pe.wait_ge(halved, 2 * t + h + 1)
                        for c in range(4):
                            mm = pe.matmul(bank[4 * h + c], flat(qT[:, tile(t), :]),
                                           kT[:, 16 * h + 4 * c:16 * h + 4 * c + 4, :].rearrange("p a d -> p (a d)"),
                                           start=True, stop=True)
                        mm.then_inc(scored, 1)

            @block.vector
            def _(dve):
                dve.sem_inc(halved, 2)
                with dve.Fori(0, TILES) as t:
                    for h in range(2):
                        dve.wait_ge(scored, 2 * t + h + 1)
                        nc.vector.tensor_reduce(top[:, tile(t), h:h + 1].rearrange("p a c -> p (a c)"),
                                                core.banks[:, 4 * h:4 * h + 4, :], AX.XY, ALU.max).then_inc(halved, 1)

        low = sb("a0_low", [P, 3, TILES])
        cut = sem("a0_cut")
        with nc.Block() as block:
            @block.vector
            def _(dve):
                then = Chain(dve, cut)
                m = [q_rows[:, :, KQ + c:KQ + c + 1].rearrange("p t a -> p (t a)") for c in range(3)]
                then(nc.vector.tensor_tensor(low[:, 0], top[:, :, 0], top[:, :, 1], ALU.max))
                then(nc.vector.tensor_scalar(low[:, 0], low[:, 0], -1.0, None, ALU.mult))
                then(nc.vector.tensor_copy(m[0], low[:, 0]))
                then(nc.vector.tensor_tensor(low[:, 1], low[:, 0], m[0], ALU.subtract))
                then(nc.vector.tensor_copy(m[1], low[:, 1]))
                then(nc.vector.tensor_tensor(low[:, 2], low[:, 1], m[1], ALU.subtract))
                nc.vector.tensor_copy(m[2], low[:, 2])

        turn_rows("m", [(qT, q_rows)])

        QC = 4
        CHUNKS = TILES // QC
        KPAIRS = TILES // 2
        expd = sb("a0_expd", [P, 2, 2, QC * P])
        accT = sb("a0_accT", [VC, QC * P])
        inv = sb("a0_inv", [P, QC])
        y = sb("a0_y", [P, QC, HD])
        paired, expd_ready, expd_used, sums_read, sums_turned, inverted, y_ready = (
            sem("a0_" + n) for n in ("paired", "expd_ready", "expd_used", "sums_read", "sums_turned", "inverted", "y_ready"))
        acc = bank[5][:, 0:QC * VC].rearrange("p (s c) -> p s c", s=QC)
        with nc.Block() as block:
            @block.tensor
            def _(pe):
                def scores(c, j):
                    pe.wait_ge(expd_ready, c * KPAIRS + j + 1)
                    for h in range(2):
                        mm = pe.matmul(bank[2 * (j % 2) + h], kT[:, 2 * j + h, :],
                                       qT[:, tile(c * QC, QC), :].rearrange("p a d -> p (a d)"), start=True, stop=True)
                    mm.then_inc(paired, 1)

                def sums(c, j):
                    pe.wait_ge(expd_ready, c * KPAIRS + j + 3)
                    for h in range(2):
                        mm = pe.matmul(bank[4][0:VC, :], v1[:, 2 * j + h, :], expd[:, j % 2, h, :],
                                       start=j == 0 and h == 0, stop=j == KPAIRS - 1 and h == 1)
                    mm.then_inc(expd_used, 1)

                with pe.Fori(0, CHUNKS) as c:
                    for j in range(KPAIRS + 1):
                        if j < KPAIRS:
                            scores(c, j)
                        if j == 1:
                            pe.wait_ge(sums_read, c + 1)
                        if j >= 1:
                            sums(c, j - 1)
                    pe.wait_ge(sums_read, c + 2)
                    pe.sem_inc(core.passed, 1)
                    for s in range(QC):
                        mm = pe.transpose(acc[:, s, :], accT[:, s * P:(s + 1) * P], core.ident[0:VC, 0:VC])
                    mm.then_inc(sums_turned, 1)

            @block.scalar
            def _(act):
                act.sem_inc(expd_ready, 2)
                with act.Fori(0, CHUNKS) as c:
                    for j in range(KPAIRS):
                        n = c * KPAIRS + j
                        act.wait_ge(paired, n + 1)
                        act.wait_ge(expd_used, n + 1)
                        nc.scalar.activation(expd[:, j % 2], core.banks[:, 2 * (j % 2):2 * (j % 2) + 2, :], ACT.Exp, scale=SCALE)\
                            .then_inc(expd_ready, 1)

            @block.vector
            def _(dve):
                dve.sem_inc(sums_read, 1)
                dve.sem_inc(expd_used, 2)
                with dve.Fori(0, CHUNKS) as c:
                    dve.wait_ge(expd_used, c * KPAIRS + KPAIRS + 2)
                    nc.vector.tensor_copy(accT[:], bank[4][0:VC, :]).then_inc(sums_read, 1)
                    dve.wait_ge(sums_turned, c + 1)
                    nc.vector.reciprocal(inv[:], acc[:, :, HD]).then_inc(inverted, 1)
                    dve.wait_ge(inverted, c + 1)
                    nc.vector.tensor_tensor(y[:], acc[:, :, 0:HD], inv[:, :, None].to_broadcast([P, QC, HD]), ALU.mult)\
                        .then_inc(y_ready, 1)
                    dve.wait_ge(y_ready, c + 1)
                    for s in range(QC):
                        xs = flat(x[:, tile(c * QC + s), :]).rearrange("p (r f) -> p r f", f=HD)
                        nc.vector.tensor_tensor(xs, xs, y[:, s, None, :].to_broadcast([P, D // HD, HD]), ALU.add)


def l0_feedforward(core):
    nc, x, bank, dram = core.nc, core.x, core.bank, core.dram
    H = 512
    C = H // P
    R = 16
    with ExitStack() as stack:
        sb, sem = scratch(core, stack)
        fc = sb("f0_fc", [P, C, D])
        proj = sb("f0_proj", [P, H])
        uT = sb("f0_uT", [R, H])
        v = sb("f0_v", [R, D])
        fbT = sb("f0_fbT", [R, R])
        gate = sb("f0_gate", [P, 1])
        load_block(core, "f0", [(fc[:], dram["L0_fc"].rearrange("(c p) d -> p c d", p=P)), (proj[:], dram["L0_proj"]),
                                (uT[:], dram["L0_uT"]), (v[:], dram["L0_v"]), (fbT[:], dram["L0_fbT"]), (gate[:], dram["L0_gate"])])
        stats_block(core, "f0s", x, LN_EPS)

        w1 = sb("f0_w1", [D, H])
        w2 = sb("f0_w2", [P, C, D])
        fbv = sb("f0_fbv", [R, D])
        scale = sb("f0_scale", [P, C + 1])
        edge = sb("f0_edge", [P, 2, C + 1])
        tern = sb("f0_tern", [P, 2, C, D])
        below = sb("f0_below", [P, 2, C, D])
        made, small, turned = sem("f0_made"), sem("f0_small"), sem("f0_turned")
        with nc.Block() as block:
            @block.vector
            def _(dve):
                then = Chain(dve, made)
                then(nc.vector.tensor_reduce(scale[:, 0:C], fc[:], AX.X, ALU.add, apply_absolute_value=True))
                then(nc.vector.tensor_reduce(scale[:, C:C + 1], proj[:], AX.X, ALU.add, apply_absolute_value=True))
                then(nc.vector.tensor_scalar(scale[:, 0:C], scale[:, 0:C], 1.0 / D, 1e-5, ALU.mult, ALU.max))
                then(nc.vector.tensor_scalar(scale[:, C:C + 1], scale[:, C:C + 1], 1.0 / H, 1e-5, ALU.mult, ALU.max))
                then(nc.vector.tensor_scalar(edge[:, 0], scale[:], 0.5, None, ALU.mult))
                then(nc.vector.tensor_scalar(edge[:, 1], scale[:], -0.5, None, ALU.mult))
                for c in range(C):
                    for m, src, e in ((0, fc[:, c, :], c), (1, proj[:, c * P:(c + 1) * P], C)):
                        then(nc.vector.tensor_scalar(below[:, m, c], src, edge[:, 1, e:e + 1], None, ALU.is_lt))
                        then(nc.vector.scalar_tensor_tensor(tern[:, m, c], src, edge[:, 0, e:e + 1], below[:, m, c],
                                                            ALU.is_gt, ALU.subtract))
                        then(nc.vector.tensor_scalar(tern[:, m, c], tern[:, m, c], scale[:, e:e + 1], None, ALU.mult))
                dve.wait_ge(small, 1)
                then(nc.vector.tensor_copy(fbv[:], bank[0][0:R, 0:D]))
                dve.wait_ge(small, 2)
                then(nc.vector.scalar_tensor_tensor(tern[:, 0], bank[1].rearrange("p (c d) -> p c d", c=C), gate[:, 0:1],
                                                    tern[:, 0], ALU.mult, ALU.add))
                dve.wait_ge(turned, 1)
                then(nc.vector.tensor_copy(w1[:], bank[2]))
                then(nc.vector.tensor_copy(w2[:].rearrange("p c d -> p (c d)"), bank[3]))

            @block.tensor
            def _(pe):
                pe.matmul(bank[0][0:R, 0:D], fbT[:], v[:], start=True, stop=True).then_inc(small, 1)
                FBV = 6 + 3 * 2 * C + 1
                pe.wait_ge(made, FBV)
                for c in range(C):
                    mm = pe.matmul(bank[1][:, c * D:(c + 1) * D], uT[:, c * P:(c + 1) * P], fbv[:], start=True, stop=True)
                mm.then_inc(small, 1)
                pe.wait_ge(made, FBV + 1)
                for c in range(C):
                    pe.transpose(bank[2][:, c * P:(c + 1) * P], tern[:, 0, c, :], core.ident[:])
                    mm = pe.transpose(bank[3][:, c * P:(c + 1) * P], tern[:, 1, c, :], core.ident[:])
                mm.then_inc(turned, 1)

        stage = sb("f0_stage", [P, TPS, D])
        xT = sb("f0_xT", [D, LEN])
        relu = sb("f0_relu", [P, 2, C * LEN])
        hid = sb("f0_hid", [P, 2, C, LEN])
        staged, turned_x, xT_ready, hidden, clipped, squared, projected, added = (
            sem("f0_" + n) for n in ("staged", "turned_x", "xT_ready", "hidden", "clipped", "squared", "projected", "added"))

        with nc.Block() as block:
            @block.vector
            def _(dve):
                def turn(b, half, before, now, following, again):
                    if following:
                        if now:
                            dve.wait_ge(turned_x, b + 1)
                        for t in range(TPS):
                            i = TPS * (b + 1) + t
                            nc.vector.tensor_scalar(stage[:, t, :], flat(x[:, tile(i), :]), core.mean[:, tile(i)],
                                                    core.rstd[:, tile(i)], ALU.subtract, ALU.mult).then_inc(staged, 1)
                    if now:
                        dve.wait_ge(clipped, b + 1)
                        nc.vector.tensor_tensor(hid[:, half].rearrange("p c t -> p (c t)"), relu[:, half], relu[:, half], ALU.mult)\
                            .then_inc(squared, 1)
                    if before:
                        dve.wait_ge(projected, b)
                        xs = x[:, tile(TPS * (b - 1), TPS), :]
                        nc.vector.tensor_tensor(xs, xs, bank[4][:, 0:LEN].rearrange("p (t d) -> p t d", t=TPS), ALU.add)\
                            .then_inc(added, 1)

                over_turns(dve, turn)

            @block.tensor
            def _(pe):
                def turn(b, half, before, now, following, again):
                    if now:
                        pe.wait_ge(xT_ready, b + 1)
                        for c in range(C):
                            mm = pe.matmul(bank[2 + 3 * half + c // 2][:, (c % 2) * LEN:(c % 2 + 1) * LEN],
                                           w1[:, c * P:(c + 1) * P], xT[:], start=True, stop=True)
                        mm.then_inc(hidden, 1)
                    if following:
                        pe.wait_ge(staged, TPS * b + 2 * TPS)
                        for t in range(TPS):
                            mm = pe.transpose(bank[0][:, t * P:(t + 1) * P], stage[:, t, :], core.ident[:])
                        mm.then_inc(turned_x, 1)
                    if before:
                        pe.wait_ge(squared, b)
                        if again:
                            pe.wait_ge(added, b - 1)
                        for t in range(TPS):
                            for c in range(C):
                                mm = pe.matmul(bank[4][:, t * D:(t + 1) * D], hid[:, 1 - half, c, t * P:(t + 1) * P], w2[:, c, :],
                                               start=c == 0, stop=c == C - 1)
                        mm.then_inc(projected, 1)

                over_turns(pe, turn)

            @block.scalar
            def _(act):
                def turn(b, half, before, now, following, again):
                    if now:
                        act.wait_ge(hidden, b + 1)
                        nc.scalar.activation(relu[:, half].rearrange("p (a f) -> p a f", a=2),
                                             core.banks[:, 2 + 3 * half:4 + 3 * half, :], ACT.Relu).then_inc(clipped, 1)
                    if following:
                        act.wait_ge(turned_x, b + 2)
                        nc.scalar.copy(xT[:], bank[0][:, 0:LEN]).then_inc(xT_ready, 1)

                over_turns(act, turn)


def put_normalized(core, dve, b, stage, staged):
    nc = core.nc
    for t in range(TPS):
        i = TPS * b + t
        nc.vector.tensor_scalar(stage[:, t, :], flat(core.x[:, tile(i), :]), core.mean[:, tile(i)], core.rstd[:, tile(i)],
                                ALU.subtract, ALU.mult).then_inc(staged, 1)


def enter_stream(core, name, saved):
    nc = core.nc
    stats_block(core, name, core.x, LN_EPS)
    kept = core.sem(f"{name}_kept")
    with nc.Block() as block:
        @block.vector
        def _(dve):
            nc.vector.tensor_copy(saved[:], core.x[:]).then_inc(kept, 1)
            dve.wait_ge(kept, 1)
            for t in range(TILES):
                nc.vector.tensor_scalar(core.x[:, t, :], saved[:, t, :], core.mean[:, t:t + 1], core.rstd[:, t:t + 1],
                                        ALU.subtract, ALU.mult)


def leave_stream(core, saved):
    nc = core.nc
    with nc.Block() as block:
        @block.vector
        def _(dve):
            nc.vector.tensor_tensor(core.x[:], core.x[:], saved[:], ALU.add)


def l1_attention(core):
    nc, x, bank, dram = core.nc, core.x, core.bank, core.dram
    HEADS, HD = 16, 8
    EPS = 1e-6
    with ExitStack() as stack:
        sb, sem = scratch(core, stack)
        wq, wkv, wo, blocks = sb("a1_wq", [D, D]), sb("a1_wkv", [D, 2 * D]), sb("a1_wo", [D, D]), sb("a1_blocks", [D, D])
        bq, bkv, bo = sb("a1_bq", [D, 1]), sb("a1_bkv", [P, 2 * D]), sb("a1_bo", [P, D])
        gamma, beta = sb("a1_gamma", [P, D]), sb("a1_beta", [P, D])
        load_block(core, "a1", [(wq[:], dram["L1_wq"]), (wkv[:], dram["L1_wkv"]), (wo[:], dram["L1_wo"]),
                                (blocks[:], dram["L1_blocks"]), (bq[:], dram["L1_bq"]), (bkv[:], dram["L1_bkv"]),
                                (bo[:], dram["L1_bo"]), (gamma[:], dram["L1_gamma"]), (beta[:], dram["L1_beta"])])
        stats_block(core, "a1s", x, LN_EPS)
        stage = sb("a1_stage", [P, TPS, D])
        xT = sb("a1_xT", [D, LEN])
        q_raw, q_exp, q_lin = (sb("a1_" + n, [D, LEN]) for n in ("q_raw", "q_exp", "q_lin"))
        q, kv, k = sb("a1_q", [D, 2, LEN]), sb("a1_kv", [P, 2, TPS, 2 * D]), sb("a1_k", [P, 2, TPS, D])
        k_exp, k_lin, k_sq = (sb("a1_" + n, [P, TPS, D]) for n in ("k_exp", "k_lin", "k_sq"))
        k_sum, k_norm, k_inv = (sb("a1_" + n, [P, TPS * HEADS]) for n in ("k_sum", "k_norm", "k_inv"))
        vk, m = sb("a1_vk", [D, D]), sb("a1_m", [D, D])
        y = sb("a1_y", [P, TPS, D])
        raw, mv, std, inv = sb("a1_raw", [P, TPS, 6]), sb("a1_mv", [P, TPS, 2]), sb("a1_std", [P, TPS]), sb("a1_inv", [P, TPS])
        eps_col = sb("a1_eps_col", [P, 1])
        (eps_set, staged, turned, xT_ready, q_made, q_biased, kv_made, q_exp_ready, kv_ready, k_exp_ready, k_summed, k_rooted,
         q_ready, k_ready, vk_made, vk_ready, m_made, m_ready, y_made, y_varied, y_rooted, k_chain, y_chain) = (
            sem("a1_" + n) for n in (
                "eps_set", "staged", "turned", "xT_ready", "q_made", "q_biased", "kv_made", "q_exp_ready", "kv_ready", "k_exp_ready",
                "k_summed", "k_rooted", "q_ready", "k_ready", "vk_made", "vk_ready", "m_made", "m_ready", "y_made",
                "y_varied", "y_rooted", "k_chain", "y_chain"))
        K_STEPS, Y_STEPS = 5, 8
        with nc.Block() as block:
            @block.vector
            def _(dve):
                nc.vector.memset(eps_col[:], EPS).then_inc(eps_set, 1)

                def turn(b, half, before, now, following, again):
                    then = Chain(dve, k_chain, b * K_STEPS)
                    if following:
                        if now:
                            dve.wait_ge(turned, b + 1)
                        put_normalized(core, dve, b + 1, stage, staged)
                    if now:
                        dve.wait_ge(q_made, b + 1)
                        nc.vector.tensor_scalar(q_raw[:], bank[1][:, 0:LEN], bq[:, 0:1], None, ALU.add).then_inc(q_biased, 1)
                        dve.wait_ge(kv_made, b + 1)
                        nc.vector.tensor_tensor(kv[:, half], bank[2].rearrange("p (t c) -> p t c", t=TPS),
                                                bkv[:, None, :].to_broadcast([P, TPS, 2 * D]), ALU.add).then_inc(kv_ready, 1)
                    if before:
                        dve.wait_ge(vk_made, b)
                        nc.vector.tensor_tensor(vk[:], bank[3][:, 0:D], blocks[:], ALU.mult).then_inc(vk_ready, 1)
                    if now:
                        dve.wait_ge(q_biased, b + 1)
                        then(nc.vector.tensor_scalar(q_lin[:], q_raw[:], 0.0, None, ALU.max))
                        dve.wait_ge(q_exp_ready, b + 1)
                        nc.vector.scalar_tensor_tensor(q[:, half], q_exp[:], 1.0, q_lin[:], ALU.min, ALU.add).then_inc(q_ready, 1)
                        dve.wait_ge(kv_ready, b + 1)
                        then(nc.vector.tensor_scalar(k_lin[:], kv[:, half, :, 0:D], 0.0, None, ALU.max))
                        dve.wait_ge(k_exp_ready, b + 1)
                        then(nc.vector.scalar_tensor_tensor(k_lin[:], k_exp[:], 1.0, k_lin[:], ALU.min, ALU.add))
                        then(nc.vector.tensor_tensor(k_sq[:], k_lin[:], k_lin[:], ALU.mult))
                        nc.vector.tensor_reduce(k_sum[:], k_sq[:].rearrange("p t (h f) -> p (t h) f", f=HD), AX.X, ALU.add)\
                            .then_inc(k_summed, 1)
                    if before:
                        then_y = Chain(dve, y_chain, (b - 1) * Y_STEPS)
                        for t in range(TPS):
                            i = TPS * b - TPS + t
                            ins = nc.vector.tensor_scalar(y[:, t, :], flat(x[:, tile(i), :]), core.mean[:, tile(i)],
                                                          core.rstd[:, tile(i)], ALU.subtract, ALU.mult)
                        then_y(ins)
                        then_y(nc.vector.tensor_tensor(y[:], y[:], bo[:, None, :].to_broadcast([P, TPS, D]), ALU.add))
                        dve.wait_ge(y_made, b)
                        then_y(nc.vector.tensor_tensor(y[:], y[:], bank[5][:, 0:LEN].rearrange("p (t d) -> p t d", t=TPS), ALU.add))
                        nc.vector.bn_stats(raw[:, 0, :], y[:, 0, :])
                        then_y(nc.vector.bn_stats(raw[:, 1, :], y[:, 1, :]))
                        xs = x[:, tile(TPS * b - TPS, TPS), :]
                        nc.vector.tensor_tensor(xs, xs, beta[:, None, :].to_broadcast([P, TPS, D]), ALU.add)
                        nc.vector.bn_aggr(mv[:, 0, :], raw[:, 0, :])
                        nc.vector.bn_aggr(mv[:, 1, :], raw[:, 1, :]).then_inc(y_varied, 1)
                    if now:
                        dve.wait_ge(k_rooted, b + 1)
                        then(nc.vector.reciprocal(k_inv[:], k_norm[:]))
                        nc.vector.tensor_tensor(k[:, half].rearrange("p t (h f) -> p (t h) f", f=HD),
                                                k_lin[:].rearrange("p t (h f) -> p (t h) f", f=HD),
                                                k_inv[:, :, None].to_broadcast([P, TPS * HEADS, HD]), ALU.mult).then_inc(k_ready, 1)
                        assert then.n == K_STEPS, then.n
                    if before:
                        dve.wait_ge(y_rooted, b)
                        then_y(nc.vector.reciprocal(inv[:], std[:]))
                        for t in range(TPS):
                            ins = nc.vector.tensor_scalar(y[:, t, :], y[:, t, :], mv[:, t, 0:1], inv[:, t:t + 1],
                                                          ALU.subtract, ALU.mult)
                        then_y(ins)
                        then_y(nc.vector.tensor_tensor(y[:], y[:], gamma[:, None, :].to_broadcast([P, TPS, D]), ALU.mult))
                        then_y(nc.vector.tensor_tensor(xs, xs, y[:], ALU.add))
                        assert then_y.n == Y_STEPS, then_y.n

                over_turns(dve, turn)

            @block.tensor
            def _(pe):
                def turn(b, half, before, now, following, again):
                    if now:
                        pe.wait_ge(xT_ready, b + 1)
                        if before:
                            pe.wait_ge(kv_ready, b)
                        pe.matmul(bank[1][:, 0:LEN], wq[:], xT[:], start=True, stop=True).then_inc(q_made, 1)
                        for t in range(TPS):
                            mm = pe.matmul(bank[2][:, t * 2 * D:(t + 1) * 2 * D], xT[:, t * P:(t + 1) * P], wkv[:],
                                           start=True, stop=True)
                        mm.then_inc(kv_made, 1)
                    if following:
                        pe.wait_ge(staged, TPS * b + 2 * TPS)
                        for t in range(TPS):
                            mm = pe.transpose(bank[0][:, t * P:(t + 1) * P], stage[:, t, :], core.ident[:])
                        mm.then_inc(turned, 1)
                    if before:
                        pe.wait_ge(k_ready, b)
                        last = 1 - half
                        for t in range(TPS):
                            mm = pe.matmul(bank[3][:, 0:D], kv[:, last, t, D:2 * D], k[:, last, t, :], start=t == 0, stop=t == TPS - 1)
                        mm.then_inc(vk_made, 1)
                        pe.wait_ge(vk_ready, b)
                        pe.matmul(bank[4][:, 0:D], vk[:], wo[:], start=True, stop=True).then_inc(m_made, 1)
                        pe.wait_ge(m_ready, b)
                        pe.wait_ge(q_ready, b)
                        for t in range(TPS):
                            mm = pe.matmul(bank[5][:, t * D:(t + 1) * D], q[:, last, t * P:(t + 1) * P], m[:], start=True, stop=True)
                        mm.then_inc(y_made, 1)

                over_turns(pe, turn)

            @block.scalar
            def _(act):
                act.wait_ge(eps_set, 1)

                def turn(b, half, before, now, following, again):
                    if now:
                        act.wait_ge(q_biased, b + 1)
                        nc.scalar.activation(q_exp[:], q_raw[:], ACT.Exp).then_inc(q_exp_ready, 1)
                        act.wait_ge(kv_ready, b + 1)
                        nc.scalar.activation(k_exp[:], kv[:, half, :, 0:D], ACT.Exp).then_inc(k_exp_ready, 1)
                    if following:
                        act.wait_ge(turned, b + 2)
                        nc.scalar.copy(xT[:], bank[0][:, 0:LEN]).then_inc(xT_ready, 1)
                    if before:
                        act.wait_ge(m_made, b)
                        nc.scalar.copy(m[:], bank[4][:, 0:D]).then_inc(m_ready, 1)
                    if now:
                        act.wait_ge(k_summed, b + 1)
                        nc.scalar.activation(k_norm[:], k_sum[:], ACT.Sqrt, bias=eps_col[:]).then_inc(k_rooted, 1)
                    if before:
                        act.wait_ge(y_varied, b)
                        nc.scalar.activation(std[:], mv[:, :, 1], ACT.Sqrt, bias=eps_col[:]).then_inc(y_rooted, 1)

                over_turns(act, turn)


def l1_feedforward(core):
    nc, x, bank, dram = core.nc, core.x, core.bank, core.dram
    H = 512
    C = H // P
    with ExitStack() as stack:
        sb, sem = scratch(core, stack)
        fc, proj = sb("f1_fc", [P, C, D]), sb("f1_proj", [P, H])
        ln_w, ln_b = sb("f1_ln_w", [P, C]), sb("f1_ln_b", [P, C])
        load_block(core, "f1", [(fc[:], dram["L1_fc"].rearrange("(c p) d -> p c d", p=P)), (proj[:], dram["L1_proj"]),
                                (ln_w[:], dram["L1_ln_w"]), (ln_b[:], dram["L1_ln_b"])])
        stats_block(core, "f1s", x, LN_EPS)

        ones = sb("f1_ones", [P, P])
        total, edge = sb("f1_total", [P, 2]), sb("f1_edge", [P, 2, 2])
        tern, below = sb("f1_tern", [P, 2, H]), sb("f1_below", [P, 2, H])
        w1, w2, w2_plain = sb("f1_w1", [D, H]), sb("f1_w2", [P, C, D]), sb("f1_w2_plain", [P, C, D])
        b_rows, shift = sb("f1_b_rows", [P, C, P]), sb("f1_shift", [P, D])
        made, product = sem("f1_made"), sem("f1_product")
        with nc.Block() as block:
            @block.vector
            def _(dve):
                then = Chain(dve, made)
                nc.vector.memset(ones[:], 1.0)
                nc.vector.tensor_reduce(total[:, 0:1], fc[:].rearrange("p c d -> p (c d)"), AX.X, ALU.add, apply_absolute_value=True)
                then(nc.vector.tensor_reduce(total[:, 1:2], proj[:], AX.X, ALU.add, apply_absolute_value=True))
                dve.wait_ge(product, 1)
                then(nc.vector.tensor_scalar(edge[:, 0], bank[0][:, 0:2], 1.0 / (H * D), 1e-6, ALU.mult, ALU.add))
                then(nc.vector.tensor_scalar(edge[:, 1], edge[:, 0], -0.5, None, ALU.mult))
                then(nc.vector.tensor_scalar(edge[:, 0], edge[:, 0], 0.5, None, ALU.mult))
                for n, src in ((0, fc[:].rearrange("p c d -> p (c d)")), (1, proj[:])):
                    then(nc.vector.tensor_scalar(below[:, n], src, edge[:, 1, n:n + 1], None, ALU.is_lt))
                    then(nc.vector.scalar_tensor_tensor(tern[:, n], src, edge[:, 0, n:n + 1], below[:, n],
                                                        ALU.is_gt, ALU.subtract))
                for c in range(C):
                    nc.vector.tensor_copy(b_rows[:, c, :], ln_b[:, c:c + 1].to_broadcast([P, P]))
                dve.wait_ge(product, 2)
                nc.vector.tensor_copy(w1[:], bank[1])
                for c in range(C):
                    nc.vector.tensor_scalar(w2[:, c, :], bank[2][:, c * D:(c + 1) * D], ln_w[:, c:c + 1], None, ALU.mult)
                then(nc.vector.tensor_copy(w2_plain[:].rearrange("p c d -> p (c d)"), bank[2]))
                dve.wait_ge(product, 3)
                nc.vector.tensor_copy(shift[:], bank[3][:, 0:D])

            @block.tensor
            def _(pe):
                pe.wait_ge(made, 1)
                pe.matmul(bank[0][:, 0:2], ones[:], total[:], start=True, stop=True).then_inc(product, 1)
                pe.wait_ge(made, 8)
                for c in range(C):
                    pe.transpose(bank[1][:, c * P:(c + 1) * P], tern[:, 0, c * P:(c + 1) * P], core.ident[:])
                    mm = pe.transpose(bank[2][:, c * P:(c + 1) * P], tern[:, 1, c * P:(c + 1) * P], core.ident[:])
                mm.then_inc(product, 1)
                pe.wait_ge(made, 9)
                for c in range(C):
                    mm = pe.matmul(bank[3][:, 0:D], b_rows[:, c, :], w2_plain[:, c, :], start=c == 0, stop=c == C - 1)
                mm.then_inc(product, 1)

        hid = sb("f1_hid", [P, TILES, H])
        stage, xT = sb("f1_stage", [P, TPS, D]), sb("f1_xT", [D, LEN])
        staged, turned, xT_ready, hidden, bent = (sem("f1_" + n) for n in ("staged", "turned", "xT_ready", "hidden", "bent"))
        with nc.Block() as block:
            @block.vector
            def _(dve):
                def turn(b, half, before, now, following, again):
                    if following:
                        if now:
                            dve.wait_ge(turned, b + 1)
                        put_normalized(core, dve, b + 1, stage, staged)

                over_turns(dve, turn)

            @block.tensor
            def _(pe):
                def turn(b, half, before, now, following, again):
                    if now:
                        pe.wait_ge(xT_ready, b + 1)
                        for t in range(TPS):
                            mm = pe.matmul(bank[1 + 2 * half + t], xT[:, t * P:(t + 1) * P], w1[:], start=True, stop=True)
                        mm.then_inc(hidden, 1)
                    if following:
                        pe.wait_ge(staged, TPS * b + 2 * TPS)
                        for t in range(TPS):
                            mm = pe.transpose(bank[0][:, t * P:(t + 1) * P], stage[:, t, :], core.ident[:])
                        mm.then_inc(turned, 1)

                over_turns(pe, turn)

            @block.scalar
            def _(act):
                def turn(b, half, before, now, following, again):
                    if following:
                        act.wait_ge(turned, b + 2)
                        nc.scalar.copy(xT[:], bank[0][:, 0:LEN]).then_inc(xT_ready, 1)
                    if now:
                        act.wait_ge(hidden, b + 1)
                        nc.scalar.activation(hid[:, tile(TPS * b, TPS), :], core.banks[:, 1 + 2 * half:3 + 2 * half, :], ACT.Gelu)\
                            .then_inc(bent, 1)

                over_turns(act, turn)

        stats_block(core, "f1h", hid, LN_EPS, width=H)

        norm, normT = sb("f1_norm", [P, 2, TPS, H]), sb("f1_normT", [P, 2, TPS, H])
        normed, flipped, normT_ready, projected, added, based = (sem("f1_" + n) for n in
                                                                 ("normed", "flipped", "normT_ready", "projected", "added", "based"))
        with nc.Block() as block:
            @block.vector
            def _(dve):
                def turn(b, half, before, now, following, again):
                    if following:
                        if before:
                            dve.wait_ge(flipped, TPS * b)
                        for t in range(TPS):
                            i = TPS * b + TPS + t
                            nc.vector.tensor_scalar(norm[:, 1 - half, t, :], flat(hid[:, tile(i), :]), core.mean[:, tile(i)],
                                                    core.rstd[:, tile(i)], ALU.subtract, ALU.mult).then_inc(normed, 1)
                    if before:
                        dve.wait_ge(projected, b)
                        dve.wait_ge(based, b)
                        xs = x[:, tile(TPS * b - TPS, TPS), :]
                        nc.vector.tensor_tensor(xs, xs, bank[7][:, 0:LEN].rearrange("p (t d) -> p t d", t=TPS), ALU.add)\
                            .then_inc(added, 1)

                over_turns(dve, turn)

            @block.gpsimd
            def _(pool):
                with pool.Fori(0, SEQS) as b:
                    xs = x[:, tile(TPS * b, TPS), :]
                    nc.gpsimd.tensor_tensor(xs, xs, shift[:, None, :].to_broadcast([P, TPS, D]), ALU.add).then_inc(based, 1)

            @block.tensor
            def _(pe):
                def turn(b, half, before, now, following, again):
                    if now:
                        for t in range(TPS):
                            pe.wait_ge(normed, TPS * b + t + 1)
                            for c in range(C):
                                mm = pe.transpose(bank[1 + 2 * half + t][:, c * P:(c + 1) * P], norm[:, half, t, c * P:(c + 1) * P],
                                                  core.ident[:])
                            mm.then_inc(flipped, 1)
                    if before:
                        pe.wait_ge(normT_ready, TPS * b)
                        if again:
                            pe.wait_ge(added, b - 1)
                        for t in range(TPS):
                            for c in range(C):
                                mm = pe.matmul(bank[7][:, t * D:(t + 1) * D], normT[:, 1 - half, t, c * P:(c + 1) * P], w2[:, c, :],
                                               start=c == 0, stop=c == C - 1)
                        mm.then_inc(projected, 1)

                over_turns(pe, turn)

            @block.scalar
            def _(act):
                def turn(b, half, before, now, following, again):
                    if now:
                        if again:
                            act.wait_ge(projected, b - 1)
                        for t in range(TPS):
                            act.wait_ge(flipped, TPS * b + t + 1)
                            nc.scalar.copy(normT[:, half, t, :], bank[1 + 2 * half + t]).then_inc(normT_ready, 1)

                over_turns(act, turn)


def l2_attention(core):
    nc, x, bank, dram = core.nc, core.x, core.bank, core.dram
    HEADS, HD, G = 16, 8, 4
    R = P // G
    with ExitStack() as stack:
        sb, sem = scratch(core, stack)
        wq, wk, wv = sb("a2_wq", [D, G, P]), sb("a2_wk", [D, G, P]), sb("a2_wv", [D, D])
        wo, bo, bv = sb("a2_wo", [D, D]), sb("a2_bo", [P, D]), sb("a2_bv", [P, D])
        bq, bk = sb("a2_bq", [P, G]), sb("a2_bk", [P, G])
        apart_f = sb("a2_apart_f", [P, TPS, LEN])
        slopes = sb("a2_slopes", [P, len(SLOPE_PARTS)])
        load_block(core, "a2", [(wq[:], dram["L2_wq"]), (wk[:], dram["L2_wk"]), (wv[:], dram["L2_wv"]), (wo[:], dram["L2_wo"]),
                                (bo[:], dram["L2_bo"]), (bv[:], dram["L2_bv"]), (bq[:], dram["L2_bq"]), (bk[:], dram["L2_bk"]),
                                (apart_f[:], dram["L2_apart"]), (slopes[:], dram["L2_slopes"])])
        stats_block(core, "a2s", x, LN_EPS)
        stage, xT = sb("a2_stage", [P, TPS, D]), sb("a2_xT", [D, LEN])
        q, k = sb("a2_q", [P, 2, G, LEN]), sb("a2_k", [P, 2, G, LEN])
        v = sb("a2_v", [P, 2, TPS, HEADS * (D + HD)])
        v_blocks = v[:].rearrange("p s t (h c) -> p s t h c", h=HEADS)
        neg_top, total, inv = sb("a2_neg_top", [P, 2, TPS]), sb("a2_total", [P, 2, TPS, HEADS]), sb("a2_inv", [P, TPS, HEADS])
        prob, probT = sb("a2_prob", [P, 2, TPS, LEN]), sb("a2_probT", [P, 2, 2 * LEN])
        inv_wide = sb("a2_inv_wide", [P, TPS, D])
        att_raw, attT = sb("a2_att_raw", [D, LEN]), sb("a2_attT", [D, LEN])
        (staged, turned, xT_ready, projected, qkv_ready, scored, topped, expd, flipped, probT_ready, summed,
         inverted, att_kept, inv_spread, inv_turned, attT_ready, out_made, based, added) = (
            sem("a2_" + n) for n in (
                "staged", "turned", "xT_ready", "projected", "qkv_ready", "scored", "topped", "expd",
                "flipped", "probT_ready", "summed", "inverted", "att_kept", "inv_spread", "inv_turned", "attT_ready", "out_made", "based", "added"))
        apart = sb("a2_apart", [P, TPS, LEN], BF16)
        diag = sb("a2_diag", [P, len(SLOPE_PARTS), P], BF16)
        first_part = [sum(1 for h, _ in SLOPE_PARTS if h < n) for n in range(HEADS + 1)]
        with nc.Block() as block:
            @block.gpsimd
            def _(pool):
                nc.gpsimd.memset(v[:], 0.0)

            @block.vector
            def _(dve):
                nc.vector.tensor_copy(apart[:], apart_f[:])
                for n in range(len(SLOPE_PARTS)):
                    nc.vector.tensor_scalar(diag[:, n, :], core.ident[:], slopes[:, n:n + 1], None, ALU.mult)

        TURN_INV, OUTPUT, FRONT, PROJECT = 3, 5, 7, 8
        PARTS = G + 1

        def over_sequences(eng, turn):
            turn(-1, 1, before=False, now=False, following=True)
            turn(0, 0, before=False, now=True, following=True)
            with eng.Fori(0, (SEQS - 2) // 2) as i:
                for n in range(2):
                    turn(2 * i + 1 + n, 1 - n, before=True, now=True, following=True)
            turn(SEQS - 1, 1, before=True, now=True, following=False)
            turn(SEQS, 0, before=True, now=False, following=False)

        with nc.Block() as block:
            @block.vector
            def _(dve):
                def project_part(b, part, half):
                    dve.wait_ge(projected, PARTS * b + part + 1)
                    made = bank[4 + 3 * (part % 2)]
                    if part < G:
                        nc.vector.tensor_scalar(q[:, half, part, :], made[:, 0:LEN], bq[:, part:part + 1],
                                                float(HD) ** -0.5, ALU.add, ALU.mult)
                        nc.vector.tensor_scalar(k[:, half, part, :], made[:, LEN:2 * LEN], bk[:, part:part + 1],
                                                None, ALU.add).then_inc(qkv_ready, 1)
                    else:
                        nc.vector.tensor_tensor(v_blocks[:, half, :, :, 0:HD],
                                                made[:, 0:LEN].rearrange("p (t h f) -> p t h f", t=TPS, h=HEADS),
                                                bv[:].rearrange("p (h f) -> p h f", h=HEADS)[:, None, :, :]
                                                .to_broadcast([P, TPS, HEADS, HD]), ALU.add).then_inc(qkv_ready, 1)

                def turn(b, half, before, now, following):
                    def has(h, back):
                        return now if h >= back else before

                    for h in range(HEADS):
                        u = b * HEADS + h
                        if now:
                            dve.wait_ge(scored, u + 1)
                            nc.vector.tensor_reduce(neg_top[:, h % 2, :], bank[h % 2].rearrange("p (t k) -> p t k", t=TPS),
                                                    AX.X, ALU.max, negate=True).then_inc(topped, 1)
                        if before and h == 1:
                            dve.wait_ge(summed, b * HEADS)
                            nc.vector.tensor_copy(att_raw[:], bank[5][:, 0:LEN]).then_inc(att_kept, 1)
                            dve.wait_ge(inverted, b)
                            nc.vector.tensor_copy(inv_wide[:].rearrange("p t (h f) -> p t h f", h=HEADS),
                                                  inv[:, :, :, None].to_broadcast([P, TPS, HEADS, HD])).then_inc(inv_spread, 1)
                        if before and h == TURN_INV + 1:
                            dve.wait_ge(inv_turned, b)
                            dve.wait_ge(att_kept, b)
                            nc.vector.tensor_tensor(attT[:], att_raw[:], bank[6][:, 0:LEN], ALU.mult).then_inc(attT_ready, 1)
                        if has(h, 1):
                            dve.wait_ge(flipped, u)
                            if has(h, 3):
                                dve.wait_ge(summed, u - 2)
                            nc.vector.tensor_copy(probT[:, (h - 1) % 2, :], bank[2 + (h - 1) % 2]).then_inc(probT_ready, 1)
                        if before and h == 0:
                            nc.vector.reciprocal(inv[:], total[:, 1 - half]).then_inc(inverted, 1)
                        if before and h == OUTPUT + 1:
                            dve.wait_ge(out_made, b)
                            dve.wait_ge(based, b)
                            xs = x[:, tile(TPS * b - TPS, TPS), :]
                            nc.vector.tensor_tensor(xs, xs, bank[7][:, 0:LEN].rearrange("p (t d) -> p t d", t=TPS), ALU.add)\
                                .then_inc(added, 1)
                        if following and h == FRONT - 2:
                            put_normalized(core, dve, b + 1, stage, staged)
                        if following and 0 <= h - PROJECT - 1 < PARTS:
                            project_part(b + 1, h - PROJECT - 1, 1 - half)

                over_sequences(dve, turn)

            @block.gpsimd
            def _(pool):
                with pool.Fori(0, SEQS) as b:
                    pool.wait_ge(staged, TPS * b + TPS)
                    xs = x[:, tile(TPS * b, TPS), :]
                    nc.gpsimd.tensor_tensor(xs, xs, bo[:, None, :].to_broadcast([P, TPS, D]), ALU.add).then_inc(based, 1)

            @block.tensor
            def _(pe):
                def scores(u, h, half, wait_bank):
                    g, r = h // G, h % G * R
                    if wait_bank:
                        pe.wait_ge(expd, u - 1)
                    for t in range(TPS):
                        out = bank[h % 2][:, t * LEN:(t + 1) * LEN]
                        for n in range(first_part[h], first_part[h + 1]):
                            pe.matmul(out, diag[:, n, :], apart[:, t, :], start=n == first_part[h], stop=False)
                        mm = pe.matmul(out, q[r:r + R, half, g, t * P:(t + 1) * P], k[r:r + R, half, g, :], start=False, stop=True)
                    mm.then_inc(scored, 1)

                def flip(u, h):
                    pe.wait_ge(expd, u + 1)
                    for t in range(TPS):
                        for c in range(TPS):
                            mm = pe.transpose(bank[2 + h % 2][:, (t * TPS + c) * P:(t * TPS + c + 1) * P],
                                              prob[:, h % 2, t, c * P:(c + 1) * P], core.ident[:])
                    mm.then_inc(flipped, 1)

                def values(u, h, half):
                    pe.wait_ge(probT_ready, u + 1)
                    for c in range(TPS):
                        mm = pe.matmul(bank[5][:, 0:LEN], v[:, half, c, h * D:(h + 1) * D],
                                       probT[:, h % 2, :].rearrange("p (t c q) -> p t c q", t=TPS, c=TPS)[:, :, c, :],
                                       start=h == 0 and c == 0, stop=h == HEADS - 1 and c == TPS - 1, skip_group_check=True)
                    mm.then_inc(summed, 1)

                def turn(b, half, before, now, following):
                    def has(h, back):
                        return now if h >= back else before

                    for h in range(HEADS):
                        u = b * HEADS + h
                        if now and h == 0:
                            pe.wait_ge(qkv_ready, PARTS * b + PARTS)
                        if now:
                            scores(u, h, half, has(h, 2))
                        if has(h, 2):
                            if before and h == 2:
                                pe.wait_ge(att_kept, b)
                            values(u - 2, (h - 2) % HEADS, half if h >= 2 else 1 - half)
                        if has(h, 1):
                            flip(u - 1, (h - 1) % HEADS)
                        if before and h == TURN_INV:
                            pe.wait_ge(inv_spread, b)
                            for t in range(TPS):
                                mm = pe.transpose(bank[6][:, t * P:(t + 1) * P], inv_wide[:, t, :], core.ident[:])
                            mm.then_inc(inv_turned, 1)
                        if before and h == OUTPUT:
                            pe.wait_ge(attT_ready, b)
                            for t in range(TPS):
                                mm = pe.matmul(bank[7][:, t * D:(t + 1) * D], attT[:, t * P:(t + 1) * P], wo[:], start=True, stop=True)
                            mm.then_inc(out_made, 1)
                        if following and h == FRONT:
                            pe.wait_ge(staged, TPS * b + 2 * TPS)
                            for t in range(TPS):
                                mm = pe.transpose(bank[6][:, t * P:(t + 1) * P], stage[:, t, :], core.ident[:])
                            mm.then_inc(turned, 1)
                        if following and 0 <= h - PROJECT < PARTS:
                            part = h - PROJECT
                            if part == 0:
                                pe.wait_ge(xT_ready, b + 2)
                            if part == 1 and before:
                                pe.wait_ge(added, b)
                            if part >= 2:
                                pe.wait_ge(qkv_ready, PARTS * b + PARTS + part - 1)
                            into = bank[4 + 3 * (part % 2)]
                            if part < G:
                                pe.matmul(into[:, 0:LEN], wq[:, part, :], xT[:], start=True, stop=True)
                                mm = pe.matmul(into[:, LEN:2 * LEN], wk[:, part, :], xT[:], start=True, stop=True)
                            else:
                                for t in range(TPS):
                                    mm = pe.matmul(into[:, t * D:(t + 1) * D], xT[:, t * P:(t + 1) * P], wv[:], start=True, stop=True)
                            mm.then_inc(projected, 1)

                over_sequences(pe, turn)

            @block.scalar
            def _(act):
                def turn(b, half, before, now, following):
                    def has(h, back):
                        return now if h >= back else before

                    for h in range(HEADS):
                        u = b * HEADS + h
                        if following and h == FRONT + 1:
                            act.wait_ge(turned, b + 2)
                            nc.scalar.copy(xT[:], bank[6][:, 0:LEN]).then_inc(xT_ready, 1)
                        if now:
                            act.wait_ge(topped, u + 1)
                            if has(h, 2):
                                act.wait_ge(flipped, u - 1)
                            for t in range(TPS):
                                e = nc.scalar.activation(prob[:, h % 2, t, :], bank[h % 2][:, t * LEN:(t + 1) * LEN], ACT.Exp,
                                                         bias=neg_top[:, h % 2, t:t + 1], accum_out=total[:, half, t, h:h + 1])
                            e.then_inc(expd, 1)

                over_sequences(act, turn)


def l2_feedforward(core):
    nc, dram = core.nc, core.dram
    DEPTH = 6
    with ExitStack() as stack:
        sb, sem = scratch(core, stack)
        tables = sb("r_tables", [P, 2, 2, LEN])
        masks_f = sb("r_masks_f", [P, TPS, WINDOW_KEYS])
        masks = sb("r_masks", [P, TPS, WINDOW_KEYS], BF16)
        head_ones = sb("r_head_ones", [P, 2])
        load_block(core, "r", [(tables[:], dram["r_tables"]), (masks_f[:], dram["r_masks"]), (head_ones[:], dram["r_head_ones"])])
        with nc.Block() as block:
            @block.vector
            def _(dve):
                nc.vector.tensor_copy(masks[:], masks_f[:])

        saved = sb("r_saved", [P, TILES, D])
        enter_stream(core, "rs", saved)
        w = sb("w_w", [D, 3, HEADS2 * HD2])
        wo = sb("w_wo", [P, PAIRS2, D])
        qk_scale = sb("w_qk_scale", [P, 2])
        w1, w2 = sb("g_w1", [D, 6, P]), sb("g_w2", [P, 3, D])
        ln_g, ln_b, b1, b2 = sb("g_ln_g", [D, 1]), sb("g_ln_b", [D, 1]), sb("g_b1", [P, 6]), sb("g_b2", [P, D])

        def attention_loads(n):
            return [(w[:].rearrange("p a n -> p (a n)"), flat2(dram["r_w"][tile(n)])),
                    (wo[:].rearrange("p a n -> p (a n)"), flat2(dram["r_wo"][tile(n)])),
                    (qk_scale[:], flat2(dram["r_qk_scale"][tile(n)]))]

        def feedforward_loads(n):
            return [(w1[:].rearrange("p a n -> p (a n)"), flat2(dram["g_w1"][tile(n)])),
                    (w2[:].rearrange("p a n -> p (a n)"), flat2(dram["g_w2"][tile(n)])),
                    (ln_g[:], flat2(dram["g_ln_g"][tile(n)])), (ln_b[:], flat2(dram["g_ln_b"][tile(n)])),
                    (b1[:], flat2(dram["g_b1"][tile(n)])), (b2[:], flat2(dram["g_b2"][tile(n)]))]

        load_block(core, "w0", attention_loads(0))
        with nc.Fori(0, DEPTH) as layer:
            windowed_attention(core, layer, tables, masks, head_ones, w, wo, qk_scale, feedforward_loads(layer))
            gated_feedforward(core, layer, w1, w2, ln_g, ln_b, b1, b2, attention_loads(layer + 1))
        leave_stream(core, saved)


HEADS2, HD2 = 16, 64
WINDOW = 32
PAIRS2 = HEADS2 // 2
WINDOW_KEYS = WINDOW + P


def start_loads(core, block, name, loads, layer):
    landed = core.sem(f"{name}_landed")

    @block.sync
    def _(sp):
        for dst, src in loads:
            sp.dma_start(dst, src).then_inc(landed, 16)
        sp.wait_ge(landed, layer * (16 * len(loads)) + 16 * len(loads))
        sp.sem_inc(core.passed, 1)


def windowed_attention(core, layer, tables, masks, head_ones, w, wo, qk_scale, next_loads):
    nc, x, bank, dram = core.nc, core.x, core.bank, core.dram
    INNER = HEADS2 * HD2
    with ExitStack() as stack:
        sb, sem = scratch(core, stack)
        cos_t, sin_t = sb("w_cos", [P, 2 * LEN]), sb("w_sin", [P, 2 * LEN])
        stage, xT = sb("w_stage", [P, LEN]), sb("w_xT", [D, LEN + 1])
        v = sb("w_v", [P, 2, TPS, INNER])
        by_cos, by_sin, square = (sb("w_" + n, [P, 2, 2 * LEN]) for n in ("by_cos", "by_sin", "square"))
        rope = sb("w_rope", [P, PAIRS2, 2 * LEN])
        NORMS = 2 * TPS * HEADS2
        norm, inv_norm = sb("w_norm", [P, NORMS]), sb("w_inv_norm", [P, NORMS])
        k_inv = sb("w_k_inv", [P, TPS, HEADS2, HD2])
        k = sb("w_k", [P, 2, WINDOW + LEN])
        top, neg_top = (sb("w_" + n, [P, 2, 4]) for n in ("top", "neg_top"))
        total, inv = sb("w_total", [P, 4, 4]), sb("w_inv", [P, 4, 4])
        prob = sb("w_prob", [P, 2, 4, 2 * P])
        probT = sb("w_probT", [P, 2, 4 * P])
        prevT = sb("w_prevT", [P, 2, 2, P])
        att, attT = sb("w_att", [P, 2, TPS * P]), sb("w_attT", [P, 2, LEN])
        names = ("staged", "turned", "xT_ready", "v_made", "v_ready", "qk_made", "rotated",
                 "squared", "roped", "sums_made", "rooted", "norms_ready", "k_spread", "k_turned", "k_ready", "scored",
                 "topped", "expd", "flipped", "probT_ready", "prevT_ready", "attended", "att_ready", "att_turned",
                 "attT_ready", "out_made", "added", "inverted")
        (staged, turned, xT_ready, v_made, v_ready, qk_made, rotated, squared, roped, sums_made,
         rooted, norms_ready, k_spread, k_turned, k_ready, scored, topped, expd, flipped, probT_ready, prevT_ready, attended,
         att_ready, att_turned, attT_ready, out_made, added, inverted) = (sem("w_" + n) for n in names)
        BS = layer * SEQS
        US = layer * (SEQS * PAIRS2)
        norm_rows, inv_rows = (a[:].rearrange("p (r h) -> p r h", h=HEADS2) for a in (norm, inv_norm))
        norms4 = inv_norm[:].rearrange("p (i t h) -> p i t h", i=2, t=TPS)

        with nc.Block() as block:
            @block.vector
            def _(dve):
                for i in range(2):
                    s = slice(i * LEN, (i + 1) * LEN)
                    nc.vector.tensor_scalar(cos_t[:, s], tables[:, 0, i], qk_scale[:, i:i + 1], None, ALU.mult)
                    nc.vector.tensor_scalar(sin_t[:, s], tables[:, 1, i], qk_scale[:, i:i + 1], None, ALU.mult)
                nc.vector.memset(xT[:, 0:1], 0.0)
                nc.vector.memset(k[:, :, 0:WINDOW], 0.0)

            @block.gpsimd
            def _(pool):
                nc.gpsimd.memset(prob[:, :, :, 0:P - WINDOW], 0.0)
                nc.gpsimd.memset(prevT[:, :, :, WINDOW:P], 0.0)

        SUMS = TPS * WINDOW_KEYS

        def over_sequences(eng, sequence):
            sequence(-1, 0, before=False, now=False, following=True, ahead=True)
            sequence(0, 1, before=False, now=True, following=True, ahead=True)
            with eng.Fori(0, (SEQS - 4) // 2) as i:
                for k in range(2):
                    sequence(2 * i + 1 + k, k, before=True, now=True, following=True, ahead=True)
            sequence(SEQS - 3, 0, before=True, now=True, following=True, ahead=True)
            sequence(SEQS - 2, 1, before=True, now=True, following=True, ahead=False)
            sequence(SEQS - 1, 0, before=True, now=True, following=False, ahead=False)
            sequence(SEQS, 1, before=True, now=False, following=False, ahead=False)

        with nc.Block() as block:
            start_loads(core, block, "g", next_loads, layer)

            @block.tensor
            def _(pe):
                def sums(u, hp, wait_scores):
                    pe.wait_ge(squared, u + PAIRS2)
                    if wait_scores:
                        pe.wait_ge(expd, u)
                    for i in range(2):
                        for t in range(TPS):
                            o = SUMS + (i * TPS + t) * HEADS2 + 2 * hp
                            mm = pe.matmul(bank[0][:, o:o + 2], square[:, hp % 2, i * LEN + t * P:i * LEN + (t + 1) * P],
                                           head_ones[:], start=True, stop=True)
                    mm.then_inc(sums_made, 1)

                def project(hp):
                    for n in range(2):
                        mm = pe.matmul(bank[2 + hp % 2][:, n * LEN:(n + 1) * LEN], w[:, n, hp * P:(hp + 1) * P],
                                       xT[:, 0:LEN], start=True, stop=True)
                    mm.then_inc(qk_made, 1)

                def values(u, hp, wait_last, outputs):
                    if wait_last:
                        pe.wait_ge(v_ready, u + PAIRS2)
                    if outputs is not None:
                        pe.wait_ge(added, outputs)
                    for t in range(TPS):
                        mm = pe.matmul(bank[7][:, LEN + t * P:LEN + (t + 1) * P], xT[:, t * P:(t + 1) * P],
                                       w[:, 2, hp * P:(hp + 1) * P], start=True, stop=True)
                    mm.then_inc(v_made, 1)

                def spread(u, hp):
                    pe.wait_ge(k_spread, u + 1)
                    for t in range(TPS):
                        mm = pe.transpose(bank[5][:, t * P:(t + 1) * P],
                                          k_inv[:, t, 2 * hp:2 * hp + 2, :].rearrange("p h f -> p (h f)"), core.ident[:])
                    mm.then_inc(k_turned, 1)

                def scores(u, hp, wait_last):
                    pe.wait_ge(k_ready, u + 1)
                    if wait_last:
                        pe.wait_ge(expd, u)
                    for h in range(2):
                        pe.matmul(bank[h][:, 0:TPS * WINDOW_KEYS], core.ident_bf[:],
                                  masks[:].rearrange("p t k -> p (t k)"), start=True, stop=False)
                    for t in range(TPS):
                        for h in range(2):
                            mm = pe.matmul(bank[h][:, t * WINDOW_KEYS:(t + 1) * WINDOW_KEYS],
                                           rope[HD2 * h:HD2 * (h + 1), hp, t * P:(t + 1) * P],
                                           k[HD2 * h:HD2 * (h + 1), hp % 2, t * P:t * P + WINDOW_KEYS], start=False, stop=t == TPS - 1)
                    mm.then_inc(scored, 1)

                def front(b):
                    pe.wait_ge(staged, BS + b + 1)
                    for t in range(TPS):
                        mm = pe.transpose(bank[4][:, t * P:(t + 1) * P], stage[:, t * P:(t + 1) * P], core.ident[:])
                    mm.then_inc(turned, 1)

                def flip(u, hp, wait_last):
                    a = hp % 2
                    pe.wait_ge(expd, u + 1)
                    if wait_last:
                        pe.wait_ge(att_ready, u)
                    for j in range(4):
                        pe.transpose(bank[4][:, j * P:(j + 1) * P], prob[:, a, j, P:2 * P], core.ident[:])
                    for h in range(2):
                        mm = pe.transpose(bank[6][:, h * WINDOW:(h + 1) * WINDOW], prob[0:WINDOW, a, 2 + h, 0:P],
                                          core.ident[0:WINDOW, 0:WINDOW])
                    mm.then_inc(flipped, 1)

                def attend(u, hp, half):
                    a = hp % 2
                    pe.wait_ge(probT_ready, u + 1)
                    pe.wait_ge(prevT_ready, u + 1)
                    for t in range(TPS):
                        for h in range(2):
                            j = 2 * t + h
                            out = bank[6][:, P + j * HD2:P + (j + 1) * HD2]
                            hs = slice((2 * hp + h) * HD2, (2 * hp + h + 1) * HD2)
                            mm = pe.matmul(out, probT[:, a, j * P:(j + 1) * P], v[:, half, t, hs], start=True, stop=t == 0)
                            if t == 1:
                                mm = pe.matmul(out, prevT[:, a, h, :], v[:, half, 0, hs], start=False, stop=True)
                    mm.then_inc(attended, 1)

                def turn_att(u, hp, wait_k):
                    pe.wait_ge(att_ready, u + 1)
                    if wait_k:
                        pe.wait_ge(k_ready, u + 4)
                    for t in range(TPS):
                        mm = pe.transpose(bank[5][:, LEN + t * P:LEN + (t + 1) * P], att[:, hp % 2, t * P:(t + 1) * P], core.ident[:])
                    mm.then_inc(att_turned, 1)

                def output(u, hp, taken, wait_last):
                    pe.wait_ge(attT_ready, u + 1)
                    if taken is not None:
                        pe.wait_ge(v_ready, taken)
                    if wait_last:
                        pe.wait_ge(added, u)
                    for t in range(TPS):
                        mm = pe.matmul(bank[7][:, t * D:(t + 1) * D], attT[:, hp % 2, t * P:(t + 1) * P], wo[:, hp, :],
                                       start=True, stop=True)
                    mm.then_inc(out_made, 1)

                def sequence(b, NEXT, before, now, following, ahead):
                    def has(s, back):
                        return now if s >= back else before

                    for s in range(PAIRS2):
                        u = US + b * PAIRS2 + s
                        if following:
                            if s == 0:
                                if not now:
                                    front(b + 1)
                                pe.wait_ge(xT_ready, BS + b + 2)
                            project(s)
                        if following and s % 4:
                            values(u, s, True, u - 3 if has(s, 4) else None)
                        if ahead and s == PAIRS2 - 1:
                            if now:
                                pe.wait_ge(probT_ready, u - 1)
                            front(b + 2)
                        if following if s >= 1 else now:
                            sums(u, (s - 1) % PAIRS2, has(s, 1))
                        if following and s % 4 == 0:
                            values(u, s, s >= 1 or now, u - 3 if has(s, 4) else None)
                        if s == 0 and now:
                            pe.wait_ge(rooted, 2 * (BS + b) + 2)
                        if s == 4 and following:
                            pe.wait_ge(rooted, 2 * (BS + b) + 3)
                        if now:
                            scores(u, s, has(s, 1))
                        if has(s, 2):
                            attend(u - 2, (s - 2) % PAIRS2, NEXT if s < 2 else 1 - NEXT)
                        if has(s, 3):
                            output(u - 3, (s - 3) % PAIRS2, u + PAIRS2 + 1 if following else None, has(s, 4))
                        spreading = now if s + 1 < PAIRS2 else following
                        if spreading:
                            spread(u + 1, (s + 1) % PAIRS2)
                        if has(s, 1):
                            if ahead and s == PAIRS2 - 1:
                                pe.wait_ge(xT_ready, BS + b + 3)
                            flip(u - 1, (s - 1) % PAIRS2, has(s, 2))
                        if has(s, 2):
                            turn_att(u - 2, (s - 2) % PAIRS2, spreading)

                over_sequences(pe, sequence)

            @block.vector
            def _(dve):
                def reduce_scores(u, s):
                    a = s % 2
                    dve.wait_ge(scored, u + 1)
                    nc.vector.tensor_reduce(top[:, a, :].rearrange("p (t h) -> p t h", t=2),
                                            core.banks[:, 0:2, 0:TPS * WINDOW_KEYS].rearrange("p h (t c) -> p t h c", t=2),
                                            AX.X, ALU.max, negate=True).then_inc(topped, 1)
                    dve.wait_ge(topped, 2 * u + 1)
                    nc.vector.tensor_tensor(neg_top[:, a, :].rearrange("p (t h) -> p t h", t=2),
                                            top[:, a, :].rearrange("p (t h) -> p t h", t=2),
                                            norms4[:, 0, :, 2 * s:2 * s + 2], ALU.mult).then_inc(topped, 1)

                def invert_norms(part, count):
                    some = slice(part * HEADS2 // 2, (part + 1) * HEADS2 // 2)
                    dve.wait_ge(rooted, count)
                    nc.vector.tensor_scalar(norm_rows[:, :, some], norm_rows[:, :, some], 1e-12, None, ALU.max).then_inc(norms_ready, 1)
                    dve.wait_ge(norms_ready, 2 * count - 1)
                    nc.vector.reciprocal(inv_rows[:, :, some], norm_rows[:, :, some]).then_inc(norms_ready, 1)

                def divide(u, hp):
                    dve.wait_ge(inverted, u + 1)
                    dve.wait_ge(attended, u + 1)
                    nc.vector.tensor_tensor(att[:, hp % 2, :].rearrange("p (j f) -> p j f", j=4),
                                            bank[6][:, P:P + 4 * HD2].rearrange("p (j f) -> p j f", j=4),
                                            inv[:, hp % 4, :, None].to_broadcast([P, 4, HD2]), ALU.mult).then_inc(att_ready, 1)

                def add_output(u, b):
                    dve.wait_ge(out_made, u + 1)
                    xs = x[:, tile(TPS * b, TPS), :]
                    nc.vector.tensor_tensor(xs, xs, bank[7][:, 0:LEN].rearrange("p (t d) -> p t d", t=TPS), ALU.add)\
                        .then_inc(added, 1)

                def scale_keys(u, hp):
                    dve.wait_ge(k_turned, u + 1)
                    dve.wait_ge(roped, u + 1)
                    nc.vector.tensor_tensor(k[:, hp % 2, WINDOW:], rope[:, hp, LEN:2 * LEN], bank[5][:, 0:LEN], ALU.mult)\
                        .then_inc(k_ready, 1)

                def rotate(u, hp, wait_buffer):
                    a = hp % 2
                    dve.wait_ge(qk_made, u + PAIRS2 + 1)
                    if wait_buffer:
                        dve.wait_ge(roped, u + PAIRS2 - 1)
                    made = bank[2 + a]
                    nc.vector.tensor_tensor(by_cos[:, a, :], made, cos_t[:], ALU.mult)
                    for half in range(4):
                        src, dst = (slice(h * HD2 // 2, (h + 1) * HD2 // 2) for h in (half, half ^ 1))
                        sine = nc.vector.tensor_tensor(by_sin[dst, a, :], made[src, :], sin_t[src, :], ALU.mult)
                    sine.then_inc(rotated, 1)

                def take_flipped(u, hp):
                    dve.wait_ge(flipped, u + 1)
                    nc.vector.tensor_copy(prevT[:, hp % 2, :, 0:WINDOW],
                                          bank[6][:, 0:2 * WINDOW].rearrange("p (h q) -> p h q", h=2)).then_inc(prevT_ready, 1)
                    nc.vector.reciprocal(inv[:, hp % 4, :], total[:, hp % 4, :]).then_inc(inverted, 1)

                def sequence(b, NEXT, before, now, following, ahead):
                    def has(s, back):
                        return now if s >= back else before

                    def stage_sequence(b):
                        nc.vector.tensor_copy(stage[:], x[:, tile(TPS * b, TPS), :].rearrange("p t d -> p (t d)")).then_inc(staged, 1)

                    if not before and not now:
                        stage_sequence(b + 1)
                    for s in range(PAIRS2):
                        u = US + b * PAIRS2 + s
                        if following:
                            rotate(u, s, s >= 2 or now)
                        if now:
                            if s % 4 == 0:
                                dve.wait_ge(norms_ready, 4 * (BS + b) + 2 + s // 2)
                            reduce_scores(u, s)
                        if has(s, 2):
                            divide(u - 2, (s - 2) % PAIRS2)
                        if has(s, 3):
                            add_output(u - 3, b if s >= 3 else b - 1)
                        if now if s + 1 < PAIRS2 else following:
                            scale_keys(u + 1, (s + 1) % PAIRS2)
                        if has(s, 1):
                            take_flipped(u - 1, (s - 1) % PAIRS2)
                        if s == 0 and now:
                            invert_norms(1, 2 * (BS + b) + 2)
                        if s == 4 and following:
                            invert_norms(0, 2 * (BS + b) + 3)
                        if ahead and s == 5:
                            stage_sequence(b + 2)

                over_sequences(dve, sequence)

            @block.gpsimd
            def _(pool):
                def sequence(b, NEXT, before, now, following, ahead):
                    for s in range(PAIRS2):
                        u = US + b * PAIRS2 + s
                        if now if s < PAIRS2 - 2 else following:
                            hp = (s + 2) % PAIRS2
                            if hp % 4 == 0:
                                pool.wait_ge(norms_ready, 4 * (BS + b) + (4 if hp else 6))
                                pool.sem_inc(core.passed, 1)
                            hs = slice(2 * hp, 2 * hp + 2)
                            nc.gpsimd.tensor_copy(k_inv[:, :, hs, :],
                                                  norms4[:, 1, :, hs, None].to_broadcast([P, TPS, 2, HD2])).then_inc(k_spread, 1)
                        if following:
                            if now:
                                pool.wait_ge(scored, u + 1)
                            pool.wait_ge(rotated, u + PAIRS2 + 1)
                            nc.gpsimd.tensor_tensor(rope[:, s, :], by_cos[:, s % 2, :], by_sin[:, s % 2, :], ALU.add).then_inc(roped, 1)

                over_sequences(pool, sequence)

            @block.scalar
            def _(act):
                def exponentials(u, s):
                    a = s % 2
                    act.wait_ge(topped, 2 * u + 2)
                    for j in range(4):
                        t, h = j // 2, j % 2
                        e = nc.scalar.activation(prob[:, a, j, P - WINDOW:2 * P],
                                                 bank[h][:, t * WINDOW_KEYS:(t + 1) * WINDOW_KEYS], ACT.Exp,
                                                 bias=neg_top[:, a, j:j + 1], scale=norms4[:, 0, t, 2 * s + h:2 * s + h + 1],
                                                 accum_out=total[:, s % 4, j:j + 1])
                    e.then_inc(expd, 1)

                def squares(u, hp, wait_buffer):
                    act.wait_ge(rotated, u + PAIRS2 + 1)
                    if wait_buffer:
                        act.wait_ge(sums_made, u + PAIRS2 - 1)
                    nc.scalar.activation(square[:, hp % 2, :], bank[2 + hp % 2], ACT.Square).then_inc(squared, 1)

                def take_values(u, hp, half):
                    act.wait_ge(v_made, u + PAIRS2 + 1)
                    nc.scalar.copy(v[:, half, :, hp * P:(hp + 1) * P], bank[7][:, LEN:2 * LEN].rearrange("p (t n) -> p t n", t=TPS))\
                        .then_inc(v_ready, 1)

                def take_flipped(u, hp):
                    act.wait_ge(flipped, u + 1)
                    nc.scalar.copy(probT[:, hp % 2, :], bank[4]).then_inc(probT_ready, 1)

                def take_turned(u, hp, wait_buffer):
                    act.wait_ge(att_turned, u + 1)
                    if wait_buffer:
                        act.wait_ge(out_made, u - 1)
                    nc.scalar.copy(attT[:, hp % 2, :], bank[5][:, LEN:2 * LEN]).then_inc(attT_ready, 1)

                def sequence(b, NEXT, before, now, following, ahead):
                    def has(s, back):
                        return now if s >= back else before

                    def take_front(b):
                        act.wait_ge(turned, BS + b + 1)
                        nc.scalar.copy(xT[0:HD2, 0:LEN], bank[4][0:HD2, 0:LEN])
                        nc.scalar.copy(xT[HD2:P, 1:LEN + 1], bank[4][HD2:P, 0:LEN]).then_inc(xT_ready, 1)

                    if not before and not now:
                        take_front(b + 1)
                    for s in range(PAIRS2):
                        u = US + b * PAIRS2 + s
                        if s == 0 and now or s == 4 and following:
                            some = slice(HEADS2 // 2, HEADS2) if s == 0 else slice(0, HEADS2 // 2)
                            act.wait_ge(sums_made, u + PAIRS2)
                            nc.scalar.activation(norm_rows[:, :, some],
                                                 bank[0][:, SUMS:SUMS + NORMS].rearrange("p (r h) -> p r h", h=HEADS2)[:, :, some],
                                                 ACT.Sqrt).then_inc(rooted, 1)
                        if following:
                            take_values(u, s, NEXT)
                        if ahead and s == PAIRS2 - 1:
                            take_front(b + 2)
                        if now:
                            exponentials(u, s)
                        if following:
                            squares(u, s, s >= 2 or now)
                        if has(s, 1):
                            take_flipped(u - 1, (s - 1) % PAIRS2)
                        if has(s, 2):
                            take_turned(u - 2, (s - 2) % PAIRS2, has(s, 4))

                over_sequences(act, sequence)


def gated_feedforward(core, layer, w1, w2, ln_g, ln_b, b1, b2, next_loads):
    nc, x, bank, dram = core.nc, core.x, core.bank, core.dram
    C = 3
    HALF = D // 2
    with ExitStack() as stack:
        sb, sem = scratch(core, stack)
        shifted = sb("g_shifted", [P, TILES, D])
        by_seq = [a.rearrange("p (s t) d -> p s t d", t=TPS) for a in (x[:], shifted[:])]
        moves = [(shifted[:, :, 0:HALF], x[:, :, 0:HALF]),
                 (shifted[1:P, :, HALF:D], x[0:P - 1, :, HALF:D]),
                 (by_seq[1][0:1, :, 1, HALF:D], by_seq[0][P - 1:P, :, 0, HALF:D])]
        summed = sem("g_summed")
        bias = sb("g_bias", [P, 2 * C])
        with nc.Block() as block:
            start_loads(core, block, "gs", moves, layer)

            @block.tensor
            def _(pe):
                for n in range(2 * C):
                    mm = pe.matmul(bank[0][:, n:n + 1], w1[:, n, :], ln_b[:], start=True, stop=True)
                mm.then_inc(summed, 1)

            @block.vector
            def _(dve):
                nc.vector.memset(by_seq[1][0:1, :, 0, HALF:D], 0.0)
                dve.wait_ge(summed, layer + 1)
                nc.vector.tensor_tensor(bias[:], bank[0][:, 0:2 * C], b1[:], ALU.add)
                nc.vector.tensor_scalar(w1[:], w1[:], ln_g[:, 0:1], None, ALU.mult)

        stats_block(core, "gs", shifted, LN_EPS, layer=layer)

        stage, xT = sb("g_stage", [P, 2, TPS, D]), sb("g_xT", [D, 2, LEN])
        gate, hid = sb("g_gate", [P, C, LEN]), sb("g_hid", [P, 2, C, LEN])
        staged, turned, xT_ready, made, bent, gated, out_made, added, based = (
            sem("g_" + n) for n in ("staged", "turned", "xT_ready", "hid_made", "bent", "gated", "out_made", "added", "based"))
        BS = layer * SEQS

        def first_of_all(b):
            return isinstance(b, int) and b == 1

        def over_sequences(eng, turn):
            turn(-1, 1, finish=False, now=False, front=True)
            turn(0, 0, finish=False, now=True, front=True)
            turn(1, 1, finish=True, now=True, front=True)
            with eng.Fori(0, (SEQS - 4) // 2) as i:
                for k in range(2):
                    turn(2 * i + 2 + k, k, finish=True, now=True, front=True)
            turn(SEQS - 2, 0, finish=True, now=True, front=True)
            turn(SEQS - 1, 1, finish=True, now=True, front=False)
            turn(SEQS, 0, finish=True, now=False, front=False)

        with nc.Block() as block:
            start_loads(core, block, "w", next_loads, layer)

            @block.vector
            def _(dve):
                def turn(b, half, finish, now, front):
                    if front:
                        if finish:
                            dve.wait_ge(turned, BS + b)
                        for t in range(TPS):
                            i = TPS * b + TPS + t
                            nc.vector.tensor_scalar(stage[:, 1 - half, t, :], flat(shifted[:, tile(i), :]), core.mean[:, tile(i)],
                                                    core.rstd[:, tile(i)], ALU.subtract, ALU.mult).then_inc(staged, 1)
                    if now:
                        for c in range(C):
                            dve.wait_ge(bent, C * (BS + b) + c + 1)
                            nc.vector.scalar_tensor_tensor(hid[:, half, c, :], bank[1 + C * half + c][:, 0:LEN], bias[:, c:c + 1],
                                                           gate[:, c, :], ALU.add, ALU.mult).then_inc(gated, 1)
                    if finish:
                        dve.wait_ge(out_made, BS + b)
                        dve.wait_ge(based, BS + b)
                        xs = x[:, tile(TPS * b - TPS, TPS), :]
                        nc.vector.tensor_tensor(xs, xs, bank[7][:, 0:LEN].rearrange("p (t d) -> p t d", t=TPS), ALU.add)\
                            .then_inc(added, 1)

                over_sequences(dve, turn)

            @block.gpsimd
            def _(pool):
                with pool.Fori(0, SEQS) as b:
                    xs = x[:, tile(TPS * b, TPS), :]
                    nc.gpsimd.tensor_tensor(xs, xs, b2[:, None, :].to_broadcast([P, TPS, D]), ALU.add).then_inc(based, 1)

            @block.tensor
            def _(pe):
                def turn(b, half, finish, now, front):
                    if now:
                        pe.wait_ge(xT_ready, BS + b + 1)
                        for c in range(C):
                            pe.matmul(bank[1 + C * half + c][:, 0:LEN], w1[:, c, :], xT[:, half, :], start=True, stop=True)
                            pe.matmul(bank[1 + C * half + c][:, LEN:2 * LEN], w1[:, C + c, :], xT[:, half, :],
                                      start=True, stop=True).then_inc(made, 1)
                    if front:
                        pe.wait_ge(staged, TPS * (BS + b) + 2 * TPS)
                        for t in range(TPS):
                            mm = pe.transpose(bank[0][:, t * P:(t + 1) * P], stage[:, 1 - half, t, :], core.ident[:])
                        mm.then_inc(turned, 1)
                    if finish:
                        pe.wait_ge(gated, C * (BS + b))
                        if not first_of_all(b):
                            pe.wait_ge(added, BS + b - 1)
                        for t in range(TPS):
                            for c in range(C):
                                mm = pe.matmul(bank[7][:, t * D:(t + 1) * D], hid[:, 1 - half, c, t * P:(t + 1) * P], w2[:, c, :],
                                               start=c == 0, stop=c == C - 1)
                        mm.then_inc(out_made, 1)

                over_sequences(pe, turn)

            @block.scalar
            def _(act):
                def turn(b, half, finish, now, front):
                    if now:
                        for c in range(C):
                            act.wait_ge(made, C * (BS + b) + c + 1)
                            if finish:
                                act.wait_ge(gated, C * (BS + b) - C + c + 1)
                            nc.scalar.activation(gate[:, c, :], bank[1 + C * half + c][:, LEN:2 * LEN], ACT.Gelu,
                                                 bias=bias[:, C + c:C + c + 1]).then_inc(bent, 1)
                    if front:
                        act.wait_ge(turned, BS + b + 2)
                        nc.scalar.copy(xT[:, 1 - half, :], bank[0][:, 0:LEN]).then_inc(xT_ready, 1)

                over_sequences(act, turn)


def flat2(ap):
    return ap.rearrange("a p n -> (a p) n")


def l3_attention(core):
    nc, x, bank, dram = core.nc, core.x, core.bank, core.dram
    with ExitStack() as stack:
        sb, sem = scratch(core, stack)
        w, bqk, bv = sb("a3_w", [D, 3 * D]), sb("a3_bqk", [D, 2]), sb("a3_bv", [P, D])
        decay = sb("a3_decay", [P, 3, P])
        load_block(core, "a3", [(w[:], dram["L3_wqkv"]), (bqk[:], dram["L3_bqk"]), (bv[:], dram["L3_bv"]),
                                (decay[:], dram["L3_decay"])])
        stats_block(core, "a3s", x, LN_EPS)
        stage, xT = sb("a3_stage", [P, TPS, D]), sb("a3_xT", [D, LEN])
        qk, v, score = sb("a3_qk", [D, 2, LEN]), sb("a3_v", [P, 2, TPS, D]), sb("a3_score", [P, 3, P])
        staged, turned, xT_ready, made, qk_ready, v_ready, scored, decayed, out_made, added = (
            sem("a3_" + n) for n in ("staged", "turned", "xT_ready", "made", "qk_ready", "v_ready", "scored", "decayed",
                                     "out_made", "added"))
        with nc.Block() as block:
            @block.vector
            def _(dve):
                def turn(b, half, before, now, following, again):
                    if following:
                        if now:
                            dve.wait_ge(turned, b + 1)
                        put_normalized(core, dve, b + 1, stage, staged)
                    if before:
                        dve.wait_ge(scored, b)
                        nc.vector.tensor_tensor(score[:], bank[3][:, 0:3 * P].rearrange("p (n q) -> p n q", n=3), decay[:], ALU.mult)\
                            .then_inc(decayed, 1)
                    if now:
                        dve.wait_ge(made, b + 1)
                        nc.vector.tensor_tensor(v[:, half], bank[2][:, 0:LEN].rearrange("p (t d) -> p t d", t=TPS),
                                                bv[:, None, :].to_broadcast([P, TPS, D]), ALU.add).then_inc(v_ready, 1)
                    if before:
                        dve.wait_ge(out_made, b)
                        xs = x[:, tile(TPS * b - TPS, TPS), :]
                        nc.vector.tensor_tensor(xs, xs, bank[4][:, 0:LEN].rearrange("p (t d) -> p t d", t=TPS), ALU.add)\
                            .then_inc(added, 1)

                over_turns(dve, turn)

            @block.tensor
            def _(pe):
                def turn(b, half, before, now, following, again):
                    if before:
                        pe.wait_ge(qk_ready, b)
                        pe.matmul(bank[3][:, 0:LEN], qk[:, 1, 0:P], qk[:, 0, :], start=True, stop=True)
                        pe.matmul(bank[3][:, LEN:LEN + P], qk[:, 1, P:LEN], qk[:, 0, P:LEN], start=True, stop=True).then_inc(scored, 1)
                    if now:
                        pe.wait_ge(xT_ready, b + 1)
                        for n in range(2):
                            pe.matmul(bank[1][:, n * LEN:(n + 1) * LEN], w[:, n * D:(n + 1) * D], xT[:], start=True, stop=True)
                        if before:
                            pe.wait_ge(v_ready, b)
                        for t in range(TPS):
                            mm = pe.matmul(bank[2][:, t * D:(t + 1) * D], xT[:, t * P:(t + 1) * P], w[:, 2 * D:3 * D], start=True, stop=True)
                        mm.then_inc(made, 1)
                    if following:
                        pe.wait_ge(staged, TPS * b + 2 * TPS)
                        for t in range(TPS):
                            mm = pe.transpose(bank[0][:, t * P:(t + 1) * P], stage[:, t, :], core.ident[:])
                        mm.then_inc(turned, 1)
                    if before:
                        pe.wait_ge(decayed, b)
                        if not now:
                            pe.wait_ge(v_ready, b)
                        if again:
                            pe.wait_ge(added, b - 1)
                        last = 1 - half
                        pe.matmul(bank[4][:, 0:D], score[:, 0, :], v[:, last, 0, :], start=True, stop=True)
                        pe.matmul(bank[4][:, D:2 * D], score[:, 1, :], v[:, last, 0, :], start=True, stop=False)
                        pe.matmul(bank[4][:, D:2 * D], score[:, 2, :], v[:, last, 1, :], start=False, stop=True).then_inc(out_made, 1)

                over_turns(pe, turn)

            @block.scalar
            def _(act):
                def turn(b, half, before, now, following, again):
                    if now:
                        act.wait_ge(made, b + 1)
                        for n in range(2):
                            ins = nc.scalar.activation(qk[:, n, :], bank[1][:, n * LEN:(n + 1) * LEN], ACT.Identity, bias=bqk[:, n:n + 1])
                        ins.then_inc(qk_ready, 1)
                    if following:
                        act.wait_ge(turned, b + 2)
                        nc.scalar.copy(xT[:], bank[0][:, 0:LEN]).then_inc(xT_ready, 1)

                over_turns(act, turn)


def l3_feedforward(core):
    nc, x, bank, dram = core.nc, core.x, core.bank, core.dram
    LAYERS, E, H = 4, 4, 512
    C = H // P
    with ExitStack() as stack:
        sb, sem = scratch(core, stack)
        w1, w2 = sb("m_w1", [D, E, H]), sb("m_w2", [P, E * C, D])
        g, b_ln, b1, b2 = sb("m_g", [D, E]), sb("m_b_ln", [D, E]), sb("m_b1", [P, E * C]), sb("m_b2", [P, E, D])
        rw, rb, earlier = sb("m_rw", [D, E]), sb("m_rb", [P, E]), sb("m_earlier", [P, E, E])
        load_block(core, "m0", [(earlier[:].rearrange("p a b -> p (a b)"), dram["m_earlier"])])
        bias = sb("m_bias", [P, E * C])
        stage, xT = sb("m_stage", [P, TPS, D]), sb("m_xT", [D, 2, LEN])
        TG = 4
        r_xT = sb("m_r_xT", [D, 2, TG * P])
        logit, top, comb, rank, kept = (sb("m_" + n, s) for n, s in (
            ("logit", [P, TILES, E]), ("top", [P, TILES]), ("comb", [P, TILES, E]), ("rank", [P, TILES, E]), ("kept", [P, TILES])))
        above, equal = sb("m_above", [P, TILES, E, E]), sb("m_equal", [P, TILES, E, E])
        hid = sb("m_hid", [P, 2, C, LEN])
        names = ("summed", "r_turned", "r_xT_ready", "routed", "route", "spread", "staged", "turned",
                 "xT_ready", "hidden", "bent", "projected", "added", "based")
        (summed, r_turned, r_xT_ready, routed, route, spread, staged, turned, xT_ready, hidden, bent,
         projected, added, based) = (sem("m_" + n) for n in names)
        saved = sb("m_saved", [P, TILES, D])
        enter_stream(core, "ms0", saved)
        with nc.Fori(0, LAYERS) as layer:
            BS = layer * SEQS
            load_layer(core, "m", [(w1[:].rearrange("p e h -> p (e h)"), flat2(dram["m_w1"][tile(layer)])),
                                   (w2[:].rearrange("p n d -> p (n d)"), flat2(dram["m_w2"][tile(layer)])),
                                   (g[:], flat2(dram["m_g"][tile(layer)])), (b_ln[:], flat2(dram["m_b_ln"][tile(layer)])),
                                   (b1[:], flat2(dram["m_b1"][tile(layer)])),
                                   (b2[:].rearrange("p e d -> p (e d)"), flat2(dram["m_b2"][tile(layer)])),
                                   (rw[:], flat2(dram["m_rw"][tile(layer)])), (rb[:], flat2(dram["m_rb"][tile(layer)]))], layer)

            GROUPS = TILES // TG
            RS = layer * GROUPS

            def route_pe(pe):
                def turn(g):
                    if g >= 2:
                        pe.wait_ge(r_xT_ready, RS + g - 1)
                    for k in range(TG):
                        mm = pe.transpose(bank[g % 2][:, k * P:(k + 1) * P], x[:, g * TG + k, :], core.ident[:])
                    mm.then_inc(r_turned, 1)

                def logits(g):
                    pe.wait_ge(r_xT_ready, RS + g + 1)
                    for k in range(TG):
                        n = g * TG + k
                        mm = pe.matmul(bank[3][:, n * E:(n + 1) * E], r_xT[:, g % 2, k * P:(k + 1) * P], rw[:], start=True, stop=True)
                    mm.then_inc(routed, 1)

                for e in range(E):
                    for c in range(C):
                        n = e * C + c
                        mm = pe.matmul(bank[2][:, n:n + 1], w1[:, e, c * P:(c + 1) * P], b_ln[:, e:e + 1], start=True, stop=True)
                mm.then_inc(summed, 1)
                for g in range(GROUPS + 1):
                    if g < GROUPS:
                        turn(g)
                    if g >= 1:
                        logits(g - 1)

            def route_act(act):
                for g in range(GROUPS):
                    if g >= 2:
                        act.wait_ge(routed, RS + g - 1)
                    act.wait_ge(r_turned, RS + g + 1)
                    nc.scalar.copy(r_xT[:, g % 2, :], bank[g % 2]).then_inc(r_xT_ready, 1)

            def route_dve(dve):
                dve.wait_ge(summed, layer + 1)
                nc.vector.tensor_tensor(bias[:], bank[2][:, 0:E * C], b1[:], ALU.add)
                for e in range(E):
                    nc.vector.tensor_scalar(w1[:, e, :], w1[:, e, :], g[:, e:e + 1], None, ALU.mult)

            stats_block(core, "ms", x, LN_EPS, layer=layer, beside=(route_pe, route_act, route_dve))

            STEPS = 10
            with nc.Block() as block:
                @block.vector
                def _(dve):
                    then = Chain(dve, route, layer * STEPS)
                    then(nc.vector.tensor_tensor(logit[:], bank[3][:, 0:TILES * E].rearrange("p (t e) -> p t e", t=TILES),
                                                 rb[:, None, :].to_broadcast([P, TILES, E]), ALU.add))
                    then(nc.vector.tensor_reduce(top[:], logit[:], AX.X, ALU.max))
                    then(nc.vector.tensor_tensor(logit[:], logit[:], top[:, :, None].to_broadcast([P, TILES, E]), ALU.subtract))
                    dve.wait_ge(spread, layer + 1)
                    other = logit[:, :, None, :].to_broadcast([P, TILES, E, E])
                    own = logit[:, :, :, None].to_broadcast([P, TILES, E, E])
                    nc.vector.tensor_tensor(above[:], other, own, ALU.is_gt)
                    then(nc.vector.tensor_tensor(equal[:], other, own, ALU.is_equal))
                    then(nc.vector.tensor_tensor(equal[:], equal[:], earlier[:, None, :, :].to_broadcast([P, TILES, E, E]), ALU.mult))
                    then(nc.vector.tensor_tensor(above[:], above[:], equal[:], ALU.add))
                    then(nc.vector.tensor_reduce(rank[:], above[:], AX.X, ALU.add))
                    then(nc.vector.scalar_tensor_tensor(comb[:], rank[:], 1.5, logit[:], ALU.is_lt, ALU.mult))
                    then(nc.vector.tensor_reduce(kept[:], comb[:], AX.X, ALU.add))
                    then(nc.vector.reciprocal(top[:], kept[:]))
                    nc.vector.tensor_tensor(comb[:], comb[:], top[:, :, None].to_broadcast([P, TILES, E]), ALU.mult)
                    assert then.n == STEPS, then.n

                @block.scalar
                def _(act):
                    act.wait_ge(route, layer * STEPS + 3)
                    nc.scalar.activation(logit[:], logit[:], ACT.Exp).then_inc(spread, 1)

            def over_sequences(eng, turn):
                turn(-1, 1, before=False, now=False, following=True)
                turn(0, 0, before=False, now=True, following=True)
                with eng.Fori(0, (SEQS - 2) // 2) as i:
                    for n in range(2):
                        turn(2 * i + 1 + n, 1 - n, before=True, now=True, following=True)
                turn(SEQS - 1, 1, before=True, now=True, following=False)
                turn(SEQS, 0, before=True, now=False, following=False)

            with nc.Block() as block:
                @block.tensor
                def _(pe):
                    def turn(b, half, before, now, following):
                        for e in range(E):
                            n = E * (BS + b) + e
                            if now:
                                if e == 0:
                                    pe.wait_ge(xT_ready, BS + b + 1)
                                if before or e >= 2:
                                    pe.wait_ge(bent, C * (n - 1))
                                for c in range(C):
                                    pe.matmul(bank[1 + 2 * (e % 2) + c // 2][:, c % 2 * LEN:(c % 2 + 1) * LEN],
                                              w1[:, e, c * P:(c + 1) * P], xT[:, half, :], start=True, stop=True).then_inc(hidden, 1)
                            if (now if e >= 1 else before):
                                last = (e - 1) % E
                                pe.wait_ge(bent, C * n)
                                if (now if e >= 3 else before):
                                    pe.wait_ge(added, TPS * (n - 2))
                                for t in range(TPS):
                                    for c in range(C):
                                        mm = pe.matmul(bank[5 + last % 2][:, t * D:(t + 1) * D], hid[:, last % 2, c, t * P:(t + 1) * P],
                                                       w2[:, last * C + c, :], start=c == 0, stop=c == C - 1)
                                mm.then_inc(projected, 1)
                            if following and e == 2:
                                pe.wait_ge(staged, TPS * (BS + b) + 2 * TPS)
                                for t in range(TPS):
                                    mm = pe.transpose(bank[0][:, t * P:(t + 1) * P], stage[:, t, :], core.ident[:])
                                mm.then_inc(turned, 1)

                    over_sequences(pe, turn)

                @block.scalar
                def _(act):
                    def turn(b, half, before, now, following):
                        for e in range(E):
                            n = E * (BS + b) + e
                            if now:
                                if before or e >= 2:
                                    act.wait_ge(projected, n - 1)
                                for c in range(C):
                                    act.wait_ge(hidden, C * n + c // 2 * 2 + 2)
                                    nc.scalar.activation(hid[:, e % 2, c, :],
                                                         bank[1 + 2 * (e % 2) + c // 2][:, c % 2 * LEN:(c % 2 + 1) * LEN],
                                                         ACT.Gelu, bias=bias[:, e * C + c:e * C + c + 1]).then_inc(bent, 1)
                            if following and e == 2:
                                act.wait_ge(turned, BS + b + 2)
                                nc.scalar.copy(xT[:, 1 - half, :], bank[0][:, 0:LEN]).then_inc(xT_ready, 1)

                    over_sequences(act, turn)

                @block.vector
                def _(dve):
                    def add_expert(b, e):
                        n = E * (BS + b) + e
                        for t in range(TPS):
                            i = TPS * b + t
                            xs = flat(x[:, tile(i), :])
                            weight = comb[:, tile(i), e:e + 1].rearrange("p a c -> p (a c)")
                            if e >= 1:
                                dve.wait_ge(added, TPS * n - 1 + t)
                            else:
                                dve.wait_ge(staged, TPS * (BS + b) + TPS)
                            nc.vector.scalar_tensor_tensor(xs, b2[:, e, :], weight, xs, ALU.mult, ALU.add).then_inc(based, 1)
                        dve.wait_ge(projected, n + 1)
                        for t in range(TPS):
                            i = TPS * b + t
                            xs = flat(x[:, tile(i), :])
                            weight = comb[:, tile(i), e:e + 1].rearrange("p a c -> p (a c)")
                            dve.wait_ge(based, TPS * n + t + 1)
                            nc.vector.scalar_tensor_tensor(xs, bank[5 + e % 2][:, t * D:(t + 1) * D], weight, xs,
                                                           ALU.mult, ALU.add).then_inc(added, 1)

                    def turn(b, half, before, now, following):
                        for e in range(E):
                            if following and e == 1:
                                if now:
                                    dve.wait_ge(turned, BS + b + 1)
                                put_normalized(core, dve, b + 1, stage, staged)
                            if e >= 1 and now:
                                add_expert(b, e - 1)
                            if e == 0 and before:
                                add_expert(b - 1, E - 1)

                    over_sequences(dve, turn)
        leave_stream(core, saved)


def build(nc, dram, out, sublayers):
    with ExitStack() as ctx:
        core = Core(nc, dram, ctx)
        landed, stored = (ctx.enter_context(nc.semaphore(name)) for name in ("x_landed", "x_stored"))
        token_major = "s (t p) d -> p (s t) d"
        with nc.Block() as block:
            @block.sync
            def _(sp):
                sp.dma_start(core.x[:], dram["x"].rearrange(token_major, p=P)).then_inc(landed, 16)
                sp.dma_start(core.ident[:], dram["ident"]).then_inc(landed, 16)
                sp.wait_ge(landed, 32)

            @block.vector
            def _(dve):
                dve.wait_ge(landed, 32)
                nc.vector.tensor_copy(core.ident_bf[:], core.ident[:])
        for sublayer in sublayers:
            core.run(sublayer)
        with nc.Block() as block:
            @block.sync
            def _(sp):
                sp.dma_start(out.rearrange(token_major, p=P), core.x[:]).then_inc(stored, 16)
                sp.wait_ge(stored, 16)


def kernel(**inputs):
    import numpy as np
    import concourse.bacc as bacc
    from concourse.bass_utils import run_bass_kernel_spmd

    def rows(v):
        v = np.asarray(v).reshape(-1)
        return np.ascontiguousarray(np.broadcast_to(v[None, :], (P, v.size)))

    inputs = {k: np.asarray(v) for k, v in inputs.items()}
    arrays = {}
    arrays["x"] = inputs["L0_attn_embeddings"]
    arrays["ident"] = np.eye(P, dtype=np.float32)
    arrays["L0_wqkv"] = np.concatenate([inputs["L0_attn_Wq"], inputs["L0_attn_Wk"], inputs["L0_attn_Wv"]], 0).T
    arrays["L0_bqkv"] = rows(np.concatenate([inputs["L0_attn_bq"], inputs["L0_attn_bk"], inputs["L0_attn_bv"]]))
    arrays["L0_fc"] = inputs["L0_ffn_w_fc"]
    arrays["L0_proj"] = inputs["L0_ffn_w_proj"]
    arrays["L0_uT"] = inputs["L0_ffn_u"].T
    arrays["L0_v"] = inputs["L0_ffn_v"]
    arrays["L0_fbT"] = inputs["L0_ffn_fast_b"].T
    arrays["L0_gate"] = rows(inputs["L0_ffn_gate"])

    def heads_apart(w):
        w = w.reshape(-1, 4, 4, 8)
        out = np.zeros((w.shape[0], 4, 4, 32), np.float32)
        out[..., 0:8] = w
        return out.reshape(-1, 4, 128)

    arrays["L1_wq"] = inputs["L1_attn_Wq"]
    arrays["L1_wkv"] = np.concatenate([inputs["L1_attn_Wk"], inputs["L1_attn_Wv"]], 1)
    arrays["L1_wo"] = inputs["L1_attn_Wo"]
    arrays["L1_blocks"] = np.kron(np.eye(16), np.ones((8, 8))).astype(np.float32)
    arrays["L1_bq"] = inputs["L1_attn_bq"].reshape(D, 1)
    arrays["L1_bkv"] = rows(np.concatenate([inputs["L1_attn_bk"], inputs["L1_attn_bv"]]))
    arrays["L1_bo"] = rows(inputs["L1_attn_bo"])
    arrays["L1_gamma"] = rows(inputs["L1_attn_gamma"])
    arrays["L1_beta"] = rows(inputs["L1_attn_beta"])
    arrays["L1_fc"] = inputs["L1_ffn_W_fc"]
    arrays["L1_proj"] = inputs["L1_ffn_W_proj"]
    arrays["L1_ln_w"] = inputs["L1_ffn_ln_w"].reshape(4, P).T
    arrays["L1_ln_b"] = inputs["L1_ffn_ln_b"].reshape(4, P).T
    wqkv, bqkv = inputs["L2_attn_Wqkv"], inputs["L2_attn_bqkv"]
    arrays["L2_wq"] = heads_apart(wqkv[:, 0:D])
    arrays["L2_wk"] = heads_apart(wqkv[:, D:2 * D])
    arrays["L2_wv"] = wqkv[:, 2 * D:3 * D]
    arrays["L2_wo"] = inputs["L2_attn_Wout"]
    arrays["L2_bo"] = rows(inputs["L2_attn_bout"])
    arrays["L2_bv"] = rows(bqkv[2 * D:3 * D])
    arrays["L2_bq"] = heads_apart(bqkv[None, 0:D])[0].T
    arrays["L2_bk"] = heads_apart(bqkv[None, D:2 * D])[0].T
    pos = np.arange(LEN)
    arrays["L2_apart"] = np.abs(pos[:, None] - pos[None, :]).astype(np.float32).reshape(TPS, P, LEN).transpose(1, 0, 2)
    arrays["L2_slopes"] = rows(np.array([value for _, value in SLOPE_PARTS], np.float32))

    half = np.arange(0, HD2, 2, dtype=np.float32)
    freqs = pos.astype(np.float32)[:, None] * (1.0 / np.float32(10000.0) ** (half / np.float32(HD2)))[None, :]
    spread = (half + np.float32(0.4 * HD2)) / np.float32(1.4 * HD2)
    power = (pos.astype(np.float32) - LEN // 2) / np.float32(WINDOW // 2)
    scale = spread[None, :] ** power[:, None]
    freqs, scale = (np.concatenate([a, a], 1).astype(np.float32) for a in (freqs, scale))
    sign = np.where(np.arange(HD2) < HD2 // 2, 1.0, -1.0).astype(np.float32)
    qk_factor = 8.0
    one = np.array([[np.cos(freqs) * scale * qk_factor, np.cos(freqs) / scale],
                    [np.sin(freqs) * scale * sign * qk_factor, np.sin(freqs) / scale * sign]], np.float32)
    arrays["r_tables"] = np.concatenate([one, one], 3).transpose(3, 0, 1, 2)
    key = np.arange(WINDOW_KEYS)[None, :] - WINDOW
    query = np.arange(P)[:, None]
    seen = (key <= query) & (query <= key + WINDOW)
    arrays["r_masks"] = np.stack([np.where(seen & (key >= 0), 0.0, -1e30), np.where(seen, 0.0, -1e30)], 1).astype(np.float32)
    arrays["r_head_ones"] = np.kron(np.eye(2), np.ones((HD2, 1))).astype(np.float32)
    w = inputs["L2_ffn_Wqkv"].reshape(-1, D, 3, HEADS2, HD2)
    arrays["r_w"] = w.reshape(-1, D, 3 * HEADS2 * HD2)
    arrays["r_wo"] = inputs["L2_ffn_Wo"].reshape(-1, PAIRS2, P, D).transpose(0, 2, 1, 3).reshape(-1, P, PAIRS2 * D)
    qs, ks = inputs["L2_ffn_q_scale"], inputs["L2_ffn_k_scale"]
    scales = np.stack([qs, ks], 2)
    arrays["r_qk_scale"] = np.concatenate([scales, scales], 1)
    w1, b1, w2 = inputs["L2_ffn_W1"], inputs["L2_ffn_b1"], inputs["L2_ffn_W2"]
    depth, width = w1.shape[0], w2.shape[1]
    filled = 3 * P
    w1p, b1p, w2p = (np.zeros(s, np.float32) for s in ((depth, D, 2, filled), (depth, 2, filled), (depth, filled, D)))
    w1p[..., 0:width] = w1.reshape(depth, D, 2, width)
    b1p[..., 0:width] = b1.reshape(depth, 2, width)
    w2p[:, 0:width] = w2
    arrays["g_w1"] = w1p.reshape(depth, D, 2 * filled)
    arrays["g_b1"] = b1p.reshape(depth, 6, P).transpose(0, 2, 1)
    arrays["g_w2"] = w2p.reshape(depth, 3, P, D).transpose(0, 2, 1, 3).reshape(depth, P, 3 * D)
    arrays["g_b2"] = np.broadcast_to(inputs["L2_ffn_b2"][:, None, :], (depth, P, D))
    arrays["g_ln_g"] = inputs["L2_ffn_ln_g"][:, :, None]
    arrays["g_ln_b"] = inputs["L2_ffn_ln_b"][:, :, None]
    for name in ("r_w", "r_wo", "r_qk_scale"):
        arrays[name] = np.concatenate([arrays[name], arrays[name][0:1]], 0)
    arrays["L3_wqkv"] = inputs["L3_attn_W_qkv"].T
    arrays["L3_bqk"] = inputs["L3_attn_b_qkv"][0:2 * D].reshape(2, D).T
    arrays["L3_bv"] = rows(inputs["L3_attn_b_qkv"][2 * D:])
    gap = (pos[None, :] - pos[:, None]).astype(np.float32)
    decay = (np.where(gap >= 0, np.float32(0.99) ** gap, 0.0) / np.sqrt(np.float32(D))).astype(np.float32)
    arrays["L3_decay"] = np.stack([decay[0:P, 0:P], decay[0:P, P:LEN], decay[P:LEN, P:LEN]], 1)
    layers = inputs["L3_ffn_w1"].shape[0]
    arrays["m_w1"] = inputs["L3_ffn_w1"].transpose(0, 2, 1, 3).reshape(layers, D, 4 * 512)
    arrays["m_w2"] = inputs["L3_ffn_w2"].reshape(layers, 16, P, D).transpose(0, 2, 1, 3).reshape(layers, P, 16 * D)
    arrays["m_g"] = inputs["L3_ffn_ln_g"].transpose(0, 2, 1)
    arrays["m_b_ln"] = inputs["L3_ffn_ln_b"].transpose(0, 2, 1)
    arrays["m_b1"] = inputs["L3_ffn_b1"].reshape(layers, 16, P).transpose(0, 2, 1)
    arrays["m_b2"] = np.broadcast_to(inputs["L3_ffn_b2"].reshape(layers, 1, 4 * D), (layers, P, 4 * D))
    arrays["m_rw"] = inputs["L3_ffn_router_w"]
    arrays["m_rb"] = np.broadcast_to(inputs["L3_ffn_router_b"][:, None, :], (layers, P, 4))
    arrays["m_earlier"] = rows(np.tril(np.ones((4, 4), np.float32), -1))
    nc = bacc.Bacc("TRN2", target_bir_lowering=False, num_devices=1)
    arrays = {f"in_{k}": np.ascontiguousarray(v) for k, v in arrays.items()}
    dram = {k[3:]: nc.dram_tensor(k, v.shape, F32, kind="ExternalInput").ap() for k, v in arrays.items()}
    out = nc.dram_tensor("out_x", (SEQS, LEN, D), F32, kind="ExternalOutput").ap()
    build(nc, dram, out, [l0_attention, l0_feedforward, l1_attention, l1_feedforward, l2_attention, l2_feedforward, l3_attention, l3_feedforward])
    result = run_bass_kernel_spmd(nc, [arrays], core_ids=[0])
    return result.results[0]["out_x"]
```
